# Optimizing a Trainium2 kernel written in Bass

```python
import numpy as np
import jax
import jax.numpy as jnp

def _softmax(x, axis=-1):
    return jax.nn.softmax(x, axis=axis)

def _gelu(x):
    return jax.nn.gelu(x, approximate=True)

def _silu(x):
    return jax.nn.silu(x)

def _sigmoid(x):
    return jax.nn.sigmoid(x)

def _layernorm(x, axis=-1, eps=1e-05):
    m = jnp.mean(x, axis=axis, keepdims=True)
    v = jnp.var(x, axis=axis, keepdims=True)
    return (x - m) / jnp.sqrt(v + eps)

def _scatter_add(tgt, idx, src, axis=0):
    return tgt.at[idx].add(src)

def _segment_sum(src, seg, n):
    return jax.ops.segment_sum(src, seg, n)
kernel_name = 'mk_gnn_preln_d1_gnn_r64_07be55'

def setup_inputs(seed: int=0):
    np.random.seed(seed)
    _w = jnp.asarray

    def _rec_inputs():
        import jax
        import jax.numpy as jnp
        _gk = jax.random.key(seed)
        x = -0.0005121 + 1.001 * jax.random.normal(jax.random.fold_in(_gk, 1), (100000, 64), jnp.float32)
        src = jax.random.randint(jax.random.fold_in(_gk, 2), (50000,), 0, 100000, jnp.int32)
        dst = jnp.minimum((100000 * jax.random.uniform(jax.random.fold_in(_gk, 3), (50000,)) ** 2.0).astype(jnp.int32), 99999)
        _o = jnp.argsort(dst, stable=True)
        src = src[_o]
        dst = dst[_o]
        edge_attr_32 = 0.000283511 + 1.00007 * jax.random.normal(jax.random.fold_in(_gk, 11), (50000, 32), jnp.float32)
        return (x, src, dst, edge_attr_32)
    x, src, dst, edge_attr_32 = _rec_inputs()

    def _L0_gnn_setup():
        import math
        import jax, jax.numpy as jnp
        import numpy as np
        N_NODES = 50000
        N_EDGES = 9375
        IN_CH = 64
        HEADS = 2
        C = 64
        HC = HEADS * C
        EDGE_DIM = 32

        def _layernorm(x, g, b, eps=1e-05):
            m = jnp.mean(x, axis=-1, keepdims=True)
            v = jnp.mean(jnp.square(x - m), axis=-1, keepdims=True)
            return (x - m) / jnp.sqrt(v + eps) * g + b
        key = jax.random.key(seed)
        ks = jax.random.split(key, 12)
        s = 0.05
        return {'x': jax.random.normal(ks[0], (N_NODES, IN_CH), jnp.float32), 'edge_index': jax.random.randint(ks[1], (2, N_EDGES), 0, N_NODES, dtype=jnp.int64), 'edge_attr': jax.random.normal(ks[2], (N_EDGES, EDGE_DIM), jnp.float32), 'Wq': s * jax.random.normal(ks[3], (IN_CH, HC), jnp.float32), 'bq': jnp.zeros((HC,), jnp.float32), 'Wk': s * jax.random.normal(ks[4], (IN_CH, HC), jnp.float32), 'bk': jnp.zeros((HC,), jnp.float32), 'Wv': s * jax.random.normal(ks[5], (IN_CH, HC), jnp.float32), 'bv': jnp.zeros((HC,), jnp.float32), 'We': s * jax.random.normal(ks[6], (EDGE_DIM, HC), jnp.float32), 'Wp': s * jax.random.normal(ks[7], (HC, IN_CH), jnp.float32), 'bp': jnp.zeros((IN_CH,), jnp.float32), 'ln1_g': jnp.ones((IN_CH,), jnp.float32), 'ln1_b': jnp.zeros((IN_CH,), jnp.float32), 'ln2_g': jnp.ones((IN_CH,), jnp.float32), 'ln2_b': jnp.zeros((IN_CH,), jnp.float32), 'W1': s * jax.random.normal(ks[8], (IN_CH, IN_CH), jnp.float32), 'b1': jnp.zeros((IN_CH,), jnp.float32), 'W2': s * jax.random.normal(ks[9], (IN_CH, IN_CH), jnp.float32), 'b2': jnp.zeros((IN_CH,), jnp.float32)}
    _L0_gnn_all = _L0_gnn_setup()
    _L0_gnn_in = {k: v for k, v in _L0_gnn_all.items() if k in ('Wq', 'bq', 'Wk', 'bk', 'Wv', 'bv', 'We', 'Wp', 'bp', 'ln1_g', 'ln1_b', 'ln2_g', 'ln2_b', 'W1', 'b1', 'W2', 'b2')}
    del _L0_gnn_all
    return {'x': x, 'src': src, 'dst': dst, 'edge_attr_32': edge_attr_32, 'L0_gnn_Wq': _L0_gnn_in['Wq'], 'L0_gnn_bq': _L0_gnn_in['bq'], 'L0_gnn_Wk': _L0_gnn_in['Wk'], 'L0_gnn_bk': _L0_gnn_in['bk'], 'L0_gnn_Wv': _L0_gnn_in['Wv'], 'L0_gnn_bv': _L0_gnn_in['bv'], 'L0_gnn_We': _L0_gnn_in['We'], 'L0_gnn_Wp': _L0_gnn_in['Wp'], 'L0_gnn_bp': _L0_gnn_in['bp'], 'L0_gnn_ln1_g': _L0_gnn_in['ln1_g'], 'L0_gnn_ln1_b': _L0_gnn_in['ln1_b'], 'L0_gnn_ln2_g': _L0_gnn_in['ln2_g'], 'L0_gnn_ln2_b': _L0_gnn_in['ln2_b'], 'L0_gnn_W1': _L0_gnn_in['W1'], 'L0_gnn_b1': _L0_gnn_in['b1'], 'L0_gnn_W2': _L0_gnn_in['W2'], 'L0_gnn_b2': _L0_gnn_in['b2']}

def reference(x, src, dst, edge_attr_32, L0_gnn_Wq, L0_gnn_bq, L0_gnn_Wk, L0_gnn_bk, L0_gnn_Wv, L0_gnn_bv, L0_gnn_We, L0_gnn_Wp, L0_gnn_bp, L0_gnn_ln1_g, L0_gnn_ln1_b, L0_gnn_ln2_g, L0_gnn_ln2_b, L0_gnn_W1, L0_gnn_b1, L0_gnn_W2, L0_gnn_b2):
    import jax
    import jax.numpy as jnp

    def _L0_gnn_ref(x, edge_index, edge_attr, Wq, bq, Wk, bk, Wv, bv, We, Wp, bp, ln1_g, ln1_b, ln2_g, ln2_b, W1, b1, W2, b2):
        import math
        import jax, jax.numpy as jnp
        import numpy as np
        N_NODES = 50000
        N_EDGES = 9375
        IN_CH = 64
        HEADS = 2
        C = 64
        HC = HEADS * C
        EDGE_DIM = 32

        def _layernorm(x, g, b, eps=1e-05):
            m = jnp.mean(x, axis=-1, keepdims=True)
            v = jnp.mean(jnp.square(x - m), axis=-1, keepdims=True)
            return (x - m) / jnp.sqrt(v + eps) * g + b
        n = x.shape[0]
        residual = x
        h = _layernorm(x, ln1_g, ln1_b)
        q = (h @ Wq + bq).reshape(n, HEADS, C)
        k = (h @ Wk + bk).reshape(n, HEADS, C)
        v = (h @ Wv + bv).reshape(n, HEADS, C)
        src, tgt = (edge_index[0], edge_index[1])
        e = (edge_attr @ We).reshape(-1, HEADS, C)
        qi = q[tgt]
        kj = k[src] + e
        vj = v[src] + e
        alpha = jnp.sum(qi * kj, axis=-1) / math.sqrt(C)
        amax = jax.ops.segment_max(alpha, tgt, num_segments=n)
        ex = jnp.exp(alpha - amax[tgt])
        den = jax.ops.segment_sum(ex, tgt, num_segments=n)
        a = ex / (den[tgt] + 1e-08)
        agg = jax.ops.segment_sum(a[:, :, None] * vj, tgt, num_segments=n)
        out = agg.reshape(n, HC) @ Wp + bp
        out = out + residual
        res2 = out
        o = _layernorm(out, ln2_g, ln2_b)
        o = jax.nn.gelu(o @ W1 + b1, approximate=False) @ W2 + b2
        return o + res2
    edge_index = jnp.stack([src, dst])
    h = jnp.maximum(_layernorm(x, axis=-1), 0.0)
    x = x + _L0_gnn_ref(h, edge_index, edge_attr_32, L0_gnn_Wq, L0_gnn_bq, L0_gnn_Wk, L0_gnn_bk, L0_gnn_Wv, L0_gnn_bv, L0_gnn_We, L0_gnn_Wp, L0_gnn_bp, L0_gnn_ln1_g, L0_gnn_ln1_b, L0_gnn_ln2_g, L0_gnn_ln2_b, L0_gnn_W1, L0_gnn_b1, L0_gnn_W2, L0_gnn_b2)
    return x

_drawn_inputs = setup_inputs


def setup_inputs(seed=0):
    import zlib

    import numpy as np

    out = dict(_drawn_inputs(seed))
    spreads = {'L0_gnn_bq': (0.0, 2.0),
     'L0_gnn_bk': (0.0, 2.0),
     'L0_gnn_bv': (0.0, 0.407),
     'L0_gnn_bp': (0.0, 0.1),
     'L0_gnn_ln1_g': (1.0, 0.6),
     'L0_gnn_ln1_b': (0.0, 0.8),
     'L0_gnn_ln2_g': (1.0, 0.6),
     'L0_gnn_ln2_b': (0.0, 0.8),
     'L0_gnn_b1': (0.0, 0.55),
     'L0_gnn_b2': (0.0, 0.1)}
    factors = {'L0_gnn_Wq': 8.0, 'L0_gnn_Wk': 8.0}
    for name, (base, spread) in spreads.items():
        noise = np.random.default_rng([zlib.crc32(name.encode()), seed]).standard_normal(out[name].shape)
        drawn = base * np.exp(spread * noise) if base else spread * noise
        out[name] = jnp.asarray(drawn.astype(out[name].dtype))
    for name, factor in factors.items():
        out[name] = (out[name] * factor).astype(out[name].dtype)
    return out
```

```python
import concourse.bass as bass
from concourse import mybir
from contextlib import ExitStack



def gnn_layer(nc, x, src, dst, eattr, Wq, bq, Wk, bk, Wv, bv, We, Wp, bp,
              g1, be1, g2, be2, W1, b1, W2, b2, edge_rows, states, out):
    f32 = mybir.dt.float32
    i32 = mybir.dt.int32
    ALU = mybir.AluOpType
    ACT = mybir.ActivationFunctionType
    AX = mybir.AxisListType

    P = 128
    N, C = x.shape
    E, ED = eattr.shape
    H = 2
    HC = H * C
    NT, ET = 16, 8
    B = -(-E // (P * ET))
    EPP = B * ET
    PF = E // EPP
    EL = E - PF * EPP
    FULL_EA = EL // ET
    XT = NT + 2 * ET
    S0, D0 = NT, NT + ET
    OT = NT + ET
    NCH = OT // 8
    EPS = 1e-5
    FAR = float(2 ** 20)
    NEG = -1e30
    ROWS = P * NT
    LASTROWS = N - (B - 1) * ROWS
    LASTP = LASTROWS // NT
    SW = HC + 2 * H
    assert PF == P - 1 and EL % ET == 0 and LASTP * NT == LASTROWS and B % 2 == 1
    KS = C + ED + 1
    KD = C + 1

    ctx = ExitStack()
    with ctx:
        def sb(name, shape, dt=f32):
            return ctx.enter_context(nc.sbuf_tensor(name, shape, dt))

        def pb(name, shape):
            return ctx.enter_context(nc.psum_tensor(name, shape, f32))

        def sem(name):
            return ctx.enter_context(nc.semaphore(name))

        ident = sb("ident", [P, P])
        center = sb("center", [C, C])
        pick = {m: (sb(f"place_center_{m}", [C, m]), sb(f"place_bias_{m}", [C, m]),
                    sb(f"place_one_{m}", [1, m])) for m in (KS, KD)}
        center2 = sb("center2", [C, 2 * C])
        place_edge = sb("place_edge", [ED, KS])
        gcol = sb("gcol", [C, 4])
        wqkv = sb("wqkv", [C, 3, HC])
        gwqkv = sb("gwqkv", [C, 3, HC])
        bqkv = sb("bqkv", [1, 3, HC])
        we = sb("we", [ED, HC])
        wq_s = sb("wq_s", [KD, HC])
        wkv_s = sb("wkv_s", [KS, 2, HC])
        wp = sb("wp", [HC, C])
        w1 = sb("w1", [C, 2, C])
        gw1 = sb("gw1", [C, C])
        w1bd = sb("w1bd", [P, P])
        w2bd = sb("w2bd", [P, P])
        b1col = sb("b1col", [P, 1])
        b1g = sb("b1g", [P, 1])
        bp_b = sb("bp_b", [P, C])
        b2row = sb("b2row", [1, 8, C])
        ones_row = sb("ones_row", [1, P])
        sel = sb("sel", [H, P])

        dsti = sb("dsti", [P, EPP + 2], i32)
        srci = sb("srci", [P, EPP + 16], i32)
        dstg = sb("dstg", [P, EPP + 16], i32)
        dstf = sb("dstf", [P, EPP + 2])
        same = sb("same", [P, EPP + 1])
        firstseg = sb("firstseg", [P, EPP])
        nofinal = sb("nofinal", [P, EPP])
        scati = sb("scati", [P, EPP], i32)
        keepm = sb("keepm", [P, B, H, ET + 1])
        fix = sb("fix", [P, 8])
        fixi = sb("fixi", [P, 2], i32)
        rowbase = sb("rowbase", [P, 1])
        idx = [sb(f"idx{i}", [P, 2 * ET], i32) for i in range(2)]

        X = [sb(f"X{i}", [P, XT, C]) for i in range(2)]
        Y = sb("Y", [P, XT, C])
        aug_s = [sb(f"aug_s{i}", [P, ET, KS]) for i in range(2)]
        aug_d = sb("aug_d", [P, ET, KD])
        O = [sb(f"O{i}", [P, OT, C]) for i in range(2)]
        XO = [sb(f"XO{i}", [P, OT, C]) for i in range(2)]
        OUTS = sb("OUTS", [P, NCH, 8 * C])
        rec = [sb(f"rec{i}", [P, ET, SW]) for i in range(2)]
        xst = sb("xst", [P, XT, 6])
        yst = sb("yst", [P, 2 * ET, 6])
        ost = sb("ost", [P, OT, 6])
        sm = sb("sm", [P, 4, XT])
        mean = sb("mean", [P, XT])
        sm2 = sb("sm2", [P, 4, 2 * ET])
        sm3 = sb("sm3", [P, 4, OT])
        VN = XT + 2 * ET + OT
        OV = XT + 2 * ET
        vars_ = sb("vars_", [P, VN])
        sd = sb("sd", [P, VN])
        rs = sb("rs", [P, VN])
        srcT = sb("srcT", [KS, 2, 512])
        dstT = sb("dstT", [KD, 2, 512])
        q_sb = sb("q_sb", [P, 2, 4 * HC])
        qk = sb("qk", [P, ET, HC])
        alpha = sb("alpha", [P, H, ET + 1])
        mx = [sb(f"mx{i}", [P, H, ET + 1]) for i in range(2)]
        den = [sb(f"den{i}", [P, H, ET + 1]) for i in range(2)]
        ex = sb("ex", [P, 2, H, ET])
        cw = sb("cw", [P, 2, H, ET + 1])
        rden = sb("rden", [P, 2, H, ET])
        aggn = sb("aggn", [P, ET, HC])
        aggT = sb("aggT", [P, 2, 512])
        z2 = sb("z2", [P, NCH, 8 * C])
        z2T = sb("z2T", [P, NCH, 512])
        hid = sb("hid", [P, NCH, 512])
        ticks = sb("ticks", [P, 3])
        frec = sb("frec", [P, SW])
        xf = sb("xf", [P, C])
        fT = sb("fT", [P, 2, P])
        fsm = sb("fsm", [H, 6, P])
        fkeep = sb("fkeep", [H, 2, P])
        mj = sb("mj", [H, P + 1])
        dj = sb("dj", [H, P + 1])
        fk = sb("fk", [H, 8, P])
        fex = sb("fex", [H, 4, P])
        fcw = sb("fcw", [H, 4, P])
        bc = sb("bc", [P, 4, P])
        aj = sb("aj", [P, P + 1])
        fa = sb("fa", [P, 3, P])
        fflag = sb("fflag", [P, 2, H])
        frow = sb("frow", [P, 6, C])
        fst = sb("fst", [P, 6])
        fsc = sb("fsc", [P, 12])
        fzT = sb("fzT", [C, 2, P])

        tp = [pb(f"tp{i}", [P, 512]) for i in range(2)]
        k_ps = pb("k_ps", [P, 512])
        q_ps = pb("q_ps", [P, 512])
        v_ps = [pb(f"v_ps{i}", [P, 512]) for i in range(2)]
        hid_ps = pb("hid_ps", [P, 512])
        res_ps = pb("res_ps", [P, 512])

        pads_set = sem("pads_set")
        tables_in = sem("tables_in")
        consts_in = sem("consts_in")
        built = sem("built")
        link_done = sem("link_done")
        w_placed = sem("w_placed")
        w_folded = sem("w_folded")
        w_ready = sem("w_ready")
        idx_ready = sem("idx_ready")
        dense_in = [sem(f"dense_in{i}") for i in range(2)]
        eattr_in = [sem(f"eattr_in{i}") for i in range(2)]
        gathered = [sem(f"gathered{i}") for i in range(2)]
        x_stats = sem("x_stats")
        x_sums = sem("x_sums")
        x_mean = sem("x_mean")
        x_diff2 = sem("x_diff2")
        x_v64 = sem("x_v64")
        x_var = sem("x_var")
        centered = sem("centered")
        relued = sem("relued")
        y_stats = sem("y_stats")
        y_sums = sem("y_sums")
        y_diff2 = sem("y_diff2")
        y_v64 = sem("y_v64")
        y_var = sem("y_var")
        sd_ready = sem("sd_ready")
        rs_ready = sem("rs_ready")
        zsrc_ready = sem("zsrc_ready")
        zdst_ready = sem("zdst_ready")
        z2_ready = sem("z2_ready")
        o_scaled = sem("o_scaled")
        o_nodes = sem("o_nodes")
        x_nodes_free = sem("x_nodes_free")
        x_edges_free = sem("x_edges_free")
        src_T, dst_T = sem("src_T"), sem("dst_T")
        z_T, agg_T = sem("z_T"), sem("agg_T")
        src_ev, dst_ev = sem("src_ev"), sem("dst_ev")
        z_ev, agg_ev = sem("z_ev"), sem("agg_ev")
        qk_mm = sem("qk_mm")
        v_mm = sem("v_mm")
        q_evac = sem("q_evac")
        qk_ready = sem("qk_ready")
        alpha_ready = sem("alpha_ready")
        mx_ready = sem("mx_ready")
        mx_diff = sem("mx_diff")
        ex_ready = sem("ex_ready")
        cw_ready = sem("cw_ready")
        den_prev_in = sem("den_prev_in")
        den_ready = sem("den_ready")
        den_eps = sem("den_eps")
        rden_ready = sem("rden_ready")
        wv_ready = sem("wv_ready")
        chain = sem("chain")
        aggn_ready = sem("aggn_ready")
        hid_mm = sem("hid_mm")
        gelu_done = sem("gelu_done")
        mlp_mm = sem("mlp_mm")
        proj_mm = sem("proj_mm")
        o_targets = sem("o_targets")
        o_stats = sem("o_stats")
        o_sums = sem("o_sums")
        o_diff2 = sem("o_diff2")
        o_v64 = sem("o_v64")
        o_var = sem("o_var")
        out_ready = sem("out_ready")
        stored = [sem(f"stored{i}") for i in range(NCH)]
        state_stored = [sem(f"state_stored{i}") for i in range(2)]
        rows_in = [sem(f"rows_in{i}") for i in range(2)]
        scattered = [sem(f"scattered{i}") for i in range(2)]
        ticked = sem("ticked")
        f_in = sem("f_in")
        f_link = sem("f_link")
        f_T = sem("f_T")
        f_exp_in = sem("f_exp_in")
        f_exp = sem("f_exp")
        f_coef = sem("f_coef")
        f_bc = sem("f_bc")
        f_agg = sem("f_agg")
        f_proj = sem("f_proj")
        f_var = sem("f_var")
        f_sd = sem("f_sd")
        f_z = sem("f_z")
        f_zT = sem("f_zT")
        f_zev = sem("f_zev")
        f_hid = sem("f_hid")
        f_gelu = sem("f_gelu")
        f_mlp = sem("f_mlp")
        f_row = sem("f_row")
        f_out = sem("f_out")

        def wide(ap, n):
            return ap.unsqueeze(2).broadcast_to([ap.shape[0], ap.shape[1], n])

        def rows(ap, n):
            return ap.unsqueeze(1).broadcast_to([ap.shape[0], n, ap.shape[1]])

        def tiles(ap):
            return ap.rearrange("p (t c) -> p t c", c=C)

        def flat(ap):
            return ap.rearrange("p a t -> p (a t)")

        ea_main = eattr[0:PF * EPP, :].rearrange("(p t) c -> p t c", t=EPP)
        ea_last = eattr[PF * EPP:E, :].rearrange("(p t) c -> p t c", p=1)
        PCUT = 96
        ECUT = 112

        block = ctx.enter_context(nc.Block())

        @block.sync
        def _(sp):
            def load_block(b, par, tail=False, full=True, first=False):
                if not first:
                    sp.wait_ge(x_nodes_free, b - 1)
                rows_ = LASTROWS if tail else ROWS
                xb = x[bass.ds(b * ROWS, rows_), :].rearrange("(p j) c -> p j c", j=NT)
                sp.dma_start(X[par][0:PCUT, 0:NT, :], xb[0:PCUT]).then_inc(dense_in[par], 16)
                sp.dma_start(X[par][PCUT:rows_ // NT, 0:NT, :], xb[PCUT:rows_ // NT])\
                  .then_inc(dense_in[par], 16)
                if not first:
                    sp.wait_ge(src_T, 2 * (b - 1))
                ea = aug_s[par][:, :, C:C + ED]
                sp.dma_start(ea[0:ECUT], ea_main[0:ECUT, bass.ds(b * ET, ET), :])\
                  .then_inc(eattr_in[par], 16)
                sp.dma_start(ea[ECUT:PF], ea_main[ECUT:PF, bass.ds(b * ET, ET), :])\
                  .then_inc(eattr_in[par], 16)
                sp.dma_start(ea[PF:P], ea_last[:, bass.ds(b * ET, ET) if full else slice(0, ET), :])\
                  .then_inc(eattr_in[par], 16)

            def store_outputs(s, tail=False):
                b = s - 1
                rows_ = LASTROWS if tail else ROWS
                ob = out[bass.ds(b * ROWS, rows_), :].rearrange("(p j) c -> p j c", j=NT)
                for c in range(NCH - 1):
                    sp.wait_ge(out_ready, NCH * b + c + 1)
                    t = slice(8 * c, 8 * c + 8)
                    if tail:
                        sp.dma_start(ob[0:PCUT, t], tiles(OUTS[0:PCUT, c, :]))\
                          .then_inc(stored[c], 16)
                        sp.dma_start(ob[PCUT:LASTP, t], tiles(OUTS[PCUT:LASTP, c, :]))\
                          .then_inc(stored[c], 16)
                    else:
                        sp.dma_start(ob[:, t], tiles(OUTS[:, c, :])).then_inc(stored[c], 16)
                sp.wait_ge(out_ready, NCH * b + NCH)
                sp.dma_start(edge_rows[:, bass.ds(b * ET, ET), :], tiles(OUTS[:, NCH - 1, :]))\
                  .then_inc(stored[NCH - 1], 16)

            def store_states(s, par):
                sp.wait_ge(chain, ET * (s + 1))
                sp.dma_start(states[:, bass.ds(s * ET, ET), :], rec[par][:, :, :])\
                  .then_inc(state_stored[par], 16)

            sp.wait_ge(pads_set, 1)
            sp.dma_start(dsti[0:PF, 1:EPP + 1], dst[0:PF * EPP].rearrange("(p t) -> p t", t=EPP))\
              .then_inc(tables_in, 16)
            sp.dma_start(dsti[PF:P, 1:EL + 1], dst[PF * EPP:E].rearrange("(p t) -> p t", p=1))\
              .then_inc(tables_in, 16)
            sp.dma_start(srci[0:PF, 0:EPP], src[0:PF * EPP].rearrange("(p t) -> p t", t=EPP))\
              .then_inc(tables_in, 16)
            sp.dma_start(srci[PF:P, 0:EL], src[PF * EPP:E].rearrange("(p t) -> p t", p=1))\
              .then_inc(tables_in, 16)
            dst_pt = dst[0:PF * EPP].rearrange("(p t) -> p t", t=EPP)
            with nc.allow_non_contiguous_dma(reason="one element per partition, once"):
                sp.dma_start(dsti[1:P, 0:1], dst_pt[:, EPP - 1:EPP]).then_inc(tables_in, 16)
                sp.dma_start(dsti[0:PF - 1, EPP + 1:EPP + 2], dst_pt[1:PF, 0:1])\
                  .then_inc(tables_in, 16)
                sp.dma_start(dsti[PF - 1:PF, EPP + 1:EPP + 2],
                             dst[PF * EPP:PF * EPP + 1].rearrange("(p t) -> p t", p=1))\
                  .then_inc(tables_in, 16)
            load_block(0, 0, first=True)
            with nc.allow_non_contiguous_dma(reason="bias columns, once"):
                for i, v in enumerate((g1, be1, g2, be2)):
                    sp.dma_start(gcol[:, i:i + 1], v.rearrange("(c a) -> c a", a=1))\
                      .then_inc(consts_in, 16)
                for h in range(2):
                    sp.dma_start(b1col[h * C:(h + 1) * C, :], b1.rearrange("(c a) -> c a", a=1))\
                      .then_inc(consts_in, 16)
            for i, (w, b) in enumerate(((Wq, bq), (Wk, bk), (Wv, bv))):
                sp.dma_start(wqkv[:, i, :], w).then_inc(consts_in, 16)
                sp.dma_start(bqkv[:, i, :], b.rearrange("(a c) -> a c", a=1)).then_inc(consts_in, 16)
            sp.dma_start(we[:, :], We).then_inc(consts_in, 16)
            sp.dma_start(wp[:, :], Wp).then_inc(consts_in, 16)
            sp.wait_ge(pads_set, 2)
            for h in range(2):
                sp.dma_start(w1[:, h, :], W1).then_inc(consts_in, 16)
                sp.dma_start(w2bd[h * C:(h + 1) * C, h * C:(h + 1) * C], W2).then_inc(consts_in, 16)
            sp.dma_start(bp_b[:, :], bp.rearrange("(a c) -> a c", a=1).broadcast_to([P, C]))\
              .then_inc(consts_in, 16)
            sp.dma_start(b2row[:, :, :], b2.rearrange("(a t c) -> a t c", a=1, t=1)
                         .broadcast_to([1, 8, C])).then_inc(consts_in, 16)
            load_block(1, 1, first=True)
            store_states(0, 0)

            def step(s, par, **kw):
                load_block(s + 1, 1 - par, **kw)
                store_outputs(s)
                store_states(s, par)

            NF = (FULL_EA - 2) // 2
            with sp.Fori(0, NF) as k:
                step(2 * k + 1, 1)
                step(2 * k + 2, 0)
            s = 2 * NF + 1
            while s + 1 < FULL_EA or s % 2:
                step(s, s % 2, full=s + 1 < FULL_EA)
                s += 1
            with sp.Fori(s // 2, (B - 3) // 2) as k:
                step(2 * k, 0, full=False)
                step(2 * k + 1, 1, full=False)
            for s in range(B - 3, B):
                if s < B - 1:
                    step(s, s % 2, full=False, tail=s + 1 == B - 1)
                else:
                    store_outputs(s)
                    store_states(s, s % 2)
            store_outputs(B, tail=True)

            sp.wait_ge(stored[NCH - 1], 16 * B)
            sp.wait_ge(x_nodes_free, B)

            def load_rows(b, par):
                sp.dma_start(X[par][:, 0:ET, :], edge_rows[:, bass.ds(b * ET, ET), :])\
                  .then_inc(rows_in[par], 16)
                sp.dma_start(idx[par][:, 0:ET], scati[:, bass.ds(b * ET, ET)])\
                  .then_inc(rows_in[par], 16)

            load_rows(0, 0)
            load_rows(1, 1)
            with sp.Fori(1, B // 2) as k:
                for par in range(2):
                    sp.wait_ge(scattered[par], 16 * ET * k)
                    load_rows(2 * k + par, par)
            sp.wait_ge(scattered[0], 16 * ET * (B // 2))
            load_rows(B - 1, 0)
            for c in range(NCH - 1):
                sp.wait_ge(stored[c], 16 * (B + 1))

        @block.gpsimd
        def _(pool):
            pool.memset(ident[:, :], 0.0).then_inc(built, 1)
            pool.memset(sel[:, :], 1.0).then_inc(built, 1)
            pool.wait_ge(built, 2)
            pool.affine_select(out=ident[:, :], in_=ident[:, :], compare_op=ALU.not_equal, fill=1.0,
                               base=0, pattern=[[-1, P]], channel_multiplier=1).then_inc(built, 1)
            pool.affine_select(out=sel[:, :], in_=sel[:, :], compare_op=ALU.is_ge, fill=0.0,
                               base=0, pattern=[[1, P]], channel_multiplier=-C).then_inc(built, 1)
            pool.wait_ge(built, 4)
            pool.affine_select(out=sel[:, :], in_=sel[:, :], compare_op=ALU.is_ge, fill=0.0,
                               base=C - 1, pattern=[[-1, P]], channel_multiplier=C).then_inc(built, 1)
            pool.iota(rowbase[:, :], [[0, 1]], base=-1, channel_multiplier=EPP,
                      allow_small_or_imprecise_dtypes=True).then_inc(built, 1)

            def tick(i, first=False):
                if not first:
                    pool.wait_ge(ticked, i)
                pool.tensor_tensor(ticks[:, 0:1], ticks[:, 1:2], ticks[:, 2:3], ALU.add)\
                    .then_inc(ticked, 1)

            pool.memset(ticks[:, :], 0.0).then_inc(built, 1)
            pool.wait_ge(built, 7)

            def gather_block(b, par, first=False):
                pool.wait_ge(idx_ready, b + 1)
                if not first:
                    pool.wait_ge(x_edges_free, b - 1)
                tick(b, first=first and b == 0)
                for t in range(2 * ET):
                    pool.indirect_dma_start(
                        X[par][:, S0 + t, :], None, x,
                        bass.IndirectOffsetOnAxis(ap=idx[par][:, t:t + 1], axis=0))\
                        .then_inc(gathered[par], 16)

            gather_block(0, 0, first=True)
            gather_block(1, 1, first=True)
            with pool.Fori(1, B // 2) as k:
                gather_block(2 * k, 0)
                gather_block(2 * k + 1, 1)
            gather_block(B - 1, 0)

            pool.wait_ge(state_stored[0], 16 * (B // 2 + 1))
            pool.wait_ge(state_stored[1], 16 * (B // 2))
            pool.wait_ge(w_ready, 1)
            pool.indirect_dma_start(frec[:, :], None, states.rearrange("p t c -> (p t) c"),
                                    bass.IndirectOffsetOnAxis(ap=fixi[:, 0:1], axis=0))\
                .then_inc(f_in, 16)
            pool.indirect_dma_start(xf[:, :], None, x,
                                    bass.IndirectOffsetOnAxis(ap=dstg[:, 0:1], axis=0))\
                .then_inc(f_in, 16)

            for c in range(NCH - 1):
                pool.wait_ge(stored[c], 16 * (B + 1))

            last_row = pool.to_reg(N - 1)

            def scatter_block(par, n):
                pool.wait_ge(rows_in[par], 32 * n)
                tick(B + 2 * (n - 1) + par)
                for t in range(ET):
                    pool.indirect_dma_start(
                        out, bass.IndirectOffsetOnAxis(ap=idx[par][:, t:t + 1], axis=0),
                        X[par][:, t, :], None, bounds_check=last_row, oob_is_err=False)\
                        .then_inc(scattered[par], 16)

            with pool.Fori(1, B // 2 + 1) as n:
                scatter_block(0, n)
                scatter_block(1, n)
            scatter_block(0, B // 2 + 1)
            pool.wait_ge(f_row, 1)
            pool.indirect_dma_start(out, bass.IndirectOffsetOnAxis(ap=fixi[:, 1:2], axis=0),
                                    frow[:, 5, :], None, bounds_check=N - 1, oob_is_err=False)\
                .then_inc(f_out, 16)
            pool.wait_ge(scattered[0], 16 * ET * (B // 2 + 1))
            pool.wait_ge(scattered[1], 16 * ET * (B // 2))
            pool.wait_ge(f_out, 16)

        @block.tensor
        def _(pe):
            pe.wait_ge(consts_in, 16 * 20)
            pe.wait_ge(w_placed, 1)

            def fold(outp, m, i, n, edge):
                lc, lb, lo = pick[m]
                def r(t):
                    return flat(t[:, i:i + n, :])
                pe.matmul(outp, lc[:, :], r(gwqkv), start=True, stop=False)
                pe.matmul(outp, lb[:, :], r(wqkv), start=False, stop=False)
                if edge:
                    for a in range(n):
                        pe.matmul(outp[:, a * HC:(a + 1) * HC], place_edge[:, :], we[:, :],
                                  start=False, stop=False)
                pe.matmul(outp, lo[:, :], r(bqkv), start=False, stop=True)

            fold(q_ps[0:KD, 0:HC], KD, 0, 1, False)
            fold(k_ps[0:KS, 0:2 * HC], KS, 1, 2, True)
            pe.matmul(tp[0][:, 0:C], center2[:, :], gw1[:, :], start=True, stop=True)
            pe.matmul(hid_ps[:, 0:1], flat(w1[:, :, :]), gcol[:, 3:4], start=True, stop=True)\
              .then_inc(w_folded, 1)
            pe.wait_ge(w_ready, 1)

            def transposes(bank, m, srcs, done):
                for j, a in enumerate(srcs):
                    ins = pe.transpose(tp[bank][0:m, j * P:(j + 1) * P], a, ident[:, :])
                ins.then_inc(done, 1)

            def stage_1(s, par, n, first):
                for h in range(2):
                    if h == 0:
                        pe.wait_ge(eattr_in[par], 48 * n)
                        pe.wait_ge(zsrc_ready, s + 1)
                        if not first:
                            pe.wait_ge(agg_ev, 2 * s)
                    else:
                        pe.wait_ge(src_ev, 2 * s + 1)
                    transposes(0, KS, [aug_s[par][:, 4 * h + j, :] for j in range(4)], src_T)
                    if h == 0:
                        pe.wait_ge(zdst_ready, s + 1)
                    else:
                        pe.wait_ge(dst_ev, 2 * s + 1)
                    transposes(1, KD, [aug_d[:, 4 * h + j, :] for j in range(4)], dst_T)
                    pe.wait_ge(src_ev, 2 * s + h + 1)
                    if h or not first:
                        pe.wait_ge(qk_ready, 2 * s + h)
                        pe.wait_ge(q_evac, 2 * s + h)
                    for j in range(4):
                        pe.matmul(k_ps[:, j * P:(j + 1) * P], srcT[:, h, j * P:(j + 1) * P],
                                  wkv_s[:, 0, :], start=True, stop=True)
                    pe.wait_ge(dst_ev, 2 * s + h + 1)
                    for j in range(4):
                        ins = pe.matmul(q_ps[:, j * P:(j + 1) * P], dstT[:, h, j * P:(j + 1) * P],
                                        wq_s[:, :], start=True, stop=True)
                    ins.then_inc(qk_mm, 1)
                    if not first:
                        pe.wait_ge(wv_ready, 2 * (s - 1) + h + 1)
                    for j in range(4):
                        ins = pe.matmul(v_ps[h][:, j * P:(j + 1) * P],
                                        srcT[:, h, j * P:(j + 1) * P],
                                        wkv_s[:, 1, :], start=True, stop=True)
                    ins.then_inc(v_mm, 1)

            def mlp(s, stage1):
                u = NCH * (s - 1)
                for c in range(NCH):
                    bank = c % 2
                    if c == 2:
                        pe.wait_ge(z_ev, u + 1)
                    elif stage1:
                        pe.wait_ge((src_ev, dst_ev)[c], 2 * s + 2)
                    else:
                        pe.wait_ge(agg_ev, 2 * s)
                    pe.wait_ge(z2_ready, u + c + 1)
                    transposes(bank, P, [z2[:, c, j * P:(j + 1) * P] for j in range(4)], z_T)
                    pe.wait_ge(z_ev, u + c + 1)
                    if c:
                        pe.wait_ge(gelu_done, u + c)
                    pe.matmul(hid_ps[:, :], w1bd[:, :], z2T[:, c, :], start=True, stop=True)\
                      .then_inc(hid_mm, 1)
                    if c:
                        pe.wait_ge(out_ready, u + c)
                    else:
                        pe.wait_ge(o_targets, s)
                    pe.matmul(res_ps[:, :], ones_row[:, :], flat(b2row[:, :, :]),
                              start=True, stop=False)
                    pe.wait_ge(gelu_done, u + c + 1)
                    for j in range(4):
                        ins = pe.matmul(res_ps[:, j * P:(j + 1) * P], hid[:, c, j * P:(j + 1) * P],
                                        w2bd[:, :], start=False, stop=j == 3)
                    ins.then_inc(mlp_mm, 1)

            def project(s, stage2):
                pe.wait_ge(aggn_ready, s + 1)
                for h, bank in enumerate((1, 0)):
                    if stage2:
                        pe.wait_ge(z_ev, NCH * (s - 1) + 2 + h)
                    transposes(bank, P, [aggn[:, 4 * h + j, :] for j in range(4)], agg_T)
                if stage2:
                    pe.wait_ge(out_ready, NCH * s)
                for h in range(2):
                    pe.wait_ge(agg_ev, 2 * s + h + 1)
                    for j in range(4):
                        ins = pe.matmul(res_ps[:, (4 * h + j) * C:(4 * h + j + 1) * C],
                                        aggT[:, h, j * P:(j + 1) * P], wp[:, :],
                                        start=True, stop=True)
                ins.then_inc(proj_mm, 1)

            stage_1(0, 0, 1, True)
            project(0, False)
            with pe.Fori(0, B // 2) as k:
                for u in range(2):
                    s, par, n = 2 * k + 1 + u, 1 - u, k + 1 + u
                    stage_1(s, par, n, False)
                    mlp(s, True)
                    project(s, True)
            mlp(B, False)

            last = rec[(B - 1) % 2]
            pe.wait_ge(f_in, 32)
            pe.transpose(k_ps[:, 0:P], frec[:, 0:HC], ident[:, :])
            pe.transpose(k_ps[:, P:2 * P], last[:, ET - 1, 0:HC], ident[:, :])
            for i, a in enumerate((frec[:, HC:HC + H], frec[:, HC + H:SW],
                                   last[:, ET - 1, HC:HC + H], last[:, ET - 1, HC + H:SW])):
                pe.transpose(q_ps[0:H, i * P:(i + 1) * P], a, ident[:, :])
            for i in range(2):
                ins = pe.transpose(k_ps[0:H, (2 + i) * P:(3 + i) * P], fflag[:, i, :], ident[:, :])
            ins.then_inc(f_T, 1)
            pe.wait_ge(f_coef, 1)
            pe.matmul(v_ps[0][:, :], sel[:, :], flat(fk[:, 0:4, :]), start=True, stop=True)\
              .then_inc(f_bc, 1)
            pe.wait_ge(f_agg, 1)
            pe.matmul(v_ps[1][:, 0:C], fa[:, 2, :], wp[:, :], start=True, stop=True)\
              .then_inc(f_proj, 1)
            pe.wait_ge(f_z, 1)
            pe.transpose(v_ps[0][0:C, 0:P], frow[:, 3, :], ident[:, :]).then_inc(f_zT, 1)
            pe.wait_ge(f_zev, 1)
            pe.matmul(v_ps[1][0:C, P:2 * P], w1bd[0:C, 0:C], fzT[:, 0, :], start=True, stop=True)\
              .then_inc(f_hid, 1)
            pe.wait_ge(f_gelu, 1)
            pe.matmul(q_ps[:, 0:C], ones_row[:, :], b2row[:, 0, :], start=True, stop=False)
            pe.matmul(q_ps[:, 0:C], fzT[:, 1, :], w2bd[0:C, 0:C], start=False, stop=True)\
              .then_inc(f_mlp, 1)

        @block.scalar
        def _(act):
            def stage_1(s):
                for h in range(2):
                    act.wait_ge(src_T, 2 * s + h + 1)
                    act.activation(srcT[:, h, :], tp[0][0:KS, :], ACT.Copy).then_inc(src_ev, 1)
                    act.wait_ge(dst_T, 2 * s + h + 1)
                    act.activation(dstT[:, h, :], tp[1][0:KD, :], ACT.Copy).then_inc(dst_ev, 1)
                    act.wait_ge(qk_mm, 2 * s + h + 1)
                    act.activation(q_sb[:, h, :], q_ps[:, :], ACT.Copy).then_inc(q_evac, 1)
                act.wait_ge(ex_ready, s + 1)
                act.activation(cw[:, :, :, 1:ET + 1].rearrange("p a h t -> p (a h) t"),
                               ex[:, :, :, :].rearrange("p a h t -> p (a h) t"), ACT.Exp)\
                   .then_inc(cw_ready, 1)

            def mlp(s):
                u = NCH * (s - 1)
                for c in range(NCH):
                    act.wait_ge(z_T, u + c + 1)
                    act.activation(z2T[:, c, :], tp[c % 2][:, :], ACT.Copy).then_inc(z_ev, 1)
                    act.wait_ge(hid_mm, u + c + 1)
                    act.activation(hid[:, c, :], hid_ps[:, :], ACT.Gelu, bias=b1g[:, 0:1])\
                       .then_inc(gelu_done, 1)

            def project(s):
                for h in range(2):
                    act.wait_ge(agg_T, 2 * s + h + 1)
                    act.activation(aggT[:, h, :], tp[1 - h][:, :], ACT.Copy).then_inc(agg_ev, 1)

            def relus(s):
                for i, (a, z) in enumerate(((S0, XT), (0, NT))):
                    act.wait_ge(centered, 2 * s + i + 1)
                    act.activation(Y[:, a:z, :], Y[:, a:z, :], ACT.Relu).then_inc(relued, 1)

            def roots(s, stage1, stage2):
                if stage1:
                    act.wait_ge(y_var, s + 1)
                if stage2:
                    act.wait_ge(o_var, s)
                act.activation(sd[:, :], vars_[:, :], ACT.Sqrt).then_inc(sd_ready, 1)

            relus(0)
            roots(0, True, False)
            stage_1(0)
            project(0)
            with act.Fori(0, B // 2) as k:
                for u in range(2):
                    s = 2 * k + 1 + u
                    relus(s)
                    roots(s, True, True)
                    stage_1(s)
                    mlp(s)
                    project(s)
            roots(B, False, True)
            mlp(B)
            act.wait_ge(f_exp_in, 1)
            act.activation(fcw[:, :, :], fex[:, :, :], ACT.Exp).then_inc(f_exp, 1)
            for i in range(2):
                act.wait_ge(f_var, i + 1)
                act.activation(fsc[:, 5 + 6 * i:6 + 6 * i], fsc[:, 4 + 6 * i:5 + 6 * i], ACT.Sqrt)\
                   .then_inc(f_sd, 1)
            act.wait_ge(f_zT, 1)
            act.activation(fzT[:, 0, :], v_ps[0][0:C, 0:P], ACT.Copy).then_inc(f_zev, 1)
            act.wait_ge(f_hid, 1)
            act.activation(fzT[:, 1, :], v_ps[1][0:C, P:2 * P], ACT.Gelu, bias=b1g[0:C, 0:1])\
               .then_inc(f_gelu, 1)

        @block.vector
        def _(dve):
            linked = [0]

            def link(ins):
                linked[0] += 1
                ins.then_inc(link_done, 1)
                dve.wait_ge(link_done, linked[0])

            dve.memset(dsti[:, :], N)
            dve.memset(dstg[:, :], 0)
            dve.memset(srci[:, :], 0).then_inc(pads_set, 1)
            for t in [w2bd[:, :], w1bd[:, :], place_edge[:, :], cw[:, :, :, :], den[1][:, :, :],
                      rec[1][:, :, :], dj[:, :], aj[:, :],
                      *(u[:, :] for m in (KS, KD) for u in pick[m])]:
                dve.memset(t, 0.0)
            dve.memset(vars_[:, :], 1.0)
            dve.memset(mx[1][:, :, :], NEG)
            dve.memset(mj[:, :], NEG)
            dve.memset(ones_row[:, :], 1.0)
            for i in range(2):
                dve.memset(aug_s[i][:, :, C + ED:KS], 1.0)
            dve.memset(keepm[:, :, :, 0:1], NEG)
            dve.memset(aug_d[:, :, C:KD], 1.0).then_inc(pads_set, 1)
            dve.wait_ge(pads_set, 2)

            dve.wait_ge(tables_in, 7 * 16)
            link(dve.tensor_copy(dstf[:, :], dsti[:, :]))
            link(dve.tensor_scalar(dstg[:, 0:EPP], dstf[:, 1:EPP + 1], float(N - 1), None, ALU.min))
            for b in range(2):
                dve.tensor_copy(idx[b][:, 0:ET], srci[:, b * ET:(b + 1) * ET])
                dve.tensor_copy(idx[b][:, ET:2 * ET], dstg[:, b * ET:(b + 1) * ET])\
                   .then_inc(idx_ready, 1)
            link(dve.tensor_tensor(same[:, :], dstf[:, 0:EPP + 1], dstf[:, 1:EPP + 2], ALU.is_equal))
            for h in range(H):
                ins = dve.tensor_scalar(keepm[:, :, h, 1:ET + 1],
                                        same[:, 0:EPP].rearrange("p (b t) -> p b t", t=ET),
                                        1.0, -NEG, ALU.subtract, ALU.mult)
            link(ins)
            dve.memset(keepm[:, 0, :, 1:2], NEG)
            link(dve.tensor_scalar(firstseg[:, :], dstf[:, 1:EPP + 1], dstf[:, 1:2], None,
                                   ALU.is_equal))
            link(dve.tensor_scalar(nofinal[:, :], firstseg[:, :], same[:, 0:1], None, ALU.mult))
            link(dve.tensor_tensor(nofinal[:, :], nofinal[:, :], same[:, 1:EPP + 1], ALU.max))
            link(dve.scalar_tensor_tensor(scati[:, :], nofinal[:, :], FAR, dstf[:, 1:EPP + 1],
                                          ALU.mult, ALU.add))
            link(dve.tensor_reduce(fix[:, 0:1], firstseg[:, :], AX.X, ALU.add))
            dve.wait_ge(built, 6)
            filled = firstseg[:, EPP - 1:EPP]
            dve.tensor_tensor(fixi[:, 0:1], fix[:, 0:1], rowbase[:, :], ALU.add)
            dve.tensor_tensor(fix[:, 1:2], filled, same[:, 0:1], ALU.mult)
            link(dve.tensor_tensor(fix[:, 2:3], filled, same[:, EPP:EPP + 1], ALU.mult))
            link(dve.tensor_scalar(fix[:, 3:4], fix[:, 2:3], -1.0, 1.0, ALU.mult, ALU.add))
            link(dve.tensor_tensor(fix[:, 3:4], fix[:, 3:4], same[:, 0:1], ALU.mult))
            link(dve.tensor_scalar(fix[:, 4:5], fix[:, 3:4], -FAR, FAR, ALU.mult, ALU.add))
            dve.tensor_tensor(fixi[:, 1:2], fix[:, 4:5], dstf[:, 1:2], ALU.add)
            for h in range(H):
                dve.tensor_copy(fflag[:, 0, h:h + 1], fix[:, 1:2])
                dve.tensor_copy(fflag[:, 1, h:h + 1], same[:, 0:1])

            dve.wait_ge(consts_in, 16 * 20)
            link(dve.tensor_scalar(center[:, :], ident[0:C, 0:C], -1.0 / C, None, ALU.add))
            for m in (KS, KD):
                dve.tensor_copy(pick[m][0][:, 0:C], center[:, :])
                dve.tensor_copy(pick[m][1][:, m - 1:m], gcol[:, 1:2])
                dve.memset(pick[m][2][:, m - 1:m], 1.0)
            for h in range(2):
                dve.tensor_copy(center2[:, h * C:(h + 1) * C], center[:, :])
            dve.tensor_copy(place_edge[:, C:C + ED], ident[0:ED, 0:ED])
            dve.tensor_scalar(gwqkv[:, :, :], wqkv[:, :, :], gcol[:, 0:1], None, ALU.mult)
            dve.tensor_scalar(gw1[:, :], w1[:, 0, :], gcol[:, 2:3], None, ALU.mult)\
               .then_inc(w_placed, 1)
            dve.wait_ge(w_folded, 1)
            dve.tensor_scalar(wq_s[:, :], q_ps[0:KD, 0:HC], float(C) ** -0.5, None, ALU.mult)
            dve.tensor_copy(flat(wkv_s[:, :, :]), k_ps[0:KS, 0:2 * HC])
            for h in range(2):
                a, z = h * C, (h + 1) * C
                dve.tensor_copy(w1bd[a:z, a:z], tp[0][a:z, 0:C])
            dve.tensor_tensor(b1g[:, :], b1col[:, :], hid_ps[:, 0:1], ALU.add).then_inc(w_ready, 1)

            def variances(st, w, sums, diff2, n, mean_to=None, mean_done=None):
                dve.tensor_tensor(w[:, 1, :], st[:, :, 1], st[:, :, 4], ALU.subtract)
                if mean_to is not None:
                    dve.tensor_tensor(w[:, 0, :], st[:, :, 1], st[:, :, 4], ALU.add)
                dve.tensor_tensor(w[:, 2, :], st[:, :, 2], st[:, :, 5], ALU.add).then_inc(sums, 1)
                dve.wait_ge(sums, n)
                if mean_to is not None:
                    dve.tensor_scalar(mean_to, w[:, 0, :], 0.5, None, ALU.mult)\
                       .then_inc(mean_done, 1)
                dve.tensor_tensor(w[:, 1, :], w[:, 1, :], w[:, 1, :], ALU.mult).then_inc(diff2, 1)
                dve.wait_ge(diff2, n)
                return dve.scalar_tensor_tensor(w[:, 3, :], w[:, 1, :], float(C // 4), w[:, 2, :],
                                                ALU.mult, ALU.add)

            def norms(s, par, n, refill):
                Xp = X[par]
                dve.wait_ge(dense_in[par], 32 * n)
                dve.wait_ge(gathered[par], 32 * ET * n)
                for t in range(XT):
                    ins = dve.bn_stats(xst[:, t, :], Xp[:, t, :])
                ins.then_inc(x_stats, 1)
                if refill:
                    dve.tensor_copy(idx[par][:, 0:ET], srci[:, bass.ds((s + 2) * ET, ET)])
                    dve.tensor_copy(idx[par][:, ET:2 * ET], dstg[:, bass.ds((s + 2) * ET, ET)])\
                       .then_inc(idx_ready, 1)
                dve.wait_ge(x_stats, s + 1)
                variances(xst, sm, x_sums, x_diff2, s + 1, mean[:, :], x_mean).then_inc(x_v64, 1)
                dve.wait_ge(x_mean, s + 1)
                for a, z in ((S0, XT), (0, NT)):
                    dve.tensor_tensor(Y[:, a:z, :], Xp[:, a:z, :], wide(mean[:, a:z], C),
                                      ALU.subtract).then_inc(centered, 1)
                dve.wait_ge(x_v64, s + 1)
                dve.tensor_scalar(vars_[:, 0:XT], sm[:, 3, :], 1.0 / C, EPS, ALU.mult, ALU.add)\
                   .then_inc(x_var, 1)
                dve.wait_ge(relued, 2 * s + 1)
                for t in range(2 * ET):
                    ins = dve.bn_stats(yst[:, t, :], Y[:, S0 + t, :])
                ins.then_inc(y_stats, 1)
                dve.wait_ge(x_var, s + 1)
                dve.tensor_scalar(sm2[:, 0, :], vars_[:, S0:XT], EPS, None, ALU.mult)
                dve.wait_ge(y_stats, s + 1)
                variances(yst, sm2, y_sums, y_diff2, s + 1).then_inc(y_v64, 1)
                dve.wait_ge(y_v64, s + 1)
                dve.scalar_tensor_tensor(vars_[:, XT:OV], sm2[:, 3, :], 1.0 / C, sm2[:, 0, :],
                                         ALU.mult, ALU.add).then_inc(y_var, 1)

            def inverse_roots(s):
                dve.wait_ge(sd_ready, s + 1)
                dve.reciprocal(rs[:, :], sd[:, :]).then_inc(rs_ready, 1)
                dve.wait_ge(rs_ready, s + 1)

            def z_second(s, par):
                for c in range(NCH):
                    dve.tensor_tensor(tiles(z2[:, c, :]), O[1 - par][:, 8 * c:8 * c + 8, :],
                                      wide(rs[:, OV + 8 * c:OV + 8 * c + 8], C), ALU.mult)\
                       .then_inc(z2_ready, 1)

            def final_chunk(s, c, par, early=False):
                dve.wait_ge(mlp_mm, NCH * (s - 1) + c + 1)
                if not early:
                    dve.wait_ge(stored[c], 16 * (s - 1))
                dve.tensor_tensor(tiles(OUTS[:, c, :]), tiles(res_ps[:, :]),
                                  XO[1 - par][:, 8 * c:8 * c + 8, :], ALU.add)\
                   .then_inc(out_ready, 1)

            def attention(s, par, n, early, stage2):
                Xp, Op, XOp, R = X[par], O[par], XO[par], rec[par]
                dve.tensor_tensor(aug_s[par][:, :, 0:C], Y[:, S0:D0, :],
                                  wide(rs[:, XT:XT + ET], C), ALU.mult).then_inc(zsrc_ready, 1)
                dve.tensor_tensor(aug_d[:, :, 0:C], Y[:, D0:XT, :],
                                  wide(rs[:, XT + ET:OV], C), ALU.mult).then_inc(zdst_ready, 1)
                if stage2:
                    z_second(s, par)
                dve.wait_ge(relued, 2 * s + 2)
                dve.tensor_tensor(Op[:, 0:NT, :], Y[:, 0:NT, :], wide(rs[:, 0:NT], C), ALU.mult)
                dve.tensor_tensor(Op[:, NT:OT, :], Y[:, D0:XT, :], wide(rs[:, D0:XT], C),
                                  ALU.mult).then_inc(o_scaled, 1)
                for h in range(2):
                    dve.wait_ge(q_evac, 2 * s + h + 1)
                    dve.tensor_tensor(qk[:, 4 * h:4 * h + 4, :].rearrange("p t c -> p (t c)"),
                                      k_ps[:, :], q_sb[:, h, :], ALU.mult).then_inc(qk_ready, 1)
                dve.wait_ge(o_scaled, s + 1)
                dve.tensor_tensor(Op[:, :, :], Op[:, :, :], rows(bp_b[:, :], OT), ALU.add)\
                   .then_inc(o_nodes, 1)
                dve.wait_ge(qk_ready, 2 * s + 2)
                dve.tensor_reduce(alpha[:, :, 1:ET + 1].rearrange("p h t -> p t h"),
                                  qk[:, :, :].rearrange("p t (h c) -> p t h c", h=H),
                                  AX.X, ALU.add)
                dve.tensor_copy(alpha[:, :, 0:1], mx[1 - par][:, :, ET:ET + 1])\
                   .then_inc(alpha_ready, 1)
                dve.wait_ge(alpha_ready, s + 1)
                m = mx[par]
                dve.tensor_tensor_scan(flat(m[:, :, :]),
                                       keepm[:, bass.ds(s, 1), :, :]
                                       .rearrange("p b h t -> p (b h t)"),
                                       flat(alpha[:, :, :]), NEG, ALU.add, ALU.max)\
                   .then_inc(mx_ready, 1)
                dve.wait_ge(mx_ready, s + 1)
                dve.tensor_tensor(ex[:, 0, :, :], m[:, :, 0:ET], m[:, :, 1:ET + 1],
                                  ALU.subtract).then_inc(mx_diff, 1)
                dve.tensor_tensor(ex[:, 1, :, :], alpha[:, :, 1:ET + 1], m[:, :, 1:ET + 1],
                                  ALU.subtract)
                dve.wait_ge(mx_diff, s + 1)
                dve.tensor_tensor(ex[:, 0, :, :], ex[:, 0, :, :],
                                  keepm[:, bass.ds(s, 1), :, 1:ET + 1]
                                  .rearrange("p b h t -> p (b h) t"), ALU.add)\
                   .then_inc(ex_ready, 1)
                dve.wait_ge(o_nodes, s + 1)
                for t in range(NT):
                    dve.bn_stats(ost[:, t, :], Op[:, t, :])
                dve.tensor_tensor(XOp[:, 0:NT, :], Xp[:, 0:NT, :], Op[:, 0:NT, :], ALU.add)\
                   .then_inc(x_nodes_free, 1)
                dve.wait_ge(cw_ready, s + 1)
                dve.tensor_copy(cw[:, 1, :, 0:1], den[1 - par][:, :, ET:ET + 1])\
                   .then_inc(den_prev_in, 1)
                if stage2:
                    final_chunk(s, 0, par, early)
                if not early:
                    dve.wait_ge(state_stored[par], 16 * (n - 1))
                for h in range(2):
                    dve.wait_ge(v_mm, 2 * s + h + 1)
                    for g in range(H):
                        ins = dve.tensor_tensor(
                            R[:, 4 * h:4 * h + 4, g * C:(g + 1) * C],
                            v_ps[h][:, :].rearrange("p (t c) -> p t c", c=HC)
                            [:, :, g * C:(g + 1) * C],
                            wide(cw[:, 1, g, 1 + 4 * h:5 + 4 * h], C), ALU.mult)
                    ins.then_inc(wv_ready, 1)
                dve.wait_ge(den_prev_in, s + 1)
                dve.tensor_tensor_scan(flat(den[par][:, :, :]), flat(cw[:, 0, :, :]),
                                       flat(cw[:, 1, :, :]), 0.0, ALU.mult, ALU.add)\
                   .then_inc(den_ready, 1)
                dve.wait_ge(wv_ready, 2 * s + 2)
                for t in range(ET):
                    prev = rec[1 - par][:, ET - 1, :] if t == 0 else R[:, t - 1, :]
                    if t > 0:
                        dve.wait_ge(chain, ET * s + t)
                    for h in range(H):
                        a, z = h * C, (h + 1) * C
                        ins = dve.scalar_tensor_tensor(R[:, t, a:z], prev[:, a:z],
                                                       cw[:, 0, h, t + 1:t + 2], R[:, t, a:z],
                                                       ALU.mult, ALU.add)
                    ins.then_inc(chain, 1)
                    if t == 0:
                        dve.wait_ge(den_ready, s + 1)
                        dve.tensor_scalar(rden[:, 0, :, :], den[par][:, :, 1:ET + 1], 1e-8,
                                          None, ALU.add).then_inc(den_eps, 1)
                        dve.tensor_copy(R[:, :, HC:HC + H].rearrange("p t h -> p h t"),
                                        m[:, :, 1:ET + 1])
                        dve.tensor_copy(R[:, :, HC + H:SW].rearrange("p t h -> p h t"),
                                        den[par][:, :, 1:ET + 1])
                    if t == 1:
                        dve.wait_ge(den_eps, s + 1)
                        dve.reciprocal(rden[:, 1, :, :], rden[:, 0, :, :]).then_inc(rden_ready, 1)
                    if stage2 and t in (3, 5):
                        final_chunk(s, (t - 1) // 2, par, early)
                dve.wait_ge(chain, ET * (s + 1))
                dve.wait_ge(rden_ready, s + 1)
                for g in range(H):
                    a, z = g * C, (g + 1) * C
                    ins = dve.tensor_tensor(aggn[:, :, a:z], R[:, :, a:z],
                                            wide(rden[:, 1, g, :], C), ALU.mult)
                ins.then_inc(aggn_ready, 1)
                dve.wait_ge(proj_mm, s + 1)
                dve.tensor_tensor(Op[:, NT:OT, :], tiles(res_ps[:, :]), Op[:, NT:OT, :],
                                  ALU.add).then_inc(o_targets, 1)
                dve.wait_ge(o_targets, s + 1)
                for t in range(NT, OT):
                    ins = dve.bn_stats(ost[:, t, :], Op[:, t, :])
                ins.then_inc(o_stats, 1)
                dve.tensor_tensor(XOp[:, NT:OT, :], Xp[:, D0:XT, :], Op[:, NT:OT, :], ALU.add)\
                   .then_inc(x_edges_free, 1)
                dve.wait_ge(o_stats, s + 1)
                variances(ost, sm3, o_sums, o_diff2, s + 1).then_inc(o_v64, 1)
                dve.wait_ge(o_v64, s + 1)
                dve.tensor_scalar(vars_[:, OV:VN], sm3[:, 3, :], 1.0 / C, EPS, ALU.mult, ALU.add)\
                   .then_inc(o_var, 1)

            def step(s, par, n, early=False, stage2=True, refill=True):
                norms(s, par, n, refill)
                inverse_roots(s)
                attention(s, par, n, early, stage2)

            step(0, 0, 1, early=True, stage2=False)
            step(1, 1, 1, early=True)
            step(2, 0, 2)
            with dve.Fori(1, B // 2) as k:
                step(2 * k + 1, 1, k + 1)
                step(2 * k + 2, 0, k + 2)
            inverse_roots(B)
            z_second(B, B % 2)
            for c in range(NCH):
                final_chunk(B, c, B % 2)

            steps = [0]

            def flink(ins, to=None):
                if to is None:
                    steps[0] += 1
                    ins.then_inc(f_link, 1)
                    dve.wait_ge(f_link, steps[0])
                else:
                    ins.then_inc(to, 1)

            dve.wait_ge(f_T, 1)
            dve.tensor_copy(flat(fT[:, :, :]), k_ps[:, 0:2 * P])
            dve.tensor_copy(flat(fsm[:, 0:4, :]), q_ps[0:H, :])
            flink(dve.tensor_scalar(flat(fkeep[:, :, :]), k_ps[0:H, 2 * P:4 * P], 1.0, -NEG,
                                    ALU.subtract, ALU.mult))
            mF, dF, mL, dL = (fsm[:, i, :] for i in range(4))
            flink(dve.tensor_tensor_scan(mj[:, 1:P + 1], fkeep[:, 0, :], mL, NEG, ALU.add, ALU.max))
            dve.tensor_tensor(fk[:, 4, :], mj[:, 0:P], fkeep[:, 1, :], ALU.add)
            dve.tensor_tensor(fk[:, 5, :], mj[:, 0:P], mj[:, 1:P + 1], ALU.subtract)
            flink(dve.tensor_tensor(fex[:, 1, :], mL, mj[:, 1:P + 1], ALU.subtract))
            flink(dve.tensor_tensor(fk[:, 6, :], fk[:, 4, :], mF, ALU.max))
            dve.tensor_tensor(fex[:, 0, :], fk[:, 5, :], fkeep[:, 0, :], ALU.add)
            dve.tensor_tensor(fex[:, 2, :], mF, fk[:, 6, :], ALU.subtract)
            flink(dve.tensor_tensor(fex[:, 3, :], fk[:, 4, :], fk[:, 6, :], ALU.subtract), f_exp_in)
            dve.wait_ge(f_exp, 1)
            flink(dve.tensor_tensor(fk[:, 4, :], fcw[:, 1, :], dL, ALU.mult))
            flink(dve.tensor_tensor_scan(dj[:, 1:P + 1], fcw[:, 0, :], fk[:, 4, :], 0.0,
                                         ALU.mult, ALU.add))
            dve.tensor_tensor(fk[:, 5, :], dF, fcw[:, 2, :], ALU.mult)
            flink(dve.tensor_tensor(fk[:, 6, :], dj[:, 0:P], fcw[:, 3, :], ALU.mult))
            flink(dve.tensor_tensor(fk[:, 5, :], fk[:, 5, :], fk[:, 6, :], ALU.add))
            flink(dve.tensor_scalar(fk[:, 6, :], fk[:, 5, :], 1e-8, None, ALU.add))
            flink(dve.reciprocal(fk[:, 7, :], fk[:, 6, :]))
            dve.tensor_copy(flat(fk[:, 0:2, :]), flat(fcw[:, 0:2, :]))
            dve.tensor_tensor(fk[:, 2, :], fcw[:, 2, :], fk[:, 7, :], ALU.mult)
            flink(dve.tensor_tensor(fk[:, 3, :], fcw[:, 3, :], fk[:, 7, :], ALU.mult), f_coef)
            dve.wait_ge(f_bc, 1)
            flink(dve.tensor_copy(flat(bc[:, :, :]), v_ps[0][:, :]))
            dve.tensor_tensor(fa[:, 1, :], fT[:, 0, :], bc[:, 2, :], ALU.mult)
            flink(dve.tensor_tensor(fa[:, 0, :], fT[:, 1, :], bc[:, 1, :], ALU.mult))
            flink(dve.tensor_tensor_scan(aj[:, 1:P + 1], bc[:, 0, :], fa[:, 0, :], 0.0,
                                         ALU.mult, ALU.add))
            flink(dve.tensor_tensor(fa[:, 0, :], aj[:, 0:P], bc[:, 3, :], ALU.mult))
            flink(dve.tensor_tensor(fa[:, 2, :], fa[:, 0, :], fa[:, 1, :], ALU.add), f_agg)

            def small_variance(row, c):
                flink(dve.bn_stats(fst[:, :], row))
                flink(dve.tensor_tensor(fsc[:, c:c + 1], fst[:, 1:2], fst[:, 4:5], ALU.subtract))
                dve.tensor_tensor(fsc[:, c + 1:c + 2], fst[:, 1:2], fst[:, 4:5], ALU.add)
                dve.tensor_tensor(fsc[:, c + 2:c + 3], fst[:, 2:3], fst[:, 5:6], ALU.add)
                flink(dve.tensor_tensor(fsc[:, c:c + 1], fsc[:, c:c + 1], fsc[:, c:c + 1],
                                        ALU.mult))
                dve.tensor_scalar(fsc[:, c + 1:c + 2], fsc[:, c + 1:c + 2], 0.5, None, ALU.mult)
                flink(dve.scalar_tensor_tensor(fsc[:, c + 3:c + 4], fsc[:, c:c + 1],
                                               float(C // 4), fsc[:, c + 2:c + 3],
                                               ALU.mult, ALU.add))
                flink(dve.tensor_scalar(fsc[:, c + 4:c + 5], fsc[:, c + 3:c + 4], 1.0 / C, EPS,
                                        ALU.mult, ALU.add), f_var)

            dve.wait_ge(f_in, 32)
            small_variance(xf[:, :], 0)
            flink(dve.tensor_scalar(frow[:, 0, :], xf[:, :], fsc[:, 1:2], 0.0,
                                    ALU.subtract, ALU.max))
            dve.wait_ge(f_sd, 1)
            flink(dve.reciprocal(fsc[:, 3:4], fsc[:, 5:6]))
            flink(dve.scalar_tensor_tensor(frow[:, 1, :], frow[:, 0, :], fsc[:, 3:4], bp_b[:, :],
                                           ALU.mult, ALU.add))
            dve.wait_ge(f_proj, 1)
            flink(dve.tensor_tensor(frow[:, 2, :], v_ps[1][:, 0:C], frow[:, 1, :], ALU.add))
            small_variance(frow[:, 2, :], 6)
            flink(dve.tensor_tensor(frow[:, 4, :], frow[:, 2, :], xf[:, :], ALU.add))
            dve.wait_ge(f_sd, 2)
            flink(dve.reciprocal(fsc[:, 9:10], fsc[:, 11:12]))
            flink(dve.tensor_scalar(frow[:, 3, :], frow[:, 2, :], fsc[:, 9:10], None, ALU.mult),
                  f_z)
            dve.wait_ge(f_mlp, 1)
            flink(dve.tensor_tensor(frow[:, 5, :], q_ps[:, 0:C], frow[:, 4, :], ALU.add), f_row)


_W = ["Wq", "bq", "Wk", "bk", "Wv", "bv", "We", "Wp", "bp", "ln1_g", "ln1_b", "ln2_g", "ln2_b",
      "W1", "b1", "W2", "b2"]
_INS = ["x", "src", "dst", "edge_attr_32"] + [f"L0_gnn_{n}" for n in _W]


def kernel(**inputs):
    import numpy as _np
    import concourse.bacc as _bacc
    from concourse import mybir as _mybir
    from concourse.bass_utils import run_bass_kernel_spmd as _run

    nc = _bacc.Bacc("TRN2", target_bir_lowering=False, num_devices=1)
    f32 = _mybir.dt.float32
    arrays, args = {}, []
    for name in _INS:
        a = _np.ascontiguousarray(inputs[name])
        arrays[f"in_{name}"] = a
        args.append(nc.dram_tensor(f"in_{name}", a.shape, _mybir.dt.from_np(a.dtype),
                                   kind="ExternalInput").ap())
    n, c = inputs["x"].shape
    e = inputs["src"].shape[0]
    per = -(-e // (128 * 8)) * 8
    edge_rows = nc.dram_tensor("edge_rows", (128, per, c), f32, kind="Internal").ap()
    states = nc.dram_tensor("states", (128, per, 2 * c + 4), f32, kind="Internal").ap()
    out = nc.dram_tensor("out_0", (n, c), f32, kind="ExternalOutput").ap()
    gnn_layer(nc, *args, edge_rows, states, out)
    r = _run(nc, [arrays], core_ids=[0])
    return r.results[0]["out_0"]
```

```python
import concourse.bass as bass
from concourse import mybir
from contextlib import ExitStack



def gnn_layer(nc, x, src, dst, eattr, Wq, bq, Wk, bk, Wv, bv, We, Wp, bp,
              g1, be1, g2, be2, W1, b1, W2, b2, edge_rows, states, out):
    f32 = mybir.dt.float32
    i32 = mybir.dt.int32
    ALU = mybir.AluOpType
    ACT = mybir.ActivationFunctionType
    AX = mybir.AxisListType

    P = 128
    N, C = x.shape
    E, ED = eattr.shape
    H = 2
    HC = H * C
    NT, ET = 16, 8
    B = -(-E // (P * ET))
    EPP = B * ET
    PF = E // EPP
    EL = E - PF * EPP
    FULL_EA = EL // ET
    XT = NT + 2 * ET
    S0, D0 = NT, NT + ET
    OT = NT + ET
    NCH = OT // 8
    EPS = 1e-5
    FAR = float(2 ** 20)
    NEG = -1e30
    ROWS = P * NT
    LASTROWS = N - (B - 1) * ROWS
    LASTP = LASTROWS // NT
    SW = HC + 2 * H
    assert PF == P - 1 and EL % ET == 0 and LASTP * NT == LASTROWS and B % 2 == 1
    KS = C + ED + 1
    KD = C + 1

    ctx = ExitStack()
    with ctx:
        def sb(name, shape, dt=f32):
            return ctx.enter_context(nc.sbuf_tensor(name, shape, dt))

        def pb(name, shape):
            return ctx.enter_context(nc.psum_tensor(name, shape, f32))

        def sem(name):
            return ctx.enter_context(nc.semaphore(name))

        ident = sb("ident", [P, P])
        center = sb("center", [C, C])
        pick = {m: (sb(f"place_center_{m}", [C, m]), sb(f"place_bias_{m}", [C, m]),
                    sb(f"place_one_{m}", [1, m])) for m in (KS, KD)}
        center2 = sb("center2", [C, 2 * C])
        place_edge = sb("place_edge", [ED, KS])
        gcol = sb("gcol", [C, 4])
        wqkv = sb("wqkv", [C, 3, HC])
        gwqkv = sb("gwqkv", [C, 3, HC])
        bqkv = sb("bqkv", [1, 3, HC])
        we = sb("we", [ED, HC])
        wq_s = sb("wq_s", [KD, HC])
        wkv_s = sb("wkv_s", [KS, 2, HC])
        wp = sb("wp", [HC, C])
        w1 = sb("w1", [C, 2, C])
        gw1 = sb("gw1", [C, C])
        w1bd = sb("w1bd", [P, P])
        w2bd = sb("w2bd", [P, P])
        b1col = sb("b1col", [P, 1])
        b1g = sb("b1g", [P, 1])
        bp_b = sb("bp_b", [P, C])
        b2row = sb("b2row", [1, 8, C])
        ones_row = sb("ones_row", [1, P])
        sel = sb("sel", [H, P])

        dsti = sb("dsti", [P, EPP + 2], i32)
        srci = sb("srci", [P, EPP + 16], i32)
        dstg = sb("dstg", [P, EPP + 16], i32)
        dstf = sb("dstf", [P, EPP + 2])
        same = sb("same", [P, EPP + 1])
        firstseg = sb("firstseg", [P, EPP])
        nofinal = sb("nofinal", [P, EPP])
        scati = sb("scati", [P, EPP], i32)
        keepm = sb("keepm", [P, B, H, ET + 1])
        fix = sb("fix", [P, 8])
        fixi = sb("fixi", [P, 2], i32)
        rowbase = sb("rowbase", [P, 1])
        idx = [sb(f"idx{i}", [P, 2 * ET], i32) for i in range(2)]

        X = [sb(f"X{i}", [P, XT, C]) for i in range(2)]
        Y = sb("Y", [P, XT, C])
        aug_s = [sb(f"aug_s{i}", [P, ET, KS]) for i in range(2)]
        aug_d = sb("aug_d", [P, ET, KD])
        O = [sb(f"O{i}", [P, OT, C]) for i in range(2)]
        XO = [sb(f"XO{i}", [P, OT, C]) for i in range(2)]
        XE = [sb(f"XE{i}", [P, ET, C]) for i in range(2)]
        OUTS = sb("OUTS", [P, NCH, 8 * C])
        rec = [sb(f"rec{i}", [P, ET, SW]) for i in range(2)]
        xst = sb("xst", [P, XT, 6])
        yst = sb("yst", [P, 2 * ET, 6])
        ost = sb("ost", [P, OT, 6])
        sm = sb("sm", [P, 4, XT])
        mean = sb("mean", [P, XT])
        sm2 = sb("sm2", [P, 4, 2 * ET])
        sm3 = sb("sm3", [P, 4, OT])
        VN = XT + 2 * ET + OT
        OV = XT + 2 * ET
        vars_ = sb("vars_", [P, VN])
        sd = sb("sd", [P, VN])
        rs = sb("rs", [P, VN])
        srcT = sb("srcT", [KS, 2, 512])
        dstT = sb("dstT", [KD, 2, 512])
        q_sb = sb("q_sb", [P, 2, 4 * HC])
        qk = sb("qk", [P, ET, HC])
        alpha = sb("alpha", [P, H, ET + 1])
        mx = [sb(f"mx{i}", [P, H, ET + 1]) for i in range(2)]
        den = [sb(f"den{i}", [P, H, ET + 1]) for i in range(2)]
        ex = sb("ex", [P, 2, H, ET])
        cw = sb("cw", [P, 2, H, ET + 1])
        rden = sb("rden", [P, 2, H, ET])
        aggn = sb("aggn", [P, ET, HC])
        aggT = sb("aggT", [P, 2, 512])
        z2 = sb("z2", [P, NCH, 8 * C])
        z2T = sb("z2T", [P, NCH, 512])
        hid = sb("hid", [P, NCH, 512])
        ticks = sb("ticks", [P, 3])
        frec = sb("frec", [P, SW])
        xf = sb("xf", [P, C])
        fT = sb("fT", [P, 2, P])
        fsm = sb("fsm", [H, 6, P])
        fkeep = sb("fkeep", [H, 2, P])
        mj = sb("mj", [H, P + 1])
        dj = sb("dj", [H, P + 1])
        fk = sb("fk", [H, 8, P])
        fex = sb("fex", [H, 4, P])
        fcw = sb("fcw", [H, 4, P])
        bc = sb("bc", [P, 4, P])
        aj = sb("aj", [P, P + 1])
        fa = sb("fa", [P, 3, P])
        fflag = sb("fflag", [P, 2, H])
        frow = sb("frow", [P, 6, C])
        fst = sb("fst", [P, 6])
        fsc = sb("fsc", [P, 12])
        fzT = sb("fzT", [C, 2, P])

        tp = [pb(f"tp{i}", [P, 512]) for i in range(2)]
        k_ps = pb("k_ps", [P, 512])
        q_ps = pb("q_ps", [P, 512])
        v_ps = [pb(f"v_ps{i}", [P, 512]) for i in range(2)]
        hid_ps = pb("hid_ps", [P, 512])
        res_ps = pb("res_ps", [P, 512])

        pads_set = sem("pads_set")
        tables_in = sem("tables_in")
        consts_in = sem("consts_in")
        built = sem("built")
        link_done = sem("link_done")
        w_placed = sem("w_placed")
        w_folded = sem("w_folded")
        w_ready = sem("w_ready")
        idx_ready = sem("idx_ready")
        dense_in = [sem(f"dense_in{i}") for i in range(2)]
        eattr_in = [sem(f"eattr_in{i}") for i in range(2)]
        gathered = [sem(f"gathered{i}") for i in range(2)]
        x_stats = sem("x_stats")
        x_sums = sem("x_sums")
        x_mean = sem("x_mean")
        x_diff2 = sem("x_diff2")
        x_v64 = sem("x_v64")
        x_var = sem("x_var")
        centered = sem("centered")
        relued = sem("relued")
        y_stats = sem("y_stats")
        y_sums = sem("y_sums")
        y_diff2 = sem("y_diff2")
        y_v64 = sem("y_v64")
        y_var = sem("y_var")
        sd_ready = sem("sd_ready")
        rs_ready = sem("rs_ready")
        zsrc_ready = sem("zsrc_ready")
        zdst_ready = sem("zdst_ready")
        z2_ready = [sem(f"z2_ready{c}") for c in range(NCH)]
        o_scaled = sem("o_scaled")
        o_biased = sem("o_biased")
        x_used = sem("x_used")
        src_T, dst_T = sem("src_T"), sem("dst_T")
        z_T = [sem(f"z_T{c}") for c in range(NCH)]
        agg_T = sem("agg_T")
        src_ev, dst_ev = sem("src_ev"), sem("dst_ev")
        z_ev = [sem(f"z_ev{c}") for c in range(NCH)]
        agg_ev = sem("agg_ev")
        q_mm, k_mm, v_mm = sem("q_mm"), sem("k_mm"), sem("v_mm")
        q_evac = sem("q_evac")
        qk_ready = sem("qk_ready")
        alpha_ready = sem("alpha_ready")
        mx_ready = sem("mx_ready")
        mx_diff = sem("mx_diff")
        ex_ready = sem("ex_ready")
        cw_ready = sem("cw_ready")
        den_prev_in = sem("den_prev_in")
        den_ready = sem("den_ready")
        den_eps = sem("den_eps")
        rden_ready = sem("rden_ready")
        wv_ready = sem("wv_ready")
        chain = sem("chain")
        aggn_ready = sem("aggn_ready")
        hid_mm = [sem(f"hid_mm{c}") for c in range(NCH)]
        gelu_done = [sem(f"gelu_done{c}") for c in range(NCH)]
        mlp_mm = [sem(f"mlp_mm{c}") for c in range(NCH)]
        out_ready = [sem(f"out_ready{c}") for c in range(NCH)]
        proj_mm = sem("proj_mm")
        o_proj = sem("o_proj")
        oe_ready = sem("oe_ready")
        oe_stats = sem("oe_stats")
        o_stats = sem("o_stats")
        o_sums = sem("o_sums")
        o_diff2 = sem("o_diff2")
        o_v64 = sem("o_v64")
        o_var = sem("o_var")
        stored = [sem(f"stored{i}") for i in range(NCH)]
        state_stored = [sem(f"state_stored{i}") for i in range(2)]
        rows_in = [sem(f"rows_in{i}") for i in range(2)]
        scattered = [sem(f"scattered{i}") for i in range(2)]
        ticked = sem("ticked")
        f_in = sem("f_in")
        f_link = sem("f_link")
        f_T = sem("f_T")
        f_exp_in = sem("f_exp_in")
        f_exp = sem("f_exp")
        f_coef = sem("f_coef")
        f_bc = sem("f_bc")
        f_agg = sem("f_agg")
        f_proj = sem("f_proj")
        f_var = sem("f_var")
        f_sd = sem("f_sd")
        f_z = sem("f_z")
        f_zT = sem("f_zT")
        f_zev = sem("f_zev")
        f_hid = sem("f_hid")
        f_gelu = sem("f_gelu")
        f_mlp = sem("f_mlp")
        f_row = sem("f_row")
        f_out = sem("f_out")

        def block_of(c, s):
            return s - 1 if c < NCH - 1 else s - 2

        def wide(ap, n):
            return ap.unsqueeze(2).broadcast_to([ap.shape[0], ap.shape[1], n])

        def rows(ap, n):
            return ap.unsqueeze(1).broadcast_to([ap.shape[0], n, ap.shape[1]])

        def tiles(ap):
            return ap.rearrange("p (t c) -> p t c", c=C)

        def flat(ap):
            return ap.rearrange("p a t -> p (a t)")

        ea_main = eattr[0:PF * EPP, :].rearrange("(p t) c -> p t c", t=EPP)
        ea_last = eattr[PF * EPP:E, :].rearrange("(p t) c -> p t c", p=1)
        PCUT = 96
        ECUT = 112

        block = ctx.enter_context(nc.Block())

        @block.sync
        def _(sp):
            def load_block(b, par, tail=False, full=True, first=False):
                if not first:
                    sp.wait_ge(x_used, b - 1)
                rows_ = LASTROWS if tail else ROWS
                xb = x[bass.ds(b * ROWS, rows_), :].rearrange("(p j) c -> p j c", j=NT)
                sp.dma_start(X[par][0:PCUT, 0:NT, :], xb[0:PCUT]).then_inc(dense_in[par], 16)
                sp.dma_start(X[par][PCUT:rows_ // NT, 0:NT, :], xb[PCUT:rows_ // NT])\
                  .then_inc(dense_in[par], 16)
                if not first:
                    sp.wait_ge(src_T, 2 * (b - 1))
                ea = aug_s[par][:, :, C:C + ED]
                sp.dma_start(ea[0:ECUT], ea_main[0:ECUT, bass.ds(b * ET, ET), :])\
                  .then_inc(eattr_in[par], 16)
                sp.dma_start(ea[ECUT:PF], ea_main[ECUT:PF, bass.ds(b * ET, ET), :])\
                  .then_inc(eattr_in[par], 16)
                sp.dma_start(ea[PF:P], ea_last[:, bass.ds(b * ET, ET) if full else slice(0, ET), :])\
                  .then_inc(eattr_in[par], 16)

            def store_nodes(b, tail=False):
                rows_ = LASTROWS if tail else ROWS
                ob = out[bass.ds(b * ROWS, rows_), :].rearrange("(p j) c -> p j c", j=NT)
                for c in range(NCH - 1):
                    sp.wait_ge(out_ready[c], b + 1)
                    t = slice(8 * c, 8 * c + 8)
                    if tail:
                        sp.dma_start(ob[0:PCUT, t], tiles(OUTS[0:PCUT, c, :]))\
                          .then_inc(stored[c], 16)
                        sp.dma_start(ob[PCUT:LASTP, t], tiles(OUTS[PCUT:LASTP, c, :]))\
                          .then_inc(stored[c], 16)
                    else:
                        sp.dma_start(ob[:, t], tiles(OUTS[:, c, :])).then_inc(stored[c], 16)

            def store_targets(b):
                sp.wait_ge(out_ready[NCH - 1], b + 1)
                sp.dma_start(edge_rows[:, bass.ds(b * ET, ET), :], tiles(OUTS[:, NCH - 1, :]))\
                  .then_inc(stored[NCH - 1], 16)

            def store_states(s, par):
                sp.wait_ge(chain, ET * (s + 1))
                sp.dma_start(states[:, bass.ds(s * ET, ET), :], rec[par][:, :, :])\
                  .then_inc(state_stored[par], 16)

            sp.wait_ge(pads_set, 1)
            sp.dma_start(dsti[0:PF, 1:EPP + 1], dst[0:PF * EPP].rearrange("(p t) -> p t", t=EPP))\
              .then_inc(tables_in, 16)
            sp.dma_start(dsti[PF:P, 1:EL + 1], dst[PF * EPP:E].rearrange("(p t) -> p t", p=1))\
              .then_inc(tables_in, 16)
            sp.dma_start(srci[0:PF, 0:EPP], src[0:PF * EPP].rearrange("(p t) -> p t", t=EPP))\
              .then_inc(tables_in, 16)
            sp.dma_start(srci[PF:P, 0:EL], src[PF * EPP:E].rearrange("(p t) -> p t", p=1))\
              .then_inc(tables_in, 16)
            dst_pt = dst[0:PF * EPP].rearrange("(p t) -> p t", t=EPP)
            with nc.allow_non_contiguous_dma(reason="one element per partition, once"):
                sp.dma_start(dsti[1:P, 0:1], dst_pt[:, EPP - 1:EPP]).then_inc(tables_in, 16)
                sp.dma_start(dsti[0:PF - 1, EPP + 1:EPP + 2], dst_pt[1:PF, 0:1])\
                  .then_inc(tables_in, 16)
                sp.dma_start(dsti[PF - 1:PF, EPP + 1:EPP + 2],
                             dst[PF * EPP:PF * EPP + 1].rearrange("(p t) -> p t", p=1))\
                  .then_inc(tables_in, 16)
            load_block(0, 0, first=True)
            with nc.allow_non_contiguous_dma(reason="bias columns, once"):
                for i, v in enumerate((g1, be1, g2, be2)):
                    sp.dma_start(gcol[:, i:i + 1], v.rearrange("(c a) -> c a", a=1))\
                      .then_inc(consts_in, 16)
                for h in range(2):
                    sp.dma_start(b1col[h * C:(h + 1) * C, :], b1.rearrange("(c a) -> c a", a=1))\
                      .then_inc(consts_in, 16)
            for i, (w, b) in enumerate(((Wq, bq), (Wk, bk), (Wv, bv))):
                sp.dma_start(wqkv[:, i, :], w).then_inc(consts_in, 16)
                sp.dma_start(bqkv[:, i, :], b.rearrange("(a c) -> a c", a=1)).then_inc(consts_in, 16)
            sp.dma_start(we[:, :], We).then_inc(consts_in, 16)
            sp.dma_start(wp[:, :], Wp).then_inc(consts_in, 16)
            sp.wait_ge(pads_set, 2)
            for h in range(2):
                sp.dma_start(w1[:, h, :], W1).then_inc(consts_in, 16)
                sp.dma_start(w2bd[h * C:(h + 1) * C, h * C:(h + 1) * C], W2).then_inc(consts_in, 16)
            sp.dma_start(bp_b[:, :], bp.rearrange("(a c) -> a c", a=1).broadcast_to([P, C]))\
              .then_inc(consts_in, 16)
            sp.dma_start(b2row[:, :, :], b2.rearrange("(a t c) -> a t c", a=1, t=1)
                         .broadcast_to([1, 8, C])).then_inc(consts_in, 16)
            load_block(1, 1, first=True)
            load_block(2, 0)
            store_states(0, 0)
            load_block(3, 1)
            store_nodes(0)
            store_states(1, 1)

            def step(s, par, load=True, **kw):
                if load:
                    load_block(s + 2, par, **kw)
                store_nodes(s - 1)
                store_targets(s - 2)
                store_states(s, par)

            SPLIT = (FULL_EA - 2) // 2
            with sp.Fori(1, SPLIT) as k:
                step(2 * k, 0)
                step(2 * k + 1, 1)
            for s in (2 * SPLIT, 2 * SPLIT + 1):
                step(s, s % 2, full=s + 2 < FULL_EA)
            with sp.Fori(SPLIT + 1, (B - 3) // 2) as k:
                step(2 * k, 0, full=False)
                step(2 * k + 1, 1, full=False)
            for s in range(B - 3, B):
                step(s, s % 2, load=s + 2 < B, full=False, tail=s + 2 == B - 1)
            store_nodes(B - 1, tail=True)
            store_targets(B - 2)
            store_targets(B - 1)

            sp.wait_ge(stored[NCH - 1], 16 * B)
            sp.wait_ge(x_used, B)

            def load_rows(b, par):
                sp.dma_start(X[par][:, 0:ET, :], edge_rows[:, bass.ds(b * ET, ET), :])\
                  .then_inc(rows_in[par], 16)
                sp.dma_start(idx[par][:, 0:ET], scati[:, bass.ds(b * ET, ET)])\
                  .then_inc(rows_in[par], 16)

            load_rows(0, 0)
            load_rows(1, 1)
            with sp.Fori(1, B // 2) as k:
                for par in range(2):
                    sp.wait_ge(scattered[par], 16 * ET * k)
                    load_rows(2 * k + par, par)
            sp.wait_ge(scattered[0], 16 * ET * (B // 2))
            load_rows(B - 1, 0)
            for c in range(NCH - 1):
                sp.wait_ge(stored[c], 16 * (B + 1))

        @block.gpsimd
        def _(pool):
            pool.memset(ident[:, :], 0.0).then_inc(built, 1)
            pool.memset(sel[:, :], 1.0).then_inc(built, 1)
            pool.wait_ge(built, 2)
            pool.affine_select(out=ident[:, :], in_=ident[:, :], compare_op=ALU.not_equal, fill=1.0,
                               base=0, pattern=[[-1, P]], channel_multiplier=1).then_inc(built, 1)
            pool.affine_select(out=sel[:, :], in_=sel[:, :], compare_op=ALU.is_ge, fill=0.0,
                               base=0, pattern=[[1, P]], channel_multiplier=-C).then_inc(built, 1)
            pool.wait_ge(built, 4)
            pool.affine_select(out=sel[:, :], in_=sel[:, :], compare_op=ALU.is_ge, fill=0.0,
                               base=C - 1, pattern=[[-1, P]], channel_multiplier=C).then_inc(built, 1)
            pool.iota(rowbase[:, :], [[0, 1]], base=-1, channel_multiplier=EPP,
                      allow_small_or_imprecise_dtypes=True).then_inc(built, 1)

            def tick(i, first=False):
                if not first:
                    pool.wait_ge(ticked, i)
                pool.tensor_tensor(ticks[:, 0:1], ticks[:, 1:2], ticks[:, 2:3], ALU.add)\
                    .then_inc(ticked, 1)

            pool.memset(ticks[:, :], 0.0).then_inc(built, 1)
            pool.wait_ge(built, 7)

            def gather_block(b, par, first=False):
                pool.wait_ge(idx_ready, b + 1)
                tick(b, first=first and b == 0)
                for t in range(2 * ET):
                    pool.indirect_dma_start(
                        X[par][:, S0 + t, :], None, x,
                        bass.IndirectOffsetOnAxis(ap=idx[par][:, t:t + 1], axis=0))\
                        .then_inc(gathered[par], 16)

            def residuals(b, par, first=False):
                pool.wait_ge(o_scaled, b + 1)
                pool.tensor_tensor(O[par][:, :, :], O[par][:, :, :], rows(bp_b[:, :], OT),
                                   ALU.add).then_inc(o_biased, 1)
                pool.wait_ge(o_biased, b + 1)
                if not first:
                    pool.wait_ge(mlp_mm[NCH - 2], b - 1)
                    pool.wait_ge(o_proj, b - 1)
                pool.tensor_tensor(XO[par][:, 0:NT, :], X[par][:, 0:NT, :], O[par][:, 0:NT, :],
                                   ALU.add)
                pool.tensor_tensor(XO[par][:, NT:OT, :], X[par][:, D0:XT, :], O[par][:, NT:OT, :],
                                   ALU.add).then_inc(x_used, 1)
                pool.wait_ge(x_used, b + 1)

            gather_block(0, 0, first=True)
            gather_block(1, 1, first=True)
            for b in range(2):
                residuals(b, b, first=True)
                gather_block(b + 2, b)
            with pool.Fori(1, B // 2 - 1) as k:
                for par in range(2):
                    residuals(2 * k + par, par)
                    gather_block(2 * k + par + 2, par)
            residuals(B - 3, 0)
            gather_block(B - 1, 0)
            residuals(B - 2, 1)
            residuals(B - 1, 0)

            pool.wait_ge(state_stored[0], 16 * (B // 2 + 1))
            pool.wait_ge(state_stored[1], 16 * (B // 2))
            pool.wait_ge(w_ready, 1)
            pool.indirect_dma_start(frec[:, :], None, states.rearrange("p t c -> (p t) c"),
                                    bass.IndirectOffsetOnAxis(ap=fixi[:, 0:1], axis=0))\
                .then_inc(f_in, 16)
            pool.indirect_dma_start(xf[:, :], None, x,
                                    bass.IndirectOffsetOnAxis(ap=dstg[:, 0:1], axis=0))\
                .then_inc(f_in, 16)

            for c in range(NCH - 1):
                pool.wait_ge(stored[c], 16 * (B + 1))

            last_row = pool.to_reg(N - 1)

            def scatter_block(par, n):
                pool.wait_ge(rows_in[par], 32 * n)
                tick(B + 2 * (n - 1) + par)
                for t in range(ET):
                    pool.indirect_dma_start(
                        out, bass.IndirectOffsetOnAxis(ap=idx[par][:, t:t + 1], axis=0),
                        X[par][:, t, :], None, bounds_check=last_row, oob_is_err=False)\
                        .then_inc(scattered[par], 16)

            with pool.Fori(1, B // 2 + 1) as n:
                scatter_block(0, n)
                scatter_block(1, n)
            scatter_block(0, B // 2 + 1)
            pool.wait_ge(f_row, 1)
            pool.indirect_dma_start(out, bass.IndirectOffsetOnAxis(ap=fixi[:, 1:2], axis=0),
                                    frow[:, 5, :], None, bounds_check=N - 1, oob_is_err=False)\
                .then_inc(f_out, 16)
            pool.wait_ge(scattered[0], 16 * ET * (B // 2 + 1))
            pool.wait_ge(scattered[1], 16 * ET * (B // 2))
            pool.wait_ge(f_out, 16)

        @block.tensor
        def _(pe):
            pe.wait_ge(consts_in, 16 * 20)
            pe.wait_ge(w_placed, 1)

            def fold(outp, m, i, n, edge):
                lc, lb, lo = pick[m]
                def r(t):
                    return flat(t[:, i:i + n, :])
                pe.matmul(outp, lc[:, :], r(gwqkv), start=True, stop=False)
                pe.matmul(outp, lb[:, :], r(wqkv), start=False, stop=False)
                if edge:
                    for a in range(n):
                        pe.matmul(outp[:, a * HC:(a + 1) * HC], place_edge[:, :], we[:, :],
                                  start=False, stop=False)
                pe.matmul(outp, lo[:, :], r(bqkv), start=False, stop=True)

            fold(q_ps[0:KD, 0:HC], KD, 0, 1, False)
            fold(k_ps[0:KS, 0:2 * HC], KS, 1, 2, True)
            pe.matmul(tp[0][:, 0:C], center2[:, :], gw1[:, :], start=True, stop=True)
            pe.matmul(hid_ps[:, 0:1], flat(w1[:, :, :]), gcol[:, 3:4], start=True, stop=True)\
              .then_inc(w_folded, 1)
            pe.wait_ge(w_ready, 1)

            def transposes(bank, m, srcs, done):
                for j, a in enumerate(srcs):
                    ins = pe.transpose(tp[bank][0:m, j * P:(j + 1) * P], a, ident[:, :])
                ins.then_inc(done, 1)

            def qkv(s, par, n, first=False):
                for h in range(2):
                    if h == 0:
                        pe.wait_ge(eattr_in[par], 48 * n)
                        pe.wait_ge(zsrc_ready, s + 1)
                        if not first:
                            pe.wait_ge(agg_ev, 2 * s)
                    else:
                        pe.wait_ge(src_ev, 2 * s + 1)
                    transposes(0, KS, [aug_s[par][:, 4 * h + j, :] for j in range(4)], src_T)
                    if h == 0:
                        pe.wait_ge(zdst_ready, s + 1)
                    else:
                        pe.wait_ge(dst_ev, 2 * s + 1)
                    transposes(1, KD, [aug_d[:, 4 * h + j, :] for j in range(4)], dst_T)
                    pe.wait_ge(src_ev, 2 * s + h + 1)
                    if not first:
                        pe.wait_ge(wv_ready, 2 * (s - 1) + h + 1)
                    for j in range(4):
                        ins = pe.matmul(v_ps[h][:, j * P:(j + 1) * P],
                                        srcT[:, h, j * P:(j + 1) * P],
                                        wkv_s[:, 1, :], start=True, stop=True)
                    ins.then_inc(v_mm, 1)
                    pe.wait_ge(dst_ev, 2 * s + h + 1)
                    if h or not first:
                        pe.wait_ge(q_evac, 2 * s + h)
                    for j in range(4):
                        ins = pe.matmul(q_ps[:, j * P:(j + 1) * P], dstT[:, h, j * P:(j + 1) * P],
                                        wq_s[:, :], start=True, stop=True)
                    ins.then_inc(q_mm, 1)
                    if h or not first:
                        pe.wait_ge(qk_ready, 2 * s + h)
                    for j in range(4):
                        ins = pe.matmul(k_ps[:, j * P:(j + 1) * P], srcT[:, h, j * P:(j + 1) * P],
                                        wkv_s[:, 0, :], start=True, stop=True)
                    ins.then_inc(k_mm, 1)

            def mlp(s, par, chunks, qkv_done=True):
                def turn(c):
                    n = block_of(c, s) + 1
                    if c == 2 and 0 in chunks:
                        pe.wait_ge(z_ev[0], s)
                    elif qkv_done:
                        pe.wait_ge((src_ev, dst_ev)[c], 2 * s + 2)
                    else:
                        pe.wait_ge(agg_ev, 2 * B)
                        pe.wait_ge(z_ev[NCH - 1], s - 2)
                    pe.wait_ge(z2_ready[c], n)
                    transposes(c % 2, P, [z2[:, c, j * P:(j + 1) * P] for j in range(4)], z_T[c])

                def up(c):
                    pe.wait_ge(z_ev[c], block_of(c, s) + 1)
                    pe.matmul(hid_ps[:, :], w1bd[:, :], z2T[:, c, :], start=True, stop=True)\
                      .then_inc(hid_mm[c], 1)

                def down(c):
                    n = block_of(c, s) + 1
                    if c == chunks[0]:
                        pe.wait_ge(o_proj, min(s, B) if isinstance(s, int) else s)
                        if c:
                            pe.wait_ge(out_ready[c], n - 1)
                    else:
                        pe.wait_ge(out_ready[c - 1], block_of(c - 1, s) + 1)
                    pe.matmul(res_ps[:, :], ones_row[:, :], flat(b2row[:, :, :]),
                              start=True, stop=False)
                    xo = XO[1 - par][:, 8 * c:8 * c + 8, :] if c < NCH - 1 else XE[par][:, :, :]
                    pe.matmul(res_ps[:, :], ident[:, :], flat(xo), start=False, stop=False)
                    pe.wait_ge(gelu_done[c], n)
                    for j in range(4):
                        ins = pe.matmul(res_ps[:, j * P:(j + 1) * P], hid[:, c, j * P:(j + 1) * P],
                                        w2bd[:, :], start=False, stop=j == 3)
                    ins.then_inc(mlp_mm[c], 1)

                turn(chunks[0])
                for i, c in enumerate(chunks):
                    up(c)
                    if i + 1 < len(chunks):
                        turn(chunks[i + 1])
                    down(c)

            def project(s, mlp_chunks):
                pe.wait_ge(aggn_ready, s + 1)
                for h, bank in enumerate((1, 0)):
                    if mlp_chunks:
                        c = 1 if h == 0 else 2 if mlp_chunks > 2 else 0
                        pe.wait_ge(z_ev[c], block_of(c, s) + 1)
                    transposes(bank, P, [aggn[:, 4 * h + j, :] for j in range(4)], agg_T)
                if mlp_chunks:
                    c = mlp_chunks - 1
                    pe.wait_ge(out_ready[c], block_of(c, s) + 1)
                for h in range(2):
                    pe.wait_ge(agg_ev, 2 * s + h + 1)
                    for j in range(4):
                        ins = pe.matmul(res_ps[:, (4 * h + j) * C:(4 * h + j + 1) * C],
                                        aggT[:, h, j * P:(j + 1) * P], wp[:, :],
                                        start=True, stop=True)
                ins.then_inc(proj_mm, 1)

            qkv(0, 0, 1, first=True)
            project(0, 0)
            qkv(1, 1, 1)
            mlp(1, 1, (0, 1))
            project(1, 2)
            with pe.Fori(1, B // 2) as k:
                for par in range(2):
                    qkv(2 * k + par, par, k + 1)
                    mlp(2 * k + par, par, (0, 1, 2))
                    project(2 * k + par, 3)
            qkv(B - 1, 0, B // 2 + 1)
            mlp(B - 1, 0, (0, 1, 2))
            project(B - 1, 3)
            mlp(B, 1, (0, 1, 2), qkv_done=False)
            mlp(B + 1, 0, (2,), qkv_done=False)

            last = rec[(B - 1) % 2]
            pe.wait_ge(f_in, 32)
            pe.transpose(k_ps[:, 0:P], frec[:, 0:HC], ident[:, :])
            pe.transpose(k_ps[:, P:2 * P], last[:, ET - 1, 0:HC], ident[:, :])
            for i, a in enumerate((frec[:, HC:HC + H], frec[:, HC + H:SW],
                                   last[:, ET - 1, HC:HC + H], last[:, ET - 1, HC + H:SW])):
                pe.transpose(q_ps[0:H, i * P:(i + 1) * P], a, ident[:, :])
            for i in range(2):
                ins = pe.transpose(k_ps[0:H, (2 + i) * P:(3 + i) * P], fflag[:, i, :], ident[:, :])
            ins.then_inc(f_T, 1)
            pe.wait_ge(f_coef, 1)
            pe.matmul(v_ps[0][:, :], sel[:, :], flat(fk[:, 0:4, :]), start=True, stop=True)\
              .then_inc(f_bc, 1)
            pe.wait_ge(f_agg, 1)
            pe.matmul(v_ps[1][:, 0:C], fa[:, 2, :], wp[:, :], start=True, stop=True)\
              .then_inc(f_proj, 1)
            pe.wait_ge(f_z, 1)
            pe.transpose(v_ps[0][0:C, 0:P], frow[:, 3, :], ident[:, :]).then_inc(f_zT, 1)
            pe.wait_ge(f_zev, 1)
            pe.matmul(v_ps[1][0:C, P:2 * P], w1bd[0:C, 0:C], fzT[:, 0, :], start=True, stop=True)\
              .then_inc(f_hid, 1)
            pe.wait_ge(f_gelu, 1)
            pe.matmul(q_ps[:, 0:C], ones_row[:, :], b2row[:, 0, :], start=True, stop=False)
            pe.matmul(q_ps[:, 0:C], fzT[:, 1, :], w2bd[0:C, 0:C], start=False, stop=True)\
              .then_inc(f_mlp, 1)

        @block.scalar
        def _(act):
            def evacuate_qkv(s):
                for h in range(2):
                    act.wait_ge(src_T, 2 * s + h + 1)
                    act.activation(srcT[:, h, :], tp[0][0:KS, :], ACT.Copy).then_inc(src_ev, 1)
                    act.wait_ge(dst_T, 2 * s + h + 1)
                    act.activation(dstT[:, h, :], tp[1][0:KD, :], ACT.Copy).then_inc(dst_ev, 1)
                    act.wait_ge(q_mm, 2 * s + h + 1)
                    act.activation(q_sb[:, h, :], q_ps[:, :], ACT.Copy).then_inc(q_evac, 1)

            def exps(s):
                act.wait_ge(ex_ready, s + 1)
                act.activation(cw[:, :, :, 1:ET + 1].rearrange("p a h t -> p (a h) t"),
                               ex[:, :, :, :].rearrange("p a h t -> p (a h) t"), ACT.Exp)\
                   .then_inc(cw_ready, 1)

            def relus(b, i):
                a, z = ((S0, XT), (0, NT))[i]
                act.wait_ge(centered, 2 * b + i + 1)
                act.activation(Y[:, a:z, :], Y[:, a:z, :], ACT.Relu).then_inc(relued, 1)

            def turned(s, c):
                act.wait_ge(z_T[c], block_of(c, s) + 1)
                act.activation(z2T[:, c, :], tp[c % 2][:, :], ACT.Copy).then_inc(z_ev[c], 1)

            def mlp(s, chunks, early=(), norms=False):
                for i, c in enumerate(chunks):
                    n = block_of(c, s) + 1
                    act.wait_ge(hid_mm[c], n)
                    act.activation(hid[:, c, :], hid_ps[:, :], ACT.Gelu, bias=b1g[:, 0:1])\
                       .then_inc(gelu_done[c], 1)
                    if i + 1 < len(chunks):
                        turned(s, chunks[i + 1])
                    if i == 0 and norms:
                        relus(s + 1, 1)
                    act.wait_ge(mlp_mm[c], n)
                    if c not in early:
                        act.wait_ge(stored[c], 16 * (n - 1))
                    act.activation(OUTS[:, c, :], res_ps[:, :], ACT.Copy).then_inc(out_ready[c], 1)

            def roots(s, norms=True, nodes=True, targets=True):
                if norms:
                    act.wait_ge(y_var, s + 2)
                if nodes:
                    act.wait_ge(o_var, s + 1)
                act.activation(sd[:, :], vars_[:, :], ACT.Sqrt).then_inc(sd_ready, 1)

            def project(s):
                for h in range(2):
                    act.wait_ge(agg_T, 2 * s + h + 1)
                    act.activation(aggT[:, h, :], tp[1 - h][:, :], ACT.Copy).then_inc(agg_ev, 1)

            def step(s, chunks=(0, 1, 2), early=(), norms=True):
                evacuate_qkv(s)
                if chunks:
                    turned(s, chunks[0])
                if norms:
                    relus(s + 1, 0)
                exps(s)
                if chunks:
                    mlp(s, chunks, early, norms)
                elif norms:
                    relus(s + 1, 1)
                roots(s, norms)
                project(s)

            relus(0, 0)
            relus(0, 1)
            roots(-1, nodes=False)
            step(0, ())
            step(1, (0, 1), early=(0, 1))
            step(2, early=(2,))
            step(3)
            with act.Fori(2, B // 2) as k:
                step(2 * k)
                step(2 * k + 1)
            step(B - 1, norms=False)
            turned(B, 0)
            mlp(B, (0, 1, 2))
            roots(B, norms=False)
            turned(B + 1, 2)
            mlp(B + 1, (2,))
            act.wait_ge(f_exp_in, 1)
            act.activation(fcw[:, :, :], fex[:, :, :], ACT.Exp).then_inc(f_exp, 1)
            for i in range(2):
                act.wait_ge(f_var, i + 1)
                act.activation(fsc[:, 5 + 6 * i:6 + 6 * i], fsc[:, 4 + 6 * i:5 + 6 * i], ACT.Sqrt)\
                   .then_inc(f_sd, 1)
            act.wait_ge(f_zT, 1)
            act.activation(fzT[:, 0, :], v_ps[0][0:C, 0:P], ACT.Copy).then_inc(f_zev, 1)
            act.wait_ge(f_hid, 1)
            act.activation(fzT[:, 1, :], v_ps[1][0:C, P:2 * P], ACT.Gelu, bias=b1g[0:C, 0:1])\
               .then_inc(f_gelu, 1)

        @block.vector
        def _(dve):
            linked = [0]

            def link(ins):
                linked[0] += 1
                ins.then_inc(link_done, 1)
                dve.wait_ge(link_done, linked[0])

            dve.memset(dsti[:, :], N)
            dve.memset(dstg[:, :], 0)
            dve.memset(srci[:, :], 0).then_inc(pads_set, 1)
            for t in [w2bd[:, :], w1bd[:, :], place_edge[:, :], cw[:, :, :, :], den[1][:, :, :],
                      rec[1][:, :, :], dj[:, :], aj[:, :],
                      *(u[:, :] for m in (KS, KD) for u in pick[m])]:
                dve.memset(t, 0.0)
            dve.memset(ost[:, :, :], 0.0)
            dve.memset(vars_[:, :], 1.0)
            dve.memset(mx[1][:, :, :], NEG)
            dve.memset(mj[:, :], NEG)
            dve.memset(ones_row[:, :], 1.0)
            for i in range(2):
                dve.memset(aug_s[i][:, :, C + ED:KS], 1.0)
            dve.memset(keepm[:, :, :, 0:1], NEG)
            dve.memset(aug_d[:, :, C:KD], 1.0).then_inc(pads_set, 1)
            dve.wait_ge(pads_set, 2)

            dve.wait_ge(tables_in, 7 * 16)
            link(dve.tensor_copy(dstf[:, :], dsti[:, :]))
            link(dve.tensor_scalar(dstg[:, 0:EPP], dstf[:, 1:EPP + 1], float(N - 1), None, ALU.min))
            for b in range(2):
                dve.tensor_copy(idx[b][:, 0:ET], srci[:, b * ET:(b + 1) * ET])
                dve.tensor_copy(idx[b][:, ET:2 * ET], dstg[:, b * ET:(b + 1) * ET])\
                   .then_inc(idx_ready, 1)
            link(dve.tensor_tensor(same[:, :], dstf[:, 0:EPP + 1], dstf[:, 1:EPP + 2], ALU.is_equal))
            for h in range(H):
                ins = dve.tensor_scalar(keepm[:, :, h, 1:ET + 1],
                                        same[:, 0:EPP].rearrange("p (b t) -> p b t", t=ET),
                                        1.0, -NEG, ALU.subtract, ALU.mult)
            link(ins)
            dve.memset(keepm[:, 0, :, 1:2], NEG)
            link(dve.tensor_scalar(firstseg[:, :], dstf[:, 1:EPP + 1], dstf[:, 1:2], None,
                                   ALU.is_equal))
            link(dve.tensor_scalar(nofinal[:, :], firstseg[:, :], same[:, 0:1], None, ALU.mult))
            link(dve.tensor_tensor(nofinal[:, :], nofinal[:, :], same[:, 1:EPP + 1], ALU.max))
            link(dve.scalar_tensor_tensor(scati[:, :], nofinal[:, :], FAR, dstf[:, 1:EPP + 1],
                                          ALU.mult, ALU.add))
            link(dve.tensor_reduce(fix[:, 0:1], firstseg[:, :], AX.X, ALU.add))
            dve.wait_ge(built, 6)
            filled = firstseg[:, EPP - 1:EPP]
            dve.tensor_tensor(fixi[:, 0:1], fix[:, 0:1], rowbase[:, :], ALU.add)
            dve.tensor_tensor(fix[:, 1:2], filled, same[:, 0:1], ALU.mult)
            link(dve.tensor_tensor(fix[:, 2:3], filled, same[:, EPP:EPP + 1], ALU.mult))
            link(dve.tensor_scalar(fix[:, 3:4], fix[:, 2:3], -1.0, 1.0, ALU.mult, ALU.add))
            link(dve.tensor_tensor(fix[:, 3:4], fix[:, 3:4], same[:, 0:1], ALU.mult))
            link(dve.tensor_scalar(fix[:, 4:5], fix[:, 3:4], -FAR, FAR, ALU.mult, ALU.add))
            dve.tensor_tensor(fixi[:, 1:2], fix[:, 4:5], dstf[:, 1:2], ALU.add)
            for h in range(H):
                dve.tensor_copy(fflag[:, 0, h:h + 1], fix[:, 1:2])
                dve.tensor_copy(fflag[:, 1, h:h + 1], same[:, 0:1])

            dve.wait_ge(consts_in, 16 * 20)
            link(dve.tensor_scalar(center[:, :], ident[0:C, 0:C], -1.0 / C, None, ALU.add))
            for m in (KS, KD):
                dve.tensor_copy(pick[m][0][:, 0:C], center[:, :])
                dve.tensor_copy(pick[m][1][:, m - 1:m], gcol[:, 1:2])
                dve.memset(pick[m][2][:, m - 1:m], 1.0)
            for h in range(2):
                dve.tensor_copy(center2[:, h * C:(h + 1) * C], center[:, :])
            dve.tensor_copy(place_edge[:, C:C + ED], ident[0:ED, 0:ED])
            dve.tensor_scalar(gwqkv[:, :, :], wqkv[:, :, :], gcol[:, 0:1], None, ALU.mult)
            dve.tensor_scalar(gw1[:, :], w1[:, 0, :], gcol[:, 2:3], None, ALU.mult)\
               .then_inc(w_placed, 1)
            dve.wait_ge(w_folded, 1)
            dve.tensor_scalar(wq_s[:, :], q_ps[0:KD, 0:HC], float(C) ** -0.5, None, ALU.mult)
            dve.tensor_copy(flat(wkv_s[:, :, :]), k_ps[0:KS, 0:2 * HC])
            for h in range(2):
                a, z = h * C, (h + 1) * C
                dve.tensor_copy(w1bd[a:z, a:z], tp[0][a:z, 0:C])
            dve.tensor_tensor(b1g[:, :], b1col[:, :], hid_ps[:, 0:1], ALU.add).then_inc(w_ready, 1)

            def variances(st, w, sums, diff2, n, mean_to=None, mean_done=None):
                dve.tensor_tensor(w[:, 1, :], st[:, :, 1], st[:, :, 4], ALU.subtract)
                if mean_to is not None:
                    dve.tensor_tensor(w[:, 0, :], st[:, :, 1], st[:, :, 4], ALU.add)
                dve.tensor_tensor(w[:, 2, :], st[:, :, 2], st[:, :, 5], ALU.add).then_inc(sums, 1)
                dve.wait_ge(sums, n)
                if mean_to is not None:
                    dve.tensor_scalar(mean_to, w[:, 0, :], 0.5, None, ALU.mult)\
                       .then_inc(mean_done, 1)
                dve.tensor_tensor(w[:, 1, :], w[:, 1, :], w[:, 1, :], ALU.mult).then_inc(diff2, 1)
                dve.wait_ge(diff2, n)
                return dve.scalar_tensor_tensor(w[:, 3, :], w[:, 1, :], float(C // 4), w[:, 2, :],
                                                ALU.mult, ALU.add)

            def inverse_roots(s):
                dve.wait_ge(sd_ready, s + 2)
                dve.reciprocal(rs[:, :], sd[:, :]).then_inc(rs_ready, 1)
                dve.wait_ge(rs_ready, s + 2)

            def x_statistics(b, par, a, z):
                for t in range(a, z):
                    ins = dve.bn_stats(xst[:, t, :], X[par][:, t, :])
                if z == XT:
                    ins.then_inc(x_stats, 1)

            def refill_indices(b, par):
                dve.tensor_copy(idx[par][:, 0:ET], srci[:, bass.ds((b + 2) * ET, ET)])
                dve.tensor_copy(idx[par][:, ET:2 * ET], dstg[:, bass.ds((b + 2) * ET, ET)])\
                   .then_inc(idx_ready, 1)

            def x_variances(b):
                variances(xst, sm, x_sums, x_diff2, b + 1, mean[:, :], x_mean).then_inc(x_v64, 1)

            def center_rows(b, par, i):
                a, z = ((S0, XT), (0, NT))[i]
                if i == 0:
                    dve.wait_ge(x_mean, b + 1)
                dve.tensor_tensor(Y[:, a:z, :], X[par][:, a:z, :], wide(mean[:, a:z], C),
                                  ALU.subtract).then_inc(centered, 1)

            def x_eps(b):
                dve.wait_ge(x_v64, b + 1)
                dve.tensor_scalar(vars_[:, 0:XT], sm[:, 3, :], 1.0 / C, EPS, ALU.mult, ALU.add)\
                   .then_inc(x_var, 1)

            def y_statistics(b, ts):
                for t in ts:
                    ins = dve.bn_stats(yst[:, t, :], Y[:, S0 + t, :])
                if ts[-1] == 2 * ET - 1:
                    ins.then_inc(y_stats, 1)

            def y_variances(b):
                dve.wait_ge(x_var, b + 1)
                dve.tensor_scalar(sm2[:, 0, :], vars_[:, S0:XT], EPS, None, ALU.mult)
                dve.wait_ge(y_stats, b + 1)
                variances(yst, sm2, y_sums, y_diff2, b + 1).then_inc(y_v64, 1)
                dve.wait_ge(y_v64, b + 1)
                dve.scalar_tensor_tensor(vars_[:, XT:OV], sm2[:, 3, :], 1.0 / C, sm2[:, 0, :],
                                         ALU.mult, ALU.add).then_inc(y_var, 1)

            def scale_rows(b, par):
                dve.tensor_tensor(aug_s[par][:, :, 0:C], Y[:, S0:D0, :],
                                  wide(rs[:, XT:XT + ET], C), ALU.mult).then_inc(zsrc_ready, 1)
                dve.tensor_tensor(aug_d[:, :, 0:C], Y[:, D0:XT, :],
                                  wide(rs[:, XT + ET:OV], C), ALU.mult).then_inc(zdst_ready, 1)

            def residual_rows(b, par, first=False):
                dve.wait_ge(relued, 2 * b + 2)
                dve.tensor_tensor(O[par][:, 0:NT, :], Y[:, 0:NT, :], wide(rs[:, 0:NT], C),
                                  ALU.mult)
                if not first:
                    dve.wait_ge(z2_ready[NCH - 1], b - 1)
                dve.tensor_tensor(O[par][:, NT:OT, :], Y[:, D0:XT, :], wide(rs[:, D0:XT], C),
                                  ALU.mult).then_inc(o_scaled, 1)

            def o_statistics(s, par):
                dve.wait_ge(o_biased, s + 1)
                for t in range(NT):
                    ins = dve.bn_stats(ost[:, t, :], O[par][:, t, :])
                ins.then_inc(o_stats, 1)

            def o_variances(s):
                dve.wait_ge(o_stats, s + 1)
                variances(ost, sm3, o_sums, o_diff2, s + 1).then_inc(o_v64, 1)
                dve.wait_ge(o_v64, s + 1)
                dve.tensor_scalar(vars_[:, OV:VN], sm3[:, 3, :], 1.0 / C, EPS, ALU.mult, ALU.add)\
                   .then_inc(o_var, 1)

            def z_second(s, par, chunks):
                for c in chunks:
                    Oc = O[par] if c < NCH - 1 else O[1 - par]
                    dve.tensor_tensor(tiles(z2[:, c, :]), Oc[:, 8 * c:8 * c + 8, :],
                                      wide(rs[:, OV + 8 * c:OV + 8 * c + 8], C), ALU.mult)\
                       .then_inc(z2_ready[c], 1)

            def products(s, h):
                dve.wait_ge(q_evac, 2 * s + h + 1)
                dve.wait_ge(k_mm, 2 * s + h + 1)
                dve.tensor_tensor(qk[:, 4 * h:4 * h + 4, :].rearrange("p t c -> p (t c)"),
                                  k_ps[:, :], q_sb[:, h, :], ALU.mult).then_inc(qk_ready, 1)

            def scores(s, par):
                dve.tensor_copy(alpha[:, :, 0:1], mx[1 - par][:, :, ET:ET + 1])
                dve.wait_ge(qk_ready, 2 * s + 2)
                dve.tensor_reduce(alpha[:, :, 1:ET + 1].rearrange("p h t -> p t h"),
                                  qk[:, :, :].rearrange("p t (h c) -> p t h c", h=H),
                                  AX.X, ALU.add).then_inc(alpha_ready, 1)

            def maxima(s, par):
                dve.wait_ge(alpha_ready, s + 1)
                dve.tensor_tensor_scan(flat(mx[par][:, :, :]),
                                       keepm[:, bass.ds(s, 1), :, :]
                                       .rearrange("p b h t -> p (b h t)"),
                                       flat(alpha[:, :, :]), NEG, ALU.add, ALU.max)\
                   .then_inc(mx_ready, 1)

            def exponents(s, par):
                m = mx[par]
                dve.wait_ge(mx_ready, s + 1)
                dve.tensor_tensor(ex[:, 0, :, :], m[:, :, 0:ET], m[:, :, 1:ET + 1],
                                  ALU.subtract).then_inc(mx_diff, 1)
                dve.tensor_tensor(ex[:, 1, :, :], alpha[:, :, 1:ET + 1], m[:, :, 1:ET + 1],
                                  ALU.subtract)
                dve.wait_ge(mx_diff, s + 1)
                dve.tensor_tensor(ex[:, 0, :, :], ex[:, 0, :, :],
                                  keepm[:, bass.ds(s, 1), :, 1:ET + 1]
                                  .rearrange("p b h t -> p (b h) t"), ALU.add)\
                   .then_inc(ex_ready, 1)

            def weighted_values(s, par, stores):
                R = rec[par]
                dve.wait_ge(cw_ready, s + 1)
                dve.tensor_copy(cw[:, 1, :, 0:1], den[1 - par][:, :, ET:ET + 1])\
                   .then_inc(den_prev_in, 1)
                if stores is not None:
                    dve.wait_ge(state_stored[par], 16 * stores)
                for h in range(2):
                    dve.wait_ge(v_mm, 2 * s + h + 1)
                    for g in range(H):
                        ins = dve.tensor_tensor(
                            R[:, 4 * h:4 * h + 4, g * C:(g + 1) * C],
                            v_ps[h][:, :].rearrange("p (t c) -> p t c", c=HC)
                            [:, :, g * C:(g + 1) * C],
                            wide(cw[:, 1, g, 1 + 4 * h:5 + 4 * h], C), ALU.mult)
                    ins.then_inc(wv_ready, 1)
                    if h == 0:
                        dve.wait_ge(den_prev_in, s + 1)
                        dve.tensor_tensor_scan(flat(den[par][:, :, :]), flat(cw[:, 0, :, :]),
                                               flat(cw[:, 1, :, :]), 0.0, ALU.mult, ALU.add)\
                           .then_inc(den_ready, 1)

            def sums(s, par, between):
                R = rec[par]
                dve.wait_ge(den_ready, s + 1)
                dve.tensor_scalar(rden[:, 0, :, :], den[par][:, :, 1:ET + 1], 1e-8,
                                  None, ALU.add).then_inc(den_eps, 1)
                dve.tensor_copy(R[:, :, HC:HC + H].rearrange("p t h -> p h t"),
                                mx[par][:, :, 1:ET + 1])
                dve.tensor_copy(R[:, :, HC + H:SW].rearrange("p t h -> p h t"),
                                den[par][:, :, 1:ET + 1])
                dve.wait_ge(den_eps, s + 1)
                dve.reciprocal(rden[:, 1, :, :], rden[:, 0, :, :]).then_inc(rden_ready, 1)
                dve.wait_ge(wv_ready, 2 * s + 2)
                for t in range(ET):
                    prev = rec[1 - par][:, ET - 1, :] if t == 0 else R[:, t - 1, :]
                    if t > 0:
                        dve.wait_ge(chain, ET * s + t)
                    for h in range(H):
                        a, z = h * C, (h + 1) * C
                        ins = dve.scalar_tensor_tensor(R[:, t, a:z], prev[:, a:z],
                                                       cw[:, 0, h, t + 1:t + 2], R[:, t, a:z],
                                                       ALU.mult, ALU.add)
                    ins.then_inc(chain, 1)
                    between(t)

            def averages(s, par):
                dve.wait_ge(chain, ET * (s + 1))
                dve.wait_ge(rden_ready, s + 1)
                for g in range(H):
                    a, z = g * C, (g + 1) * C
                    ins = dve.tensor_tensor(aggn[:, :, a:z], rec[par][:, :, a:z],
                                            wide(rden[:, 1, g, :], C), ALU.mult)
                ins.then_inc(aggn_ready, 1)

            def add_projection(s, par, first):
                Oe = O[par][:, NT:OT, :]
                dve.wait_ge(x_used, s + 1)
                if not first:
                    dve.wait_ge(mlp_mm[NCH - 1], s - 1)
                dve.wait_ge(proj_mm, s + 1)
                dve.tensor_tensor(Oe, tiles(res_ps[:, :]), Oe, ALU.add).then_inc(oe_ready, 1)
                dve.tensor_tensor(XE[par][:, :, :], tiles(res_ps[:, :]), XO[par][:, NT:OT, :],
                                  ALU.add).then_inc(o_proj, 1)
                dve.wait_ge(oe_ready, s + 1)
                for t in range(NT, OT):
                    ins = dve.bn_stats(ost[:, t, :], O[par][:, t, :])
                ins.then_inc(oe_stats, 1)

            def step(s, par, n=None, stores=None, first=False, targets=True, norms=True,
                     refill=True):
                b = s + 1
                if norms:
                    dve.wait_ge(dense_in[1 - par], 32 * n)
                    dve.wait_ge(gathered[1 - par], 32 * ET * n)
                    x_statistics(b, 1 - par, 0, XT // 2)
                products(s, 0)
                if norms:
                    x_statistics(b, 1 - par, XT // 2, XT)
                    if refill:
                        refill_indices(b, 1 - par)
                    dve.wait_ge(x_stats, b + 1)
                    x_variances(b)
                products(s, 1)
                if norms:
                    center_rows(b, 1 - par, 0)
                scores(s, par)
                if norms:
                    x_eps(b)
                maxima(s, par)
                if norms:
                    center_rows(b, 1 - par, 1)
                exponents(s, par)
                o_statistics(s, par)
                if not first:
                    dve.wait_ge(oe_stats, s)
                o_variances(s)
                weighted_values(s, par, stores)
                if norms:
                    dve.wait_ge(relued, 2 * b + 1)
                sums(s, par, (lambda t: y_statistics(b, (2 * t, 2 * t + 1))) if norms
                     else lambda t: None)
                if norms:
                    y_variances(b)
                averages(s, par)
                inverse_roots(s)
                if norms:
                    scale_rows(b, 1 - par)
                z_second(s, par, (2, 0, 1) if targets else (0, 1))
                if norms:
                    residual_rows(b, 1 - par, first)
                add_projection(s, par, first or not targets or (isinstance(s, int) and s < 2))

            dve.wait_ge(dense_in[0], 32)
            dve.wait_ge(gathered[0], 32 * ET)
            x_statistics(0, 0, 0, XT)
            refill_indices(0, 0)
            dve.wait_ge(x_stats, 1)
            x_variances(0)
            center_rows(0, 0, 0)
            center_rows(0, 0, 1)
            x_eps(0)
            dve.wait_ge(relued, 1)
            y_statistics(0, range(2 * ET))
            y_variances(0)
            inverse_roots(-1)
            scale_rows(0, 0)
            residual_rows(0, 0, first=True)
            step(0, 0, 1, first=True, targets=False)
            step(1, 1, 2)
            with dve.Fori(1, B // 2) as k:
                step(2 * k, 0, k + 1, stores=k)
                step(2 * k + 1, 1, k + 2, stores=k)
            step(B - 1, 0, stores=B // 2, norms=False)
            dve.wait_ge(oe_stats, B)
            dve.memset(ost[:, 0:NT, :], 0.0).then_inc(o_stats, 1)
            o_variances(B)
            inverse_roots(B)
            z_second(B, 1, (NCH - 1,))

            steps = [0]

            def flink(ins, to=None):
                if to is None:
                    steps[0] += 1
                    ins.then_inc(f_link, 1)
                    dve.wait_ge(f_link, steps[0])
                else:
                    ins.then_inc(to, 1)

            dve.wait_ge(f_T, 1)
            dve.tensor_copy(flat(fT[:, :, :]), k_ps[:, 0:2 * P])
            dve.tensor_copy(flat(fsm[:, 0:4, :]), q_ps[0:H, :])
            flink(dve.tensor_scalar(flat(fkeep[:, :, :]), k_ps[0:H, 2 * P:4 * P], 1.0, -NEG,
                                    ALU.subtract, ALU.mult))
            mF, dF, mL, dL = (fsm[:, i, :] for i in range(4))
            flink(dve.tensor_tensor_scan(mj[:, 1:P + 1], fkeep[:, 0, :], mL, NEG, ALU.add, ALU.max))
            dve.tensor_tensor(fk[:, 4, :], mj[:, 0:P], fkeep[:, 1, :], ALU.add)
            dve.tensor_tensor(fk[:, 5, :], mj[:, 0:P], mj[:, 1:P + 1], ALU.subtract)
            flink(dve.tensor_tensor(fex[:, 1, :], mL, mj[:, 1:P + 1], ALU.subtract))
            flink(dve.tensor_tensor(fk[:, 6, :], fk[:, 4, :], mF, ALU.max))
            dve.tensor_tensor(fex[:, 0, :], fk[:, 5, :], fkeep[:, 0, :], ALU.add)
            dve.tensor_tensor(fex[:, 2, :], mF, fk[:, 6, :], ALU.subtract)
            flink(dve.tensor_tensor(fex[:, 3, :], fk[:, 4, :], fk[:, 6, :], ALU.subtract), f_exp_in)
            dve.wait_ge(f_exp, 1)
            flink(dve.tensor_tensor(fk[:, 4, :], fcw[:, 1, :], dL, ALU.mult))
            flink(dve.tensor_tensor_scan(dj[:, 1:P + 1], fcw[:, 0, :], fk[:, 4, :], 0.0,
                                         ALU.mult, ALU.add))
            dve.tensor_tensor(fk[:, 5, :], dF, fcw[:, 2, :], ALU.mult)
            flink(dve.tensor_tensor(fk[:, 6, :], dj[:, 0:P], fcw[:, 3, :], ALU.mult))
            flink(dve.tensor_tensor(fk[:, 5, :], fk[:, 5, :], fk[:, 6, :], ALU.add))
            flink(dve.tensor_scalar(fk[:, 6, :], fk[:, 5, :], 1e-8, None, ALU.add))
            flink(dve.reciprocal(fk[:, 7, :], fk[:, 6, :]))
            dve.tensor_copy(flat(fk[:, 0:2, :]), flat(fcw[:, 0:2, :]))
            dve.tensor_tensor(fk[:, 2, :], fcw[:, 2, :], fk[:, 7, :], ALU.mult)
            flink(dve.tensor_tensor(fk[:, 3, :], fcw[:, 3, :], fk[:, 7, :], ALU.mult), f_coef)
            dve.wait_ge(f_bc, 1)
            flink(dve.tensor_copy(flat(bc[:, :, :]), v_ps[0][:, :]))
            dve.tensor_tensor(fa[:, 1, :], fT[:, 0, :], bc[:, 2, :], ALU.mult)
            flink(dve.tensor_tensor(fa[:, 0, :], fT[:, 1, :], bc[:, 1, :], ALU.mult))
            flink(dve.tensor_tensor_scan(aj[:, 1:P + 1], bc[:, 0, :], fa[:, 0, :], 0.0,
                                         ALU.mult, ALU.add))
            flink(dve.tensor_tensor(fa[:, 0, :], aj[:, 0:P], bc[:, 3, :], ALU.mult))
            flink(dve.tensor_tensor(fa[:, 2, :], fa[:, 0, :], fa[:, 1, :], ALU.add), f_agg)

            def small_variance(row, c):
                flink(dve.bn_stats(fst[:, :], row))
                flink(dve.tensor_tensor(fsc[:, c:c + 1], fst[:, 1:2], fst[:, 4:5], ALU.subtract))
                dve.tensor_tensor(fsc[:, c + 1:c + 2], fst[:, 1:2], fst[:, 4:5], ALU.add)
                dve.tensor_tensor(fsc[:, c + 2:c + 3], fst[:, 2:3], fst[:, 5:6], ALU.add)
                flink(dve.tensor_tensor(fsc[:, c:c + 1], fsc[:, c:c + 1], fsc[:, c:c + 1],
                                        ALU.mult))
                dve.tensor_scalar(fsc[:, c + 1:c + 2], fsc[:, c + 1:c + 2], 0.5, None, ALU.mult)
                flink(dve.scalar_tensor_tensor(fsc[:, c + 3:c + 4], fsc[:, c:c + 1],
                                               float(C // 4), fsc[:, c + 2:c + 3],
                                               ALU.mult, ALU.add))
                flink(dve.tensor_scalar(fsc[:, c + 4:c + 5], fsc[:, c + 3:c + 4], 1.0 / C, EPS,
                                        ALU.mult, ALU.add), f_var)

            dve.wait_ge(f_in, 32)
            small_variance(xf[:, :], 0)
            flink(dve.tensor_scalar(frow[:, 0, :], xf[:, :], fsc[:, 1:2], 0.0,
                                    ALU.subtract, ALU.max))
            dve.wait_ge(f_sd, 1)
            flink(dve.reciprocal(fsc[:, 3:4], fsc[:, 5:6]))
            flink(dve.scalar_tensor_tensor(frow[:, 1, :], frow[:, 0, :], fsc[:, 3:4], bp_b[:, :],
                                           ALU.mult, ALU.add))
            dve.wait_ge(f_proj, 1)
            flink(dve.tensor_tensor(frow[:, 2, :], v_ps[1][:, 0:C], frow[:, 1, :], ALU.add))
            small_variance(frow[:, 2, :], 6)
            flink(dve.tensor_tensor(frow[:, 4, :], frow[:, 2, :], xf[:, :], ALU.add))
            dve.wait_ge(f_sd, 2)
            flink(dve.reciprocal(fsc[:, 9:10], fsc[:, 11:12]))
            flink(dve.tensor_scalar(frow[:, 3, :], frow[:, 2, :], fsc[:, 9:10], None, ALU.mult),
                  f_z)
            dve.wait_ge(f_mlp, 1)
            flink(dve.tensor_tensor(frow[:, 5, :], q_ps[:, 0:C], frow[:, 4, :], ALU.add), f_row)


_W = ["Wq", "bq", "Wk", "bk", "Wv", "bv", "We", "Wp", "bp", "ln1_g", "ln1_b", "ln2_g", "ln2_b",
      "W1", "b1", "W2", "b2"]
_INS = ["x", "src", "dst", "edge_attr_32"] + [f"L0_gnn_{n}" for n in _W]


def kernel(**inputs):
    import numpy as _np
    import concourse.bacc as _bacc
    from concourse import mybir as _mybir
    from concourse.bass_utils import run_bass_kernel_spmd as _run

    nc = _bacc.Bacc("TRN2", target_bir_lowering=False, num_devices=1)
    f32 = _mybir.dt.float32
    arrays, args = {}, []
    for name in _INS:
        a = _np.ascontiguousarray(inputs[name])
        arrays[f"in_{name}"] = a
        args.append(nc.dram_tensor(f"in_{name}", a.shape, _mybir.dt.from_np(a.dtype),
                                   kind="ExternalInput").ap())
    n, c = inputs["x"].shape
    e = inputs["src"].shape[0]
    per = -(-e // (128 * 8)) * 8
    edge_rows = nc.dram_tensor("edge_rows", (128, per, c), f32, kind="Internal").ap()
    states = nc.dram_tensor("states", (128, per, 2 * c + 4), f32, kind="Internal").ap()
    out = nc.dram_tensor("out_0", (n, c), f32, kind="ExternalOutput").ap()
    gnn_layer(nc, *args, edge_rows, states, out)
    r = _run(nc, [arrays], core_ids=[0])
    return r.results[0]["out_0"]
```

```python
import concourse.bass as bass
from concourse import mybir
from contextlib import ExitStack



def gnn_layer(nc, x, src, dst, eattr, Wq, bq, Wk, bk, Wv, bv, We, Wp, bp,
              g1, be1, g2, be2, W1, b1, W2, b2, ends, edge_rows, states, out):
    f32 = mybir.dt.float32
    i32 = mybir.dt.int32
    bf16 = mybir.dt.bfloat16
    ALU = mybir.AluOpType
    ACT = mybir.ActivationFunctionType
    AX = mybir.AxisListType

    P = 128
    N, C = x.shape
    E, ED = eattr.shape
    H = 2
    HC = H * C
    NT, ET = 32, 8
    B = -(-E // (P * ET))
    EPP = B * ET
    PF = E // EPP
    EL = E - PF * EPP
    FULL_EA = EL // ET
    XT = 2 * ET
    ROWS = P * NT
    NB = -(-N // ROWS)
    LASTP = (N - (NB - 1) * ROWS) // NT
    NCH = NT // 8
    EPS = 1e-5
    FAR = float(2 ** 20)
    NEG = -1e30
    SW = HC + 2 * H
    assert NT == 2 * XT and NCH == 4 and PF == P - 1 and EL % ET == 0 and B % 2 == 1 and NB % 2 == 1
    assert (N - (NB - 1) * ROWS) % NT == 0
    KS = C + ED + 1
    KD = C + 1

    ctx = ExitStack()
    with ctx:
        def sb(name, shape, dt=f32):
            return ctx.enter_context(nc.sbuf_tensor(name, shape, dt))

        def pb(name, shape):
            return ctx.enter_context(nc.psum_tensor(name, shape, f32))

        def sem(name):
            return ctx.enter_context(nc.semaphore(name))

        def flat(ap):
            return ap.rearrange("p a t -> p (a t)")

        ident = sb("ident", [P, P])
        center = sb("center", [C, C])
        pick = {m: (sb(f"place_center_{m}", [C, m]), sb(f"place_bias_{m}", [C, m]),
                    sb(f"place_one_{m}", [1, m])) for m in (KS, KD)}
        center2 = sb("center2", [C, 2 * C])
        place_edge = sb("place_edge", [ED, KS])
        gcol = sb("gcol", [C, 4])
        wqkv = sb("wqkv", [C, 3, HC])
        gwqkv = sb("gwqkv", [C, 3, HC])
        bqkv = sb("bqkv", [1, 3, HC])
        we = sb("we", [ED, HC])
        wq_s = sb("wq_s", [KD, HC])
        wkv_s = sb("wkv_s", [KS, 2, HC])
        wp = sb("wp", [HC, C])
        w1 = sb("w1", [C, 2, C])
        gw1 = sb("gw1", [C, C])
        w1bd = sb("w1bd", [P, P])
        w2bd = sb("w2bd", [P, P])
        b1col = sb("b1col", [P, 1])
        b1g = sb("b1g", [P, 1])
        bp_b = sb("bp_b", [P, C])
        BR = (0, 32, 64)
        brow = sb("brow", [BR[-1] + 1, 2, C])
        bsplit = [sb(f"bsplit{i}", [BR[-1] + 1, 2, C], bf16) for i in range(3)]
        biases = sb("biases", [BR[-1] + 1, 2, 8, C], bf16)
        ones = sb("ones", [BR[-1] + 1, P], bf16)
        sel = sb("sel", [H, P])

        dsti = sb("dsti", [P, EPP + 2], i32)
        srci = sb("srci", [P, EPP], i32)
        dstg = sb("dstg", [P, EPP], i32)
        dstf = sb("dstf", [P, EPP + 2])
        same = sb("same", [P, EPP + 1])
        firstseg = sb("firstseg", [P, EPP])
        nofinal = sb("nofinal", [P, EPP])
        scati = sb("scati", [P, EPP], i32)
        keepm = sb("keepm", [P, B, H, ET + 1])
        fix = sb("fix", [P, 8])
        fixi = sb("fixi", [P, 2], i32)
        rowbase = sb("rowbase", [P, 1])
        idx = [sb(f"idx{i}", [P, XT], i32) for i in range(2)]
        ticks = sb("ticks", [P, 3])

        DX = [sb(f"DX{i}", [P, NT, C]) for i in range(2)]
        DY = sb("DY", [P, NT, C])
        DO = [sb(f"DO{i}", [P, NT, C]) for i in range(2)]
        XO = [sb(f"XO{i}", [P, NT, C]) for i in range(2)]
        OUTS = sb("OUTS", [P, NCH, 8 * C])
        z2 = sb("z2", [P, NCH, 8 * C])
        z2T = sb("z2T", [P, NCH, 512])
        hid = sb("hid", [P, NCH, 512])
        dst_x = sb("dst_x", [P, NT, 6])
        dst_o = sb("dst_o", [P, NT, 6])
        dsm = sb("dsm", [P, 4, NT])
        dsm2 = sb("dsm2", [P, 4, NT])
        dmean = sb("dmean", [P, NT])
        dvars = sb("dvars", [P, 2 * NT])
        dsd = sb("dsd", [P, 2 * NT])
        drs = sb("drs", [P, 2 * NT])

        G = [sb(f"G{i}", [P, XT, C]) for i in range(2)]
        X = [sb(f"X{i}", [P, XT, C]) for i in range(2)]
        XD = [sb(f"XD{i}", [P, ET, C]) for i in range(2)]
        Y = sb("Y", [P, XT, C])
        aug_s = [sb(f"aug_s{i}", [P, ET, KS]) for i in range(2)]
        aug_d = sb("aug_d", [P, ET, KD])
        HB = sb("HB", [P, ET, C])
        OE = [sb(f"OE{i}", [P, ET, C]) for i in range(2)]
        OUTE = sb("OUTE", [P, 8 * C])
        rec = [sb(f"rec{i}", [P, ET, SW]) for i in range(2)]
        xst = sb("xst", [P, XT, 6])
        yst = sb("yst", [P, XT, 6])
        ost = sb("ost", [P, ET, 6])
        sm = sb("sm", [P, 4, XT])
        nmean = sb("nmean", [P, XT])
        sm2 = sb("sm2", [P, 4, XT])
        sm3 = sb("sm3", [P, 4, ET])
        OV = 2 * XT
        VN = OV + ET
        vars_ = sb("vars_", [P, VN])
        sd = sb("sd", [P, VN])
        rs = sb("rs", [P, VN])
        srcT = DO[0][0:KS, 0:XT, :].rearrange("p (h t) c -> p h (t c)", h=2)
        dstT = DO[0][0:KD, XT:2 * XT, :].rearrange("p (h t) c -> p h (t c)", h=2)
        q_sb = DO[1][:, 0:XT, :].rearrange("p (h t) c -> p h (t c)", h=2)
        aggT = DO[1][:, XT:2 * XT, :].rearrange("p (h t) c -> p h (t c)", h=2)
        qk = DY[:, 0:XT, :].rearrange("p (t g) c -> p t (g c)", g=2)
        factors = sb("factors", [P, H, C, ET + 1])
        weighted = flat(XO[0][:, :, :])[:, 0:HC * (ET + 1)].rearrange("p (c t) -> p c t", c=HC)
        running = flat(XO[1][:, :, :])[:, 0:HC * (ET + 1)].rearrange("p (c t) -> p c t", c=HC)
        alpha = sb("alpha", [P, H, ET + 1])
        mx = [sb(f"mx{i}", [P, H, ET + 1]) for i in range(2)]
        den = [sb(f"den{i}", [P, H, ET + 1]) for i in range(2)]
        ex = sb("ex", [P, 2, H, ET])
        cw = sb("cw", [P, 2, H, ET + 1])
        rden = sb("rden", [P, 2, H, ET])
        z2e = sb("z2e", [P, 8 * C])
        z2eT = sb("z2eT", [P, 512])
        hide = sb("hide", [P, 512])
        frec = sb("frec", [P, SW])
        xf = sb("xf", [P, C])
        fT = sb("fT", [P, 2, P])
        fsm = sb("fsm", [H, 6, P])
        fkeep = sb("fkeep", [H, 2, P])
        mj = sb("mj", [H, P + 1])
        dj = sb("dj", [H, P + 1])
        fk = sb("fk", [H, 8, P])
        fex = sb("fex", [H, 4, P])
        fcw = sb("fcw", [H, 4, P])
        bc = sb("bc", [P, 4, P])
        aj = sb("aj", [P, P + 1])
        fa = sb("fa", [P, 3, P])
        fflag = sb("fflag", [P, 2, H])
        frow = sb("frow", [P, 6, C])
        fst = sb("fst", [P, 6])
        fsc = sb("fsc", [P, 12])
        fzT = sb("fzT", [C, 2, P])

        tp = [pb(f"tp{i}", [P, 512]) for i in range(2)]
        k_ps = pb("k_ps", [P, 512])
        q_ps = pb("q_ps", [P, 512])
        v_ps = [pb(f"v_ps{i}", [P, 512]) for i in range(2)]
        hid_ps = pb("hid_ps", [P, 512])
        res_ps = pb("res_ps", [P, 512])
        hid_b, res_b = (hid_ps, k_ps), (res_ps, q_ps)

        pads_set = sem("pads_set")
        tables_in = sem("tables_in")
        consts_in = sem("consts_in")
        built = sem("built")
        link_done = sem("link_done")
        w_placed = sem("w_placed")
        w_folded = sem("w_folded")
        w_ready = sem("w_ready")
        d_in = [sem(f"d_in{i}") for i in range(2)]
        d_xstats, d_xsums, d_mean = sem("d_xstats"), sem("d_xsums"), sem("d_mean")
        d_xdiff2, d_xv64, d_xvar = sem("d_xdiff2"), sem("d_xv64"), sem("d_xvar")
        d_ostats, d_osums = sem("d_ostats"), sem("d_osums")
        d_odiff2, d_ov64, d_ovar = sem("d_odiff2"), sem("d_ov64"), sem("d_ovar")
        d_centered = sem("d_centered")
        d_relued = sem("d_relued")
        d_biased = sem("d_biased")
        d_xused = sem("d_xused")
        d_sd, d_rs = sem("d_sd"), sem("d_rs")
        z2_ready = [sem(f"z2_ready{c}") for c in range(NCH)]
        z_T = [sem(f"z_T{c}") for c in range(NCH)]
        z_ev = [sem(f"z_ev{c}") for c in range(NCH)]
        hid_mm = [sem(f"hid_mm{c}") for c in range(NCH)]
        gelu_done = [sem(f"gelu_done{c}") for c in range(NCH)]
        mlp_mm = [sem(f"mlp_mm{c}") for c in range(NCH)]
        out_ready = [sem(f"out_ready{c}") for c in range(NCH)]
        stored = [sem(f"stored{c}") for c in range(NCH)]
        tabled = sem("tabled")
        idx_ready = sem("idx_ready")
        ticked = sem("ticked")
        gathered = [sem(f"gathered{i}") for i in range(2)]
        ends_stored = [sem(f"ends_stored{i}") for i in range(2)]
        ends_in = [sem(f"ends_in{i}") for i in range(2)]
        xd_in = [sem(f"xd_in{i}") for i in range(2)]
        eattr_in = [sem(f"eattr_in{i}") for i in range(2)]
        x_stats = sem("x_stats")
        x_sums = sem("x_sums")
        x_mean = sem("x_mean")
        x_diff2 = sem("x_diff2")
        x_v64 = sem("x_v64")
        x_var = sem("x_var")
        relued = sem("relued")
        y_stats = sem("y_stats")
        y_sums = sem("y_sums")
        y_diff2 = sem("y_diff2")
        y_v64 = sem("y_v64")
        y_var = sem("y_var")
        sd_ready = sem("sd_ready")
        rs_ready = sem("rs_ready")
        zsrc_ready = sem("zsrc_ready")
        zdst_ready = sem("zdst_ready")
        h_ready = sem("h_ready")
        src_T, dst_T = sem("src_T"), sem("dst_T")
        agg_T = sem("agg_T")
        src_ev, dst_ev = sem("src_ev"), sem("dst_ev")
        agg_ev = sem("agg_ev")
        q_mm, k_mm, v_mm = sem("q_mm"), sem("k_mm"), sem("v_mm")
        q_evac = sem("q_evac")
        qk_ready = sem("qk_ready")
        alpha_ready = sem("alpha_ready")
        mx_ready = sem("mx_ready")
        mx_diff = sem("mx_diff")
        ex_ready = sem("ex_ready")
        cw_ready = sem("cw_ready")
        den_prev_in = sem("den_prev_in")
        den_ready = sem("den_ready")
        den_eps = sem("den_eps")
        rden_ready = sem("rden_ready")
        wv_ready = sem("wv_ready")
        spread_ready = sem("spread_ready")
        scanned = sem("scanned")
        aggn_ready = sem("aggn_ready")
        proj_mm = sem("proj_mm")
        o_proj = sem("o_proj")
        o_stats = sem("o_stats")
        o_sums = sem("o_sums")
        o_diff2 = sem("o_diff2")
        o_v64 = sem("o_v64")
        o_var = sem("o_var")
        z2e_ready = sem("z2e_ready")
        ze_T = sem("ze_T")
        ze_ev = sem("ze_ev")
        hide_mm = sem("hide_mm")
        gelue_done = sem("gelue_done")
        mlpe_mm = sem("mlpe_mm")
        oute_ready = sem("oute_ready")
        rows_stored = sem("rows_stored")
        state_stored = [sem(f"state_stored{i}") for i in range(2)]
        rows_in = [sem(f"rows_in{i}") for i in range(2)]
        scattered = [sem(f"scattered{i}") for i in range(2)]
        f_in = sem("f_in")
        f_link = sem("f_link")
        f_T = sem("f_T")
        f_exp_in = sem("f_exp_in")
        f_exp = sem("f_exp")
        f_coef = sem("f_coef")
        f_bc = sem("f_bc")
        f_agg = sem("f_agg")
        f_proj = sem("f_proj")
        f_var = sem("f_var")
        f_sd = sem("f_sd")
        f_z = sem("f_z")
        f_zT = sem("f_zT")
        f_zev = sem("f_zev")
        f_hid = sem("f_hid")
        f_gelu = sem("f_gelu")
        f_mlp = sem("f_mlp")
        f_row = sem("f_row")
        f_out = sem("f_out")

        def wide(ap, n):
            return ap.unsqueeze(2).broadcast_to([ap.shape[0], ap.shape[1], n])

        def rows(ap, n):
            return ap.unsqueeze(1).broadcast_to([ap.shape[0], n, ap.shape[1]])

        def tiles(ap):
            return ap.rearrange("p (t c) -> p t c", c=C)

        ea_main = eattr[0:PF * EPP, :].rearrange("(p t) c -> p t c", t=EPP)
        ea_last = eattr[PF * EPP:E, :].rearrange("(p t) c -> p t c", p=1)
        ECUT = PF // 16 * 16
        LCUT = LASTP // 16 * 16

        block = ctx.enter_context(nc.Block())

        @block.sync
        def _(sp):
            def load_nodes(d, par, tail=False, first=False):
                if not first:
                    sp.wait_ge(d_xused, d - 1)
                if tail:
                    xb = x[d * ROWS:N, :].rearrange("(p j) c -> p j c", j=NT)
                    sp.dma_start(DX[par][0:LCUT], xb[0:LCUT]).then_inc(d_in[par], 16)
                    sp.dma_start(DX[par][LCUT:LASTP], xb[LCUT:LASTP]).then_inc(d_in[par], 16)
                else:
                    xb = x[bass.ds(d * ROWS, ROWS), :].rearrange("(p j) c -> p j c", j=NT)
                    sp.dma_start(DX[par][0:P // 2], xb[0:P // 2]).then_inc(d_in[par], 16)
                    sp.dma_start(DX[par][P // 2:P], xb[P // 2:P]).then_inc(d_in[par], 16)

            def store_nodes(d, tail=False):
                for c in range(NCH):
                    sp.wait_ge(out_ready[c], d + 1)
                    t = slice(8 * c, 8 * c + 8)
                    if tail:
                        ob = out[d * ROWS:N, :].rearrange("(p j) c -> p j c", j=NT)[:, t]
                        sp.dma_start(ob[0:LCUT], tiles(OUTS[0:LCUT, c, :])).then_inc(stored[c], 16)
                        sp.dma_start(ob[LCUT:LASTP], tiles(OUTS[LCUT:LASTP, c, :]))\
                          .then_inc(stored[c], 16)
                    else:
                        ob = out[bass.ds(d * ROWS, ROWS), :].rearrange("(p j) c -> p j c", j=NT)
                        sp.dma_start(ob[:, t], tiles(OUTS[:, c, :])).then_inc(stored[c], 16)

            def load_edges(b, par, n, full=True, first=False):
                sp.wait_ge(ends_stored[par], 16 * n)
                if not first:
                    sp.wait_ge(relued, 2 * b - 2)
                sp.dma_start(X[par][:, :, :], ends[:, bass.ds(b * XT, XT), :])\
                  .then_inc(ends_in[par], 16)
                if not first:
                    sp.wait_ge(src_T, 2 * (b - 1))
                ea = aug_s[par][:, :, C:C + ED]
                sp.dma_start(ea[0:ECUT], ea_main[0:ECUT, bass.ds(b * ET, ET), :])\
                  .then_inc(eattr_in[par], 16)
                sp.dma_start(ea[ECUT:PF], ea_main[ECUT:PF, bass.ds(b * ET, ET), :])\
                  .then_inc(eattr_in[par], 16)
                sp.dma_start(ea[PF:P], ea_last[:, bass.ds(b * ET, ET) if full else slice(0, ET), :])\
                  .then_inc(eattr_in[par], 16)

            def load_targets(b, par, first=False):
                if not first:
                    sp.wait_ge(mlpe_mm, b - 1)
                sp.dma_start(XD[par][:, :, :], ends[:, bass.ds(b * XT + ET, ET), :])\
                  .then_inc(xd_in[par], 16)

            def store_targets(b):
                sp.wait_ge(oute_ready, b + 1)
                sp.dma_start(edge_rows[:, bass.ds(b * ET, ET), :], tiles(OUTE[:, :]))\
                  .then_inc(rows_stored, 16)

            def store_states(s, par):
                sp.wait_ge(aggn_ready, 2 * (s + 1))
                sp.dma_start(states[:, bass.ds(s * ET, ET), :], rec[par][:, :, :])\
                  .then_inc(state_stored[par], 16)

            sp.wait_ge(pads_set, 1)
            sp.dma_start(dsti[0:PF, 1:EPP + 1], dst[0:PF * EPP].rearrange("(p t) -> p t", t=EPP))\
              .then_inc(tables_in, 16)
            sp.dma_start(dsti[PF:P, 1:EL + 1], dst[PF * EPP:E].rearrange("(p t) -> p t", p=1))\
              .then_inc(tables_in, 16)
            sp.dma_start(srci[0:PF, 0:EPP], src[0:PF * EPP].rearrange("(p t) -> p t", t=EPP))\
              .then_inc(tables_in, 16)
            sp.dma_start(srci[PF:P, 0:EL], src[PF * EPP:E].rearrange("(p t) -> p t", p=1))\
              .then_inc(tables_in, 16)
            dst_pt = dst[0:PF * EPP].rearrange("(p t) -> p t", t=EPP)
            with nc.allow_non_contiguous_dma(reason="one element per partition, once"):
                sp.dma_start(dsti[1:P, 0:1], dst_pt[:, EPP - 1:EPP]).then_inc(tables_in, 16)
                sp.dma_start(dsti[0:PF - 1, EPP + 1:EPP + 2], dst_pt[1:PF, 0:1])\
                  .then_inc(tables_in, 16)
                sp.dma_start(dsti[PF - 1:PF, EPP + 1:EPP + 2],
                             dst[PF * EPP:PF * EPP + 1].rearrange("(p t) -> p t", p=1))\
                  .then_inc(tables_in, 16)
            load_nodes(0, 0, first=True)
            with nc.allow_non_contiguous_dma(reason="bias columns, once"):
                for i, v in enumerate((g1, be1, g2, be2)):
                    sp.dma_start(gcol[:, i:i + 1], v.rearrange("(c a) -> c a", a=1))\
                      .then_inc(consts_in, 16)
                for h in range(2):
                    sp.dma_start(b1col[h * C:(h + 1) * C, :], b1.rearrange("(c a) -> c a", a=1))\
                      .then_inc(consts_in, 16)
            for i, (w, b) in enumerate(((Wq, bq), (Wk, bk), (Wv, bv))):
                sp.dma_start(wqkv[:, i, :], w).then_inc(consts_in, 16)
                sp.dma_start(bqkv[:, i, :], b.rearrange("(a c) -> a c", a=1)).then_inc(consts_in, 16)
            sp.dma_start(we[:, :], We).then_inc(consts_in, 16)
            sp.dma_start(wp[:, :], Wp).then_inc(consts_in, 16)
            sp.wait_ge(pads_set, 2)
            for h in range(2):
                sp.dma_start(w1[:, h, :], W1).then_inc(consts_in, 16)
                sp.dma_start(w2bd[h * C:(h + 1) * C, h * C:(h + 1) * C], W2).then_inc(consts_in, 16)
            sp.dma_start(bp_b[:, :], bp.rearrange("(a c) -> a c", a=1).broadcast_to([P, C]))\
              .then_inc(consts_in, 16)
            for i, b in enumerate((bp, b2)):
                sp.dma_start(brow[:, i, :], b.rearrange("(a c) -> a c", a=1)
                             .broadcast_to([BR[-1] + 1, C])).then_inc(consts_in, 16)
            load_nodes(1, 1, first=True)
            load_nodes(2, 0)
            with sp.Fori(1, NB // 2 - 1) as k:
                load_nodes(2 * k + 1, 1)
                store_nodes(2 * k - 2)
                load_nodes(2 * k + 2, 0)
                store_nodes(2 * k - 1)
            load_nodes(NB - 2, 1)
            store_nodes(NB - 5)
            load_nodes(NB - 1, 0, tail=True)
            store_nodes(NB - 4)
            load_edges(0, 0, 1, first=True)
            load_edges(1, 1, 1, first=True)
            store_nodes(NB - 3)
            store_nodes(NB - 2)
            store_nodes(NB - 1, tail=True)

            def step(s, par, n, load=True, targets=True, **kw):
                if load:
                    load_edges(s + 2, par, n + 1, **kw)
                load_targets(s, par, first=not targets)
                if targets:
                    store_targets(s - 2)
                store_states(s, par)

            step(0, 0, 1, targets=False)
            step(1, 1, 1, targets=False)
            SPLIT = (FULL_EA - 2) // 2
            with sp.Fori(1, SPLIT) as k:
                step(2 * k, 0, k + 1)
                step(2 * k + 1, 1, k + 1)
            for s in (2 * SPLIT, 2 * SPLIT + 1):
                step(s, s % 2, SPLIT + 1, full=s + 2 < FULL_EA)
            with sp.Fori(SPLIT + 1, (B - 3) // 2) as k:
                step(2 * k, 0, k + 1, full=False)
                step(2 * k + 1, 1, k + 1, full=False)
            for s in range(B - 3, B):
                step(s, s % 2, s // 2 + 1, load=s + 2 < B, full=False)
            store_targets(B - 2)
            store_targets(B - 1)

        @block.gpsimd
        def _(pool):
            pool.memset(ident[:, :], 0.0).then_inc(built, 1)
            pool.memset(sel[:, :], 1.0).then_inc(built, 1)
            pool.wait_ge(built, 2)
            pool.affine_select(out=ident[:, :], in_=ident[:, :], compare_op=ALU.not_equal, fill=1.0,
                               base=0, pattern=[[-1, P]], channel_multiplier=1).then_inc(built, 1)
            pool.affine_select(out=sel[:, :], in_=sel[:, :], compare_op=ALU.is_ge, fill=0.0,
                               base=0, pattern=[[1, P]], channel_multiplier=-C).then_inc(built, 1)
            pool.wait_ge(built, 4)
            pool.affine_select(out=sel[:, :], in_=sel[:, :], compare_op=ALU.is_ge, fill=0.0,
                               base=C - 1, pattern=[[-1, P]], channel_multiplier=C).then_inc(built, 1)
            pool.iota(rowbase[:, :], [[0, 1]], base=-1, channel_multiplier=EPP,
                      allow_small_or_imprecise_dtypes=True).then_inc(built, 1)

            pool.memset(ticks[:, :], 0.0).then_inc(built, 1)
            pool.wait_ge(built, 7)

            def tick(i, first=False):
                if not first:
                    pool.wait_ge(ticked, i)
                pool.tensor_tensor(ticks[:, 0:1], ticks[:, 1:2], ticks[:, 2:3], ALU.add)\
                    .then_inc(ticked, 1)

            def gather_block(b, par, n, i, first=False):
                if not first:
                    pool.wait_ge(ends_stored[par], 16 * (n - 1))
                pool.tensor_copy(idx[par][:, 0:ET], srci[:, bass.ds(b * ET, ET)])
                pool.tensor_copy(idx[par][:, ET:XT], dstg[:, bass.ds(b * ET, ET)])\
                    .then_inc(idx_ready, 1)
                pool.wait_ge(idx_ready, b + 1)
                tick(i, first=isinstance(i, int) and i == 0)
                for t in range(XT):
                    pool.indirect_dma_start(
                        G[par][:, t, :], None, x,
                        bass.IndirectOffsetOnAxis(ap=idx[par][:, t:t + 1], axis=0))\
                        .then_inc(gathered[par], 16)

            def keep_block(b, par, n, i):
                pool.wait_ge(gathered[par], 16 * XT * n)
                tick(i)
                pool.dma_start(ends[:, bass.ds(b * XT, XT), :], G[par][:, :, :])\
                    .then_inc(ends_stored[par], 16)

            pool.wait_ge(tabled, 1)
            gather_block(0, 0, 1, 0, first=True)
            gather_block(1, 1, 1, 1, first=True)
            keep_block(0, 0, 1, 2)
            with pool.Fori(1, B // 2) as k:
                gather_block(2 * k, 0, k + 1, 4 * k - 1)
                keep_block(2 * k - 1, 1, k, 4 * k)
                gather_block(2 * k + 1, 1, k + 1, 4 * k + 1)
                keep_block(2 * k, 0, k + 1, 4 * k + 2)
            gather_block(B - 1, 0, B // 2 + 1, 2 * B - 3)
            keep_block(B - 2, 1, B // 2, 2 * B - 2)
            keep_block(B - 1, 0, B // 2 + 1, 2 * B - 1)

            for c in range(NCH):
                pool.wait_ge(stored[c], 16 * (NB + 1))
            pool.wait_ge(ends_stored[1], 16 * (B // 2))
            pool.wait_ge(ends_stored[0], 16 * (B // 2 + 1))
            last_row = pool.to_reg(N - 1)
            T0 = 2 * B

            def fetch_rows(b, par, n, i, first=False):
                pool.wait_ge(rows_stored, 16 * (b + 1))
                if not first:
                    pool.wait_ge(scattered[par], 16 * ET * (n - 1))
                pool.tensor_copy(idx[par][:, 0:ET], scati[:, bass.ds(b * ET, ET)])\
                    .then_inc(idx_ready, 1)
                pool.wait_ge(idx_ready, B + b + 1)
                tick(i)
                pool.dma_start(G[par][:, 0:ET, :], edge_rows[:, bass.ds(b * ET, ET), :])\
                    .then_inc(rows_in[par], 16)

            def scatter_block(par, n, i):
                pool.wait_ge(rows_in[par], 16 * n)
                tick(i)
                for t in range(ET):
                    pool.indirect_dma_start(
                        out, bass.IndirectOffsetOnAxis(ap=idx[par][:, t:t + 1], axis=0),
                        G[par][:, t, :], None, bounds_check=last_row, oob_is_err=False)\
                        .then_inc(scattered[par], 16)

            fetch_rows(0, 0, 1, T0, first=True)
            fetch_rows(1, 1, 1, T0 + 1, first=True)
            scatter_block(0, 1, T0 + 2)
            with pool.Fori(1, B // 2) as k:
                fetch_rows(2 * k, 0, k + 1, T0 + 4 * k - 1)
                scatter_block(1, k, T0 + 4 * k)
                fetch_rows(2 * k + 1, 1, k + 1, T0 + 4 * k + 1)
                scatter_block(0, k + 1, T0 + 4 * k + 2)

            pool.wait_ge(state_stored[0], 16 * (B // 2 + 1))
            pool.wait_ge(state_stored[1], 16 * (B // 2))
            pool.wait_ge(w_ready, 1)
            pool.indirect_dma_start(frec[:, :], None, states.rearrange("p t c -> (p t) c"),
                                    bass.IndirectOffsetOnAxis(ap=fixi[:, 0:1], axis=0))\
                .then_inc(f_in, 16)
            pool.indirect_dma_start(xf[:, :], None, x,
                                    bass.IndirectOffsetOnAxis(ap=dstg[:, 0:1], axis=0))\
                .then_inc(f_in, 16)
            scatter_block(1, B // 2, T0 + 2 * B - 3)
            fetch_rows(B - 1, 0, B // 2 + 1, T0 + 2 * B - 2)
            scatter_block(0, B // 2 + 1, T0 + 2 * B - 1)
            pool.wait_ge(f_row, 1)
            pool.indirect_dma_start(out, bass.IndirectOffsetOnAxis(ap=fixi[:, 1:2], axis=0),
                                    frow[:, 5, :], None, bounds_check=N - 1, oob_is_err=False)\
                .then_inc(f_out, 16)
            pool.wait_ge(scattered[0], 16 * ET * (B // 2 + 1))
            pool.wait_ge(scattered[1], 16 * ET * (B // 2))
            pool.wait_ge(f_out, 16)

        @block.tensor
        def _(pe):
            pe.wait_ge(consts_in, 16 * 21)
            pe.wait_ge(w_placed, 1)

            def fold(outp, m, i, n, edge):
                lc, lb, lo = pick[m]
                def r(t):
                    return flat(t[:, i:i + n, :])
                pe.matmul(outp, lc[:, :], r(gwqkv), start=True, stop=False)
                pe.matmul(outp, lb[:, :], r(wqkv), start=False, stop=False)
                if edge:
                    for a in range(n):
                        pe.matmul(outp[:, a * HC:(a + 1) * HC], place_edge[:, :], we[:, :],
                                  start=False, stop=False)
                pe.matmul(outp, lo[:, :], r(bqkv), start=False, stop=True)

            fold(q_ps[0:KD, 0:HC], KD, 0, 1, False)
            fold(k_ps[0:KS, 0:2 * HC], KS, 1, 2, True)
            pe.matmul(tp[0][:, 0:C], center2[:, :], gw1[:, :], start=True, stop=True)
            pe.matmul(hid_ps[:, 0:1], flat(w1[:, :, :]), gcol[:, 3:4], start=True, stop=True)\
              .then_inc(w_folded, 1)
            pe.wait_ge(w_ready, 1)

            def transposes(bank, m, srcs, done):
                for j, a in enumerate(srcs):
                    ins = pe.transpose(tp[bank][0:m, j * P:(j + 1) * P], a, ident[:, :])
                ins.then_inc(done, 1)

            def nodes_mlp(d, par, first=False):
                def turn(c):
                    pe.wait_ge(z2_ready[c], d + 1)
                    if c >= 2:
                        pe.wait_ge(z_ev[c - 2], d + 1)
                    elif not first:
                        pe.wait_ge(z_ev[c + 2], d)
                    transposes(c % 2, P, [z2[:, c, j * P:(j + 1) * P] for j in range(4)], z_T[c])

                def up(c):
                    pe.wait_ge(z_ev[c], d + 1)
                    if c >= 2:
                        pe.wait_ge(gelu_done[c - 2], d + 1)
                    pe.matmul(hid_b[c % 2][:, :], w1bd[:, :], z2T[:, c, :], start=True, stop=True)\
                      .then_inc(hid_mm[c], 1)

                def rest(c):
                    if c >= 2:
                        pe.wait_ge(out_ready[c - 2], d + 1)
                    elif not first:
                        pe.wait_ge(out_ready[c + 2], d)
                    if c == 0:
                        pe.wait_ge(d_xused, d + 1)
                    r = res_b[c % 2]
                    pe.matmul(r[:, :], ones[:, :], flat(biases[:, 1, :, :]),
                              start=True, stop=False)
                    pe.matmul(r[:, :], ident[:, :], flat(XO[par][:, 8 * c:8 * c + 8, :]),
                              start=False, stop=False)

                def down(c):
                    pe.wait_ge(gelu_done[c], d + 1)
                    r = res_b[c % 2]
                    for j in range(4):
                        ins = pe.matmul(r[:, j * P:(j + 1) * P], hid[:, c, j * P:(j + 1) * P],
                                        w2bd[:, :], start=False, stop=j == 3)
                    ins.then_inc(mlp_mm[c], 1)

                for c in range(2):
                    turn(c)
                    rest(c)
                    up(c)
                down(0)
                for c in range(2, NCH):
                    turn(c)
                    down(c - 1)
                    up(c)
                    rest(c)
                down(NCH - 1)

            nodes_mlp(0, 0, first=True)
            with pe.Fori(0, NB // 2) as k:
                nodes_mlp(2 * k + 1, 1)
                nodes_mlp(2 * k + 2, 0)
            for c in range(NCH):
                pe.wait_ge(out_ready[c], NB)

            def project_half(s, h):
                pe.wait_ge(agg_ev, 2 * s + h + 1)
                for j in range(4):
                    ins = pe.matmul(res_ps[:, (4 * h + j) * C:(4 * h + j + 1) * C],
                                    aggT[:, h, j * P:(j + 1) * P], wp[:, :],
                                    start=False, stop=h == 1 and j == 3)
                if h == 1:
                    ins.then_inc(proj_mm, 1)

            def turn_targets(s, qkv_done=True):
                if qkv_done:
                    pe.wait_ge(src_ev, 2 * s + 2)
                else:
                    pe.wait_ge(agg_ev, 2 * B)
                    pe.wait_ge(ze_ev, s - 2)
                pe.wait_ge(z2e_ready, s - 1)
                transposes(0, P, [z2e[:, j * P:(j + 1) * P] for j in range(4)], ze_T)

            def qkv(s, par, n, with_mlp=True, first=False):
                pe.wait_ge(eattr_in[par], 48 * n)
                pe.wait_ge(zsrc_ready, s + 1)
                if not first:
                    pe.wait_ge(agg_ev, 2 * s)
                for h in range(2):
                    if h:
                        pe.wait_ge(src_ev, 2 * s + 1)
                    transposes(0, KS, [aug_s[par][:, 4 * h + j, :] for j in range(4)], src_T)
                    if h:
                        pe.wait_ge(dst_ev, 2 * s + 1)
                    else:
                        pe.wait_ge(zdst_ready, s + 1)
                    transposes(1, KD, [aug_d[:, 4 * h + j, :] for j in range(4)], dst_T)

                def q(h):
                    pe.wait_ge(dst_ev, 2 * s + h + 1)
                    if h or not first:
                        pe.wait_ge(q_evac, 2 * s + h)
                    for j in range(4):
                        ins = pe.matmul(q_ps[:, j * P:(j + 1) * P], dstT[:, h, j * P:(j + 1) * P],
                                        wq_s[:, :], start=True, stop=True)
                    ins.then_inc(q_mm, 1)

                def k(h):
                    pe.wait_ge(src_ev, 2 * s + h + 1)
                    if h or not first:
                        pe.wait_ge(qk_ready, 2 * s + h)
                    for j in range(4):
                        ins = pe.matmul(k_ps[:, j * P:(j + 1) * P], srcT[:, h, j * P:(j + 1) * P],
                                        wkv_s[:, 0, :], start=True, stop=True)
                    ins.then_inc(k_mm, 1)

                def v(h):
                    if not first:
                        pe.wait_ge(wv_ready, 2 * (s - 1) + h + 1)
                    for j in range(4):
                        ins = pe.matmul(v_ps[h][:, j * P:(j + 1) * P],
                                        srcT[:, h, j * P:(j + 1) * P],
                                        wkv_s[:, 1, :], start=True, stop=True)
                    ins.then_inc(v_mm, 1)

                q(0)
                k(0)
                q(1)
                if with_mlp:
                    turn_targets(s)
                k(1)
                v(0)
                v(1)

            def targets_mlp(s, par, n, qkv_done=True):
                pe.wait_ge(ze_ev, s - 1)
                pe.matmul(hid_ps[:, :], w1bd[:, :], z2eT[:, :], start=True, stop=True)\
                  .then_inc(hide_mm, 1)
                pe.wait_ge(o_proj, s if qkv_done else B)
                if not qkv_done:
                    pe.wait_ge(oute_ready, s - 2)
                pe.wait_ge(xd_in[par], 16 * n)
                pe.matmul(res_ps[:, :], ones[:, :], flat(biases[:, 1, :, :]),
                          start=True, stop=False)
                pe.matmul(res_ps[:, :], ident[:, :], flat(XD[par][:, :, :]),
                          start=False, stop=False)
                pe.matmul(res_ps[:, :], ident[:, :], flat(OE[par][:, :, :]),
                          start=False, stop=False)
                pe.wait_ge(gelue_done, s - 1)
                for j in range(4):
                    ins = pe.matmul(res_ps[:, j * P:(j + 1) * P], hide[:, j * P:(j + 1) * P],
                                    w2bd[:, :], start=False, stop=j == 3)
                ins.then_inc(mlpe_mm, 1)

            def project(s, par, mlp_before):
                for h, bank in enumerate((tp[0], hid_ps)):
                    pe.wait_ge(aggn_ready, 2 * s + h + 1)
                    if mlp_before and h == 0:
                        pe.wait_ge(ze_ev, s - 1)
                    for j in range(4):
                        ins = pe.transpose(bank[:, j * P:(j + 1) * P],
                                           rec[par][:, 4 * h + j, 0:HC], ident[:, :])
                    ins.then_inc(agg_T, 1)
                if mlp_before:
                    pe.wait_ge(oute_ready, s - 1)
                pe.matmul(res_ps[:, :], ones[:, :], flat(biases[:, 0, :, :]),
                          start=True, stop=False)
                project_half(s, 0)
                project_half(s, 1)

            qkv(0, 0, 1, with_mlp=False, first=True)
            project(0, 0, False)
            qkv(1, 1, 1, with_mlp=False)
            project(1, 1, False)
            with pe.Fori(1, B // 2) as k:
                for par in range(2):
                    qkv(2 * k + par, par, k + 1)
                    targets_mlp(2 * k + par, par, k)
                    project(2 * k + par, par, True)
            qkv(B - 1, 0, B // 2 + 1)
            targets_mlp(B - 1, 0, B // 2)
            project(B - 1, 0, True)
            turn_targets(B, qkv_done=False)
            targets_mlp(B, 1, B // 2, qkv_done=False)
            turn_targets(B + 1, qkv_done=False)
            targets_mlp(B + 1, 0, B // 2 + 1, qkv_done=False)

            last = rec[(B - 1) % 2]
            pe.wait_ge(f_in, 32)
            pe.transpose(k_ps[:, 0:P], frec[:, 0:HC], ident[:, :])
            pe.transpose(k_ps[:, P:2 * P], last[:, ET - 1, 0:HC], ident[:, :])
            for i, a in enumerate((frec[:, HC:HC + H], frec[:, HC + H:SW],
                                   last[:, ET - 1, HC:HC + H], last[:, ET - 1, HC + H:SW])):
                pe.transpose(q_ps[0:H, i * P:(i + 1) * P], a, ident[:, :])
            for i in range(2):
                ins = pe.transpose(k_ps[0:H, (2 + i) * P:(3 + i) * P], fflag[:, i, :], ident[:, :])
            ins.then_inc(f_T, 1)
            pe.wait_ge(f_coef, 1)
            pe.matmul(v_ps[0][:, :], sel[:, :], flat(fk[:, 0:4, :]), start=True, stop=True)\
              .then_inc(f_bc, 1)
            pe.wait_ge(f_agg, 1)
            pe.matmul(v_ps[1][:, 0:C], fa[:, 2, :], wp[:, :], start=True, stop=True)\
              .then_inc(f_proj, 1)
            pe.wait_ge(f_z, 1)
            pe.transpose(v_ps[0][0:C, 0:P], frow[:, 3, :], ident[:, :]).then_inc(f_zT, 1)
            pe.wait_ge(f_zev, 1)
            pe.matmul(v_ps[1][0:C, P:2 * P], w1bd[0:C, 0:C], fzT[:, 0, :], start=True, stop=True)\
              .then_inc(f_hid, 1)
            pe.wait_ge(f_gelu, 1)
            pe.matmul(q_ps[:, 0:C], ones[:, :], biases[:, 1, 0, :], start=True, stop=False)
            pe.matmul(q_ps[:, 0:C], fzT[:, 1, :], w2bd[0:C, 0:C], start=False, stop=True)\
              .then_inc(f_mlp, 1)

        @block.scalar
        def _(act):
            def nodes_relu(d, par, c, half, early=False):
                if c % 2 == 0 and half == 0:
                    act.wait_ge(d_centered, 2 * d + c // 2 + 1)
                if c == 0 and half == 0:
                    act.wait_ge(d_rs, d + 1)
                    if not early:
                        act.wait_ge(d_xused, d - 1)
                for t in range(8 * c + 4 * half, 8 * c + 4 * half + 4):
                    ins = act.activation(DO[par][:, t, :], DY[:, t, :], ACT.Relu,
                                         scale=drs[:, t:t + 1])
                if half == 1:
                    ins.then_inc(d_relued, 1)

            def turned_chunk(d, c):
                act.wait_ge(z_T[c], d)
                act.activation(z2T[:, c, :], tp[c % 2][:, :], ACT.Copy).then_inc(z_ev[c], 1)

            def out_chunk(d, c, early=False):
                act.wait_ge(mlp_mm[c], d)
                if not early:
                    act.wait_ge(stored[c], 16 * (d - 1))
                act.activation(OUTS[:, c, :], res_b[c % 2][:, :], ACT.Copy)\
                   .then_inc(out_ready[c], 1)

            def nodes_step(d, par, relus=True, mlp=True, outs=True, early=False, early_outs=False,
                           between=None):
                if relus:
                    act.wait_ge(d_xvar, d + 1)
                if mlp:
                    act.wait_ge(d_ovar, d)
                act.activation(dsd[:, :], dvars[:, :], ACT.Sqrt).then_inc(d_sd, 1)
                if outs:
                    out_chunk(d - 1, NCH - 2, early_outs)
                    out_chunk(d - 1, NCH - 1, early_outs)

                def relu(c, half):
                    if relus:
                        nodes_relu(d, par, c, half, isinstance(d, int) and d < 2)

                def gelu(c):
                    if mlp:
                        act.wait_ge(hid_mm[c], d)
                        act.activation(hid[:, c, :], hid_b[c % 2][:, :], ACT.Gelu,
                                       bias=b1g[:, 0:1]).then_inc(gelu_done[c], 1)

                relu(0, 0)
                if mlp:
                    turned_chunk(d, 0)
                relu(0, 1)
                relu(1, 0)
                if mlp:
                    turned_chunk(d, 1)
                relu(1, 1)
                for c in (2, 3):
                    relu(c, 0)
                    relu(c, 1)
                gelu(0)
                gelu(1)
                for c in range(2, NCH):
                    if mlp:
                        turned_chunk(d, c)
                        out_chunk(d, c - 2, early)
                    gelu(c)
                    if between is not None and c == 2:
                        between()

            nodes_step(0, 0, mlp=False, outs=False)
            nodes_step(1, 1, outs=False, early=True)
            nodes_step(2, 0, early_outs=True)
            with act.Fori(1, NB // 2) as k:
                nodes_step(2 * k + 1, 1)
                nodes_step(2 * k + 2, 0)

            def evacuate_qkv(s, between):
                for h in range(2):
                    act.wait_ge(src_T, 2 * s + h + 1)
                    act.activation(srcT[:, h, :], tp[0][0:KS, :], ACT.Copy).then_inc(src_ev, 1)
                    act.wait_ge(dst_T, 2 * s + h + 1)
                    act.activation(dstT[:, h, :], tp[1][0:KD, :], ACT.Copy).then_inc(dst_ev, 1)
                for h in range(2):
                    if h:
                        between()
                    act.wait_ge(q_mm, 2 * s + h + 1)
                    act.activation(q_sb[:, h, :], q_ps[:, :], ACT.Copy).then_inc(q_evac, 1)

            def exps(s):
                act.wait_ge(ex_ready, s + 1)
                act.activation(cw[:, :, :, 1:ET + 1].rearrange("p a h t -> p (a h) t"),
                               ex[:, :, :, :].rearrange("p a h t -> p (a h) t"), ACT.Exp)\
                   .then_inc(cw_ready, 1)
                act.wait_ge(scanned, s + 1)
                act.activation(factors[:, :, :, 1:ET + 1],
                               ex[:, 0, :, :].unsqueeze(2).broadcast_to([P, H, C, ET]), ACT.Exp)\
                   .then_inc(spread_ready, 1)

            def residuals(s):
                act.wait_ge(rs_ready, s + 1)
                if not (isinstance(s, int) and s == 0):
                    act.wait_ge(o_proj, s)
                for t in range(ET):
                    ins = act.activation(HB[:, t, :], Y[:, ET + t, :], ACT.Copy,
                                         scale=rs[:, ET + t:ET + t + 1])
                ins.then_inc(h_ready, 1)

            def relus(b, par, a, z):
                if a == 0:
                    act.wait_ge(x_mean, b + 1)
                if a == ET and not (isinstance(b, int) and b == 0):
                    act.wait_ge(h_ready, b)
                for t in range(a, z):
                    ins = act.activation(Y[:, t, :], X[par][:, t, :], ACT.Relu,
                                         bias=nmean[:, t:t + 1])
                if z % ET == 0:
                    ins.then_inc(relued, 1)

            def turned(s):
                act.wait_ge(ze_T, s - 1)
                act.activation(z2eT[:, :], tp[0][:, :], ACT.Copy).then_inc(ze_ev, 1)

            def mlp(s):
                act.wait_ge(hide_mm, s - 1)
                act.activation(hide[:, :], hid_ps[:, :], ACT.Gelu, bias=b1g[:, 0:1])\
                   .then_inc(gelue_done, 1)

            def rows_out(s, early=False):
                act.wait_ge(mlpe_mm, s - 1)
                if not early:
                    act.wait_ge(rows_stored, 16 * (s - 2))
                act.activation(OUTE[:, :], res_ps[:, :], ACT.Copy).then_inc(oute_ready, 1)

            def roots(s, norms=True, targets=True):
                if norms:
                    act.wait_ge(y_var, s + 2)
                if targets:
                    act.wait_ge(o_var, s)
                act.activation(sd[:, :], vars_[:, :], ACT.Sqrt).then_inc(sd_ready, 1)

            def project(s, h):
                act.wait_ge(agg_T, 2 * s + h + 1)
                act.activation(aggT[:, h, :], (tp[0], hid_ps)[h][:, :], ACT.Copy)\
                   .then_inc(agg_ev, 1)

            def step(s, par, with_mlp=True, early=False, norms=True, targets=True):
                def first_sources():
                    if norms:
                        relus(s + 1, 1 - par, 0, ET // 2)

                evacuate_qkv(s, first_sources)
                if with_mlp:
                    turned(s)
                if norms:
                    relus(s + 1, 1 - par, ET // 2, ET)
                residuals(s)
                exps(s)
                if with_mlp:
                    mlp(s)
                if norms:
                    relus(s + 1, 1 - par, ET, XT)
                if with_mlp:
                    rows_out(s, early)
                project(s, 0)
                roots(s, norms, targets)
                project(s, 1)

            def first_relus():
                relus(0, 0, 0, ET)
                relus(0, 0, ET, XT)

            nodes_step(NB, 1, relus=False, between=first_relus)
            roots(-1, targets=False)
            out_chunk(NB, NCH - 2)
            out_chunk(NB, NCH - 1)
            step(0, 0, with_mlp=False, targets=False)
            step(1, 1, with_mlp=False)
            step(2, 0, early=True)
            step(3, 1)
            with act.Fori(2, B // 2) as k:
                step(2 * k, 0)
                step(2 * k + 1, 1)
            step(B - 1, 0, norms=False)
            turned(B)
            mlp(B)
            rows_out(B)
            roots(B, norms=False)
            turned(B + 1)
            mlp(B + 1)
            rows_out(B + 1)
            act.wait_ge(f_exp_in, 1)
            act.activation(fcw[:, :, :], fex[:, :, :], ACT.Exp).then_inc(f_exp, 1)
            for i in range(2):
                act.wait_ge(f_var, i + 1)
                act.activation(fsc[:, 5 + 6 * i:6 + 6 * i], fsc[:, 4 + 6 * i:5 + 6 * i], ACT.Sqrt)\
                   .then_inc(f_sd, 1)
            act.wait_ge(f_zT, 1)
            act.activation(fzT[:, 0, :], v_ps[0][0:C, 0:P], ACT.Copy).then_inc(f_zev, 1)
            act.wait_ge(f_hid, 1)
            act.activation(fzT[:, 1, :], v_ps[1][0:C, P:2 * P], ACT.Gelu, bias=b1g[0:C, 0:1])\
               .then_inc(f_gelu, 1)

        @block.vector
        def _(dve):
            linked = [0]

            def link(ins):
                linked[0] += 1
                ins.then_inc(link_done, 1)
                dve.wait_ge(link_done, linked[0])

            dve.memset(dsti[:, :], N)
            dve.memset(dstg[:, :], 0)
            dve.memset(srci[:, :], 0).then_inc(pads_set, 1)
            for t in [w2bd[:, :], w1bd[:, :], place_edge[:, :], cw[:, :, :, :], den[1][:, :, :],
                      factors[:, :, :, :], ost[:, :, :], dvars[:, NT:2 * NT], dj[:, :], aj[:, :],
                      *(u[:, :] for m in (KS, KD) for u in pick[m])]:
                dve.memset(t, 0.0)
            dve.memset(vars_[:, :], 1.0)
            dve.memset(mx[1][:, :, :], NEG)
            dve.memset(mj[:, :], NEG)
            dve.memset(ones[:, :], 1.0)
            dve.memset(biases[:, :, :, :], 0.0)
            for i in range(2):
                dve.memset(aug_s[i][:, :, C + ED:KS], 1.0)
            dve.memset(keepm[:, :, :, 0:1], NEG)
            dve.memset(aug_d[:, :, C:KD], 1.0).then_inc(pads_set, 1)
            dve.wait_ge(pads_set, 2)

            dve.wait_ge(tables_in, 7 * 16)
            link(dve.tensor_copy(dstf[:, :], dsti[:, :]))
            link(dve.tensor_scalar(dstg[:, 0:EPP], dstf[:, 1:EPP + 1], float(N - 1), None, ALU.min))
            dve.memset(vars_[:, OV:VN], 1.0).then_inc(tabled, 1)
            link(dve.tensor_tensor(same[:, :], dstf[:, 0:EPP + 1], dstf[:, 1:EPP + 2], ALU.is_equal))
            for h in range(H):
                ins = dve.tensor_scalar(keepm[:, :, h, 1:ET + 1],
                                        same[:, 0:EPP].rearrange("p (b t) -> p b t", t=ET),
                                        1.0, -NEG, ALU.subtract, ALU.mult)
            link(ins)
            dve.memset(keepm[:, 0, :, 1:2], NEG)
            link(dve.tensor_scalar(firstseg[:, :], dstf[:, 1:EPP + 1], dstf[:, 1:2], None,
                                   ALU.is_equal))
            link(dve.tensor_scalar(nofinal[:, :], firstseg[:, :], same[:, 0:1], None, ALU.mult))
            link(dve.tensor_tensor(nofinal[:, :], nofinal[:, :], same[:, 1:EPP + 1], ALU.max))
            link(dve.scalar_tensor_tensor(scati[:, :], nofinal[:, :], FAR, dstf[:, 1:EPP + 1],
                                          ALU.mult, ALU.add))
            link(dve.tensor_reduce(fix[:, 0:1], firstseg[:, :], AX.X, ALU.add))
            dve.wait_ge(built, 6)
            filled = firstseg[:, EPP - 1:EPP]
            dve.tensor_tensor(fixi[:, 0:1], fix[:, 0:1], rowbase[:, :], ALU.add)
            dve.tensor_tensor(fix[:, 1:2], filled, same[:, 0:1], ALU.mult)
            link(dve.tensor_tensor(fix[:, 2:3], filled, same[:, EPP:EPP + 1], ALU.mult))
            link(dve.tensor_scalar(fix[:, 3:4], fix[:, 2:3], -1.0, 1.0, ALU.mult, ALU.add))
            link(dve.tensor_tensor(fix[:, 3:4], fix[:, 3:4], same[:, 0:1], ALU.mult))
            link(dve.tensor_scalar(fix[:, 4:5], fix[:, 3:4], -FAR, FAR, ALU.mult, ALU.add))
            dve.tensor_tensor(fixi[:, 1:2], fix[:, 4:5], dstf[:, 1:2], ALU.add)
            for h in range(H):
                dve.tensor_copy(fflag[:, 0, h:h + 1], fix[:, 1:2])
                dve.tensor_copy(fflag[:, 1, h:h + 1], same[:, 0:1])

            dve.wait_ge(consts_in, 16 * 21)
            link(dve.tensor_scalar(center[:, :], ident[0:C, 0:C], -1.0 / C, None, ALU.add))
            for i in range(3):
                link(dve.tensor_copy(bsplit[i][:, :, :], brow[:, :, :]))
                if i < 2:
                    link(dve.tensor_tensor(brow[:, :, :], brow[:, :, :], bsplit[i][:, :, :],
                                           ALU.subtract))
            for r, part in zip(BR, bsplit):
                for i in range(2):
                    dve.tensor_copy(biases[r:r + 1, i, :, :], rows(part[r:r + 1, i, :], 8))
            for m in (KS, KD):
                dve.tensor_copy(pick[m][0][:, 0:C], center[:, :])
                dve.tensor_copy(pick[m][1][:, m - 1:m], gcol[:, 1:2])
                dve.memset(pick[m][2][:, m - 1:m], 1.0)
            for h in range(2):
                dve.tensor_copy(center2[:, h * C:(h + 1) * C], center[:, :])
            dve.tensor_copy(place_edge[:, C:C + ED], ident[0:ED, 0:ED])
            dve.tensor_scalar(gwqkv[:, :, :], wqkv[:, :, :], gcol[:, 0:1], None, ALU.mult)
            dve.tensor_scalar(gw1[:, :], w1[:, 0, :], gcol[:, 2:3], None, ALU.mult)\
               .then_inc(w_placed, 1)
            dve.wait_ge(w_folded, 1)
            dve.tensor_scalar(wq_s[:, :], q_ps[0:KD, 0:HC], float(C) ** -0.5, None, ALU.mult)
            dve.tensor_copy(flat(wkv_s[:, :, :]), k_ps[0:KS, 0:2 * HC])
            for h in range(2):
                a, z = h * C, (h + 1) * C
                dve.tensor_copy(w1bd[a:z, a:z], tp[0][a:z, 0:C])
            dve.tensor_tensor(b1g[:, :], b1col[:, :], hid_ps[:, 0:1], ALU.add).then_inc(w_ready, 1)

            def variances(st, w, sums, diff2, n, mean_to=None, mean_done=None, factor=0.5):
                dve.tensor_tensor(w[:, 1, :], st[:, :, 1], st[:, :, 4], ALU.subtract)
                if mean_to is not None:
                    dve.tensor_tensor(w[:, 0, :], st[:, :, 1], st[:, :, 4], ALU.add)
                dve.tensor_tensor(w[:, 2, :], st[:, :, 2], st[:, :, 5], ALU.add).then_inc(sums, 1)
                dve.wait_ge(sums, n)
                if mean_to is not None:
                    dve.tensor_scalar(mean_to, w[:, 0, :], factor, None, ALU.mult)\
                       .then_inc(mean_done, 1)
                dve.tensor_tensor(w[:, 1, :], w[:, 1, :], w[:, 1, :], ALU.mult).then_inc(diff2, 1)
                dve.wait_ge(diff2, n)
                return dve.scalar_tensor_tensor(w[:, 3, :], w[:, 1, :], float(C // 4), w[:, 2, :],
                                                ALU.mult, ALU.add)

            def nodes_statistics(d, par, n):
                dve.wait_ge(d_in[par], 32 * n)
                for t in range(NT):
                    ins = dve.bn_stats(dst_x[:, t, :], DX[par][:, t, :])
                ins.then_inc(d_xstats, 1)

            def nodes_bias(d, par):
                for c in range(NCH):
                    dve.wait_ge(d_relued, NCH * d + c + 1)
                    o = DO[par][:, 8 * c:8 * c + 8, :]
                    ins = dve.tensor_tensor(o, o, rows(bp_b[:, :], 8), ALU.add)
                ins.then_inc(d_biased, 1)

            def nodes_variances(d):
                dve.wait_ge(d_xstats, d + 1)
                variances(dst_x, dsm, d_xsums, d_xdiff2, d + 1, dmean[:, :], d_mean)\
                    .then_inc(d_xv64, 1)
                dve.wait_ge(d_xv64, d + 1)
                dve.tensor_scalar(dvars[:, 0:NT], dsm[:, 3, :], 1.0 / C, EPS, ALU.mult, ALU.add)\
                   .then_inc(d_xvar, 1)

            def nodes_second(d, par, early=False):
                dve.wait_ge(d_biased, d + 1)
                if not early:
                    dve.wait_ge(mlp_mm[NCH - 1], d - 1)
                dve.tensor_tensor(XO[par][:, :, :], DX[par][:, :, :], DO[par][:, :, :], ALU.add)\
                   .then_inc(d_xused, 1)
                for t in range(NT):
                    ins = dve.bn_stats(dst_o[:, t, :], DO[par][:, t, :])
                ins.then_inc(d_ostats, 1)
                dve.wait_ge(d_ostats, d + 1)
                variances(dst_o, dsm2, d_osums, d_odiff2, d + 1).then_inc(d_ov64, 1)
                dve.wait_ge(d_ov64, d + 1)
                dve.tensor_scalar(dvars[:, NT:2 * NT], dsm2[:, 3, :], 1.0 / C, EPS,
                                  ALU.mult, ALU.add).then_inc(d_ovar, 1)

            def nodes_center(d, par):
                dve.wait_ge(d_mean, d + 1)
                for a, z in ((0, NT // 2), (NT // 2, NT)):
                    dve.tensor_tensor(DY[:, a:z, :], DX[par][:, a:z, :], wide(dmean[:, a:z], C),
                                      ALU.subtract).then_inc(d_centered, 1)

            def nodes_roots(d):
                dve.wait_ge(d_sd, d + 1)
                dve.reciprocal(drs[:, :], dsd[:, :]).then_inc(d_rs, 1)
                dve.wait_ge(d_rs, d + 1)

            def nodes_z(d, par):
                for c in range(NCH):
                    dve.tensor_tensor(tiles(z2[:, c, :]), DO[par][:, 8 * c:8 * c + 8, :],
                                      wide(drs[:, NT + 8 * c:NT + 8 * c + 8], C), ALU.mult)\
                       .then_inc(z2_ready[c], 1)

            def nodes_step(d, par, n, early=False):
                nodes_statistics(d, par, n)
                nodes_variances(d)
                nodes_bias(d - 1, 1 - par)
                nodes_second(d - 1, 1 - par, early)
                nodes_center(d, par)
                nodes_roots(d)
                nodes_z(d - 1, 1 - par)

            nodes_statistics(0, 0, 1)
            nodes_variances(0)
            nodes_center(0, 0)
            nodes_roots(0)
            nodes_step(1, 1, 1, early=True)
            nodes_step(2, 0, 2, early=True)
            with dve.Fori(1, NB // 2) as k:
                nodes_step(2 * k + 1, 1, k + 1)
                nodes_step(2 * k + 2, 0, k + 2)
            nodes_bias(NB - 1, 0)
            nodes_second(NB - 1, 0)
            nodes_roots(NB)
            nodes_z(NB - 1, 0)

            def inverse_roots(s):
                dve.wait_ge(sd_ready, s + 2)
                dve.reciprocal(rs[:, :], sd[:, :]).then_inc(rs_ready, 1)
                dve.wait_ge(rs_ready, s + 2)

            def x_statistics(b, par, a, z):
                for t in range(a, z):
                    ins = dve.bn_stats(xst[:, t, :], X[par][:, t, :])
                if z == XT:
                    ins.then_inc(x_stats, 1)

            def x_variances(b):
                dve.wait_ge(x_stats, b + 1)
                variances(xst, sm, x_sums, x_diff2, b + 1, nmean[:, :], x_mean, -0.5)\
                    .then_inc(x_v64, 1)

            def x_eps(b):
                dve.wait_ge(x_v64, b + 1)
                dve.tensor_scalar(vars_[:, 0:XT], sm[:, 3, :], 1.0 / C, EPS, ALU.mult, ALU.add)\
                   .then_inc(x_var, 1)

            def y_statistics(b, ts):
                for t in ts:
                    if t % ET == 0:
                        dve.wait_ge(relued, 2 * b + t // ET + 1)
                    ins = dve.bn_stats(yst[:, t, :], Y[:, t, :])
                if ts[-1] == XT - 1:
                    ins.then_inc(y_stats, 1)

            def y_variances(b):
                dve.wait_ge(x_var, b + 1)
                dve.tensor_scalar(sm2[:, 0, :], vars_[:, 0:XT], EPS, None, ALU.mult)
                dve.wait_ge(y_stats, b + 1)
                variances(yst, sm2, y_sums, y_diff2, b + 1).then_inc(y_v64, 1)
                dve.wait_ge(y_v64, b + 1)
                dve.scalar_tensor_tensor(vars_[:, XT:OV], sm2[:, 3, :], 1.0 / C, sm2[:, 0, :],
                                         ALU.mult, ALU.add).then_inc(y_var, 1)

            def scale_rows(b, par):
                dve.tensor_tensor(aug_s[par][:, :, 0:C], Y[:, 0:ET, :],
                                  wide(rs[:, XT:XT + ET], C), ALU.mult).then_inc(zsrc_ready, 1)
                dve.tensor_tensor(aug_d[:, :, 0:C], Y[:, ET:XT, :],
                                  wide(rs[:, XT + ET:OV], C), ALU.mult).then_inc(zdst_ready, 1)

            def o_variances(s):
                dve.wait_ge(o_stats, s + 1)
                variances(ost, sm3, o_sums, o_diff2, s + 1).then_inc(o_v64, 1)
                dve.wait_ge(o_v64, s + 1)
                dve.tensor_scalar(vars_[:, OV:VN], sm3[:, 3, :], 1.0 / C, EPS, ALU.mult, ALU.add)\
                   .then_inc(o_var, 1)

            def z_second(s, par):
                dve.tensor_tensor(tiles(z2e[:, :]), OE[par][:, :, :], wide(rs[:, OV:VN], C),
                                  ALU.mult).then_inc(z2e_ready, 1)

            def products(s, h):
                dve.wait_ge(q_evac, 2 * s + h + 1)
                dve.wait_ge(k_mm, 2 * s + h + 1)
                dve.tensor_tensor(qk[:, 4 * h:4 * h + 4, :].rearrange("p t c -> p (t c)"),
                                  k_ps[:, :], q_sb[:, h, :], ALU.mult).then_inc(qk_ready, 1)

            def scores(s, par):
                dve.tensor_copy(alpha[:, :, 0:1], mx[1 - par][:, :, ET:ET + 1])
                dve.wait_ge(qk_ready, 2 * s + 2)
                dve.tensor_reduce(alpha[:, :, 1:ET + 1].rearrange("p h t -> p t h"),
                                  qk[:, :, :].rearrange("p t (h c) -> p t h c", h=H),
                                  AX.X, ALU.add).then_inc(alpha_ready, 1)

            def maxima(s, par):
                dve.wait_ge(alpha_ready, s + 1)
                dve.tensor_tensor_scan(flat(mx[par][:, :, :]),
                                       keepm[:, bass.ds(s, 1), :, :]
                                       .rearrange("p b h t -> p (b h t)"),
                                       flat(alpha[:, :, :]), NEG, ALU.add, ALU.max)\
                   .then_inc(mx_ready, 1)

            def exponents(s, par):
                m = mx[par]
                dve.wait_ge(mx_ready, s + 1)
                dve.tensor_tensor(ex[:, 0, :, :], m[:, :, 0:ET], m[:, :, 1:ET + 1],
                                  ALU.subtract).then_inc(mx_diff, 1)
                dve.tensor_tensor(ex[:, 1, :, :], alpha[:, :, 1:ET + 1], m[:, :, 1:ET + 1],
                                  ALU.subtract)
                dve.wait_ge(mx_diff, s + 1)
                dve.tensor_tensor(ex[:, 0, :, :], ex[:, 0, :, :],
                                  keepm[:, bass.ds(s, 1), :, 1:ET + 1]
                                  .rearrange("p b h t -> p (b h) t"), ALU.add)\
                   .then_inc(ex_ready, 1)

            def weighted_values(s, par, stores):
                dve.wait_ge(cw_ready, s + 1)
                dve.tensor_copy(cw[:, 1, :, 0:1], den[1 - par][:, :, ET:ET + 1])\
                   .then_inc(den_prev_in, 1)
                if stores is not None:
                    dve.wait_ge(state_stored[par], 16 * stores)
                dve.wait_ge(scanned, s + 1)
                dve.tensor_copy(weighted[:, :, 0:1], running[:, :, ET:ET + 1])
                for h in range(2):
                    dve.wait_ge(v_mm, 2 * s + h + 1)
                    for g in range(H):
                        ins = dve.tensor_tensor(
                            weighted[:, g * C:(g + 1) * C, 1 + 4 * h:5 + 4 * h]
                            .rearrange("p c t -> p t c"),
                            v_ps[h][:, :].rearrange("p (t c) -> p t c", c=HC)
                            [:, :, g * C:(g + 1) * C],
                            wide(cw[:, 1, g, 1 + 4 * h:5 + 4 * h], C), ALU.mult)
                    ins.then_inc(wv_ready, 1)
                    if h == 0:
                        dve.wait_ge(den_prev_in, s + 1)
                        dve.tensor_tensor_scan(flat(den[par][:, :, :]), flat(cw[:, 0, :, :]),
                                               flat(cw[:, 1, :, :]), 0.0, ALU.mult, ALU.add)\
                           .then_inc(den_ready, 1)

            def averages(s, par, half):
                R = rec[par]
                if half == 0:
                    dve.wait_ge(scanned, s + 2)
                    dve.wait_ge(rden_ready, s + 1)
                t = slice(4 * half, 4 * half + 4)
                for g in range(H):
                    a, z = g * C, (g + 1) * C
                    ins = dve.tensor_tensor(R[:, t, a:z],
                                            running[:, a:z, 1 + 4 * half:5 + 4 * half]
                                            .rearrange("p c t -> p t c"),
                                            wide(rden[:, 1, g, t], C), ALU.mult)
                ins.then_inc(aggn_ready, 1)

            def sums(s, par, s_before):
                R = rec[par]
                dve.wait_ge(den_ready, s + 1)
                dve.tensor_scalar(rden[:, 0, :, :], den[par][:, :, 1:ET + 1], 1e-8,
                                  None, ALU.add).then_inc(den_eps, 1)
                dve.tensor_copy(R[:, :, HC:HC + H].rearrange("p t h -> p h t"),
                                mx[par][:, :, 1:ET + 1])
                dve.tensor_copy(R[:, :, HC + H:SW].rearrange("p t h -> p h t"),
                                den[par][:, :, 1:ET + 1])
                dve.wait_ge(den_eps, s + 1)
                dve.reciprocal(rden[:, 1, :, :], rden[:, 0, :, :]).then_inc(rden_ready, 1)
                dve.wait_ge(wv_ready, 2 * s + 2)
                if s_before is not None:
                    dve.wait_ge(aggn_ready, s_before)
                dve.wait_ge(spread_ready, s + 1)
                dve.tensor_tensor_scan(running[:, :, :].rearrange("p c t -> p (c t)"),
                                       factors[:, :, :, :].rearrange("p h c t -> p (h c t)"),
                                       weighted[:, :, :].rearrange("p c t -> p (c t)"), 0.0,
                                       ALU.mult, ALU.add).then_inc(scanned, 1)

            def add_projection(s, par, first):
                if not first:
                    dve.wait_ge(mlpe_mm, s - 1)
                dve.wait_ge(h_ready, s + 1)
                dve.wait_ge(proj_mm, s + 1)
                dve.tensor_tensor(OE[par][:, :, :], tiles(res_ps[:, :]), HB[:, :, :],
                                  ALU.add).then_inc(o_proj, 1)
                dve.wait_ge(o_proj, s + 1)

            def o_statistics(par, a, z):
                for t in range(a, z):
                    ins = dve.bn_stats(ost[:, t, :], OE[par][:, t, :])
                if z == ET:
                    ins.then_inc(o_stats, 1)

            def step(s, par, n=None, stores=None, early=False, norms=True, targets=True):
                b = s + 1
                if norms:
                    dve.wait_ge(ends_in[1 - par], 16 * n)
                    x_statistics(b, 1 - par, 0, XT)
                    x_variances(b)
                if targets:
                    add_projection(s - 1, 1 - par, early)
                    o_statistics(1 - par, 0, ET // 2)
                products(s, 0)
                if norms:
                    x_eps(b)
                if targets:
                    o_statistics(1 - par, ET // 2, ET)
                products(s, 1)
                scores(s, par)
                maxima(s, par)
                exponents(s, par)
                if targets:
                    o_variances(s - 1)
                if norms:
                    y_statistics(b, range(ET // 2))
                weighted_values(s, par, stores)
                if norms:
                    y_statistics(b, range(ET // 2, ET))
                sums(s, par, None if isinstance(s, int) and s == 0 else 2 * s)
                averages(s, par, 0)
                averages(s, par, 1)
                if norms:
                    y_statistics(b, range(ET, XT))
                    y_variances(b)
                inverse_roots(s)
                if norms:
                    scale_rows(b, 1 - par)
                if targets:
                    z_second(s - 1, 1 - par)

            dve.wait_ge(ends_in[0], 16)
            x_statistics(0, 0, 0, XT)
            x_variances(0)
            x_eps(0)
            y_statistics(0, range(XT))
            y_variances(0)
            inverse_roots(-1)
            scale_rows(0, 0)
            dve.memset(running[:, :, ET:ET + 1], 0.0).then_inc(scanned, 1)
            step(0, 0, 1, early=True, targets=False)
            step(1, 1, 2, early=True)
            step(2, 0, 2, stores=1, early=True)
            step(3, 1, 3, stores=1)
            with dve.Fori(2, B // 2) as k:
                step(2 * k, 0, k + 1, stores=k)
                step(2 * k + 1, 1, k + 2, stores=k)
            step(B - 1, 0, stores=B // 2, norms=False)
            add_projection(B - 1, 0, False)
            o_statistics(0, 0, ET)
            o_variances(B - 1)
            inverse_roots(B)
            z_second(B - 1, 0)

            steps = [0]

            def flink(ins, to=None):
                if to is None:
                    steps[0] += 1
                    ins.then_inc(f_link, 1)
                    dve.wait_ge(f_link, steps[0])
                else:
                    ins.then_inc(to, 1)

            dve.wait_ge(f_T, 1)
            dve.tensor_copy(flat(fT[:, :, :]), k_ps[:, 0:2 * P])
            dve.tensor_copy(flat(fsm[:, 0:4, :]), q_ps[0:H, :])
            flink(dve.tensor_scalar(flat(fkeep[:, :, :]), k_ps[0:H, 2 * P:4 * P], 1.0, -NEG,
                                    ALU.subtract, ALU.mult))
            mF, dF, mL, dL = (fsm[:, i, :] for i in range(4))
            flink(dve.tensor_scalar(fsm[:, 4, :], dF, 1e-8, None, ALU.add))
            flink(dve.tensor_scalar(fsm[:, 5, :], dL, 1e-8, None, ALU.add))
            flink(dve.tensor_tensor_scan(mj[:, 1:P + 1], fkeep[:, 0, :], mL, NEG, ALU.add, ALU.max))
            dve.tensor_tensor(fk[:, 4, :], mj[:, 0:P], fkeep[:, 1, :], ALU.add)
            dve.tensor_tensor(fk[:, 5, :], mj[:, 0:P], mj[:, 1:P + 1], ALU.subtract)
            flink(dve.tensor_tensor(fex[:, 1, :], mL, mj[:, 1:P + 1], ALU.subtract))
            flink(dve.tensor_tensor(fk[:, 6, :], fk[:, 4, :], mF, ALU.max))
            dve.tensor_tensor(fex[:, 0, :], fk[:, 5, :], fkeep[:, 0, :], ALU.add)
            dve.tensor_tensor(fex[:, 2, :], mF, fk[:, 6, :], ALU.subtract)
            flink(dve.tensor_tensor(fex[:, 3, :], fk[:, 4, :], fk[:, 6, :], ALU.subtract), f_exp_in)
            dve.wait_ge(f_exp, 1)
            flink(dve.tensor_tensor(fk[:, 4, :], fcw[:, 1, :], dL, ALU.mult))
            flink(dve.tensor_tensor_scan(dj[:, 1:P + 1], fcw[:, 0, :], fk[:, 4, :], 0.0,
                                         ALU.mult, ALU.add))
            dve.tensor_tensor(fk[:, 5, :], dF, fcw[:, 2, :], ALU.mult)
            flink(dve.tensor_tensor(fk[:, 6, :], dj[:, 0:P], fcw[:, 3, :], ALU.mult))
            flink(dve.tensor_tensor(fk[:, 5, :], fk[:, 5, :], fk[:, 6, :], ALU.add))
            flink(dve.tensor_scalar(fk[:, 6, :], fk[:, 5, :], 1e-8, None, ALU.add))
            flink(dve.reciprocal(fk[:, 7, :], fk[:, 6, :]))
            dve.tensor_copy(fk[:, 0, :], fcw[:, 0, :])
            dve.tensor_tensor(fk[:, 1, :], fcw[:, 1, :], fsm[:, 5, :], ALU.mult)
            flink(dve.tensor_tensor(fk[:, 2, :], fcw[:, 2, :], fk[:, 7, :], ALU.mult))
            flink(dve.tensor_tensor(fk[:, 2, :], fk[:, 2, :], fsm[:, 4, :], ALU.mult))
            flink(dve.tensor_tensor(fk[:, 3, :], fcw[:, 3, :], fk[:, 7, :], ALU.mult), f_coef)
            dve.wait_ge(f_bc, 1)
            flink(dve.tensor_copy(flat(bc[:, :, :]), v_ps[0][:, :]))
            dve.tensor_tensor(fa[:, 1, :], fT[:, 0, :], bc[:, 2, :], ALU.mult)
            flink(dve.tensor_tensor(fa[:, 0, :], fT[:, 1, :], bc[:, 1, :], ALU.mult))
            flink(dve.tensor_tensor_scan(aj[:, 1:P + 1], bc[:, 0, :], fa[:, 0, :], 0.0,
                                         ALU.mult, ALU.add))
            flink(dve.tensor_tensor(fa[:, 0, :], aj[:, 0:P], bc[:, 3, :], ALU.mult))
            flink(dve.tensor_tensor(fa[:, 2, :], fa[:, 0, :], fa[:, 1, :], ALU.add), f_agg)

            def small_variance(row, c):
                flink(dve.bn_stats(fst[:, :], row))
                flink(dve.tensor_tensor(fsc[:, c:c + 1], fst[:, 1:2], fst[:, 4:5], ALU.subtract))
                dve.tensor_tensor(fsc[:, c + 1:c + 2], fst[:, 1:2], fst[:, 4:5], ALU.add)
                dve.tensor_tensor(fsc[:, c + 2:c + 3], fst[:, 2:3], fst[:, 5:6], ALU.add)
                flink(dve.tensor_tensor(fsc[:, c:c + 1], fsc[:, c:c + 1], fsc[:, c:c + 1],
                                        ALU.mult))
                dve.tensor_scalar(fsc[:, c + 1:c + 2], fsc[:, c + 1:c + 2], 0.5, None, ALU.mult)
                flink(dve.scalar_tensor_tensor(fsc[:, c + 3:c + 4], fsc[:, c:c + 1],
                                               float(C // 4), fsc[:, c + 2:c + 3],
                                               ALU.mult, ALU.add))
                flink(dve.tensor_scalar(fsc[:, c + 4:c + 5], fsc[:, c + 3:c + 4], 1.0 / C, EPS,
                                        ALU.mult, ALU.add), f_var)

            dve.wait_ge(f_in, 32)
            small_variance(xf[:, :], 0)
            flink(dve.tensor_scalar(frow[:, 0, :], xf[:, :], fsc[:, 1:2], 0.0,
                                    ALU.subtract, ALU.max))
            dve.wait_ge(f_sd, 1)
            flink(dve.reciprocal(fsc[:, 3:4], fsc[:, 5:6]))
            flink(dve.scalar_tensor_tensor(frow[:, 1, :], frow[:, 0, :], fsc[:, 3:4], bp_b[:, :],
                                           ALU.mult, ALU.add))
            dve.wait_ge(f_proj, 1)
            flink(dve.tensor_tensor(frow[:, 2, :], v_ps[1][:, 0:C], frow[:, 1, :], ALU.add))
            small_variance(frow[:, 2, :], 6)
            flink(dve.tensor_tensor(frow[:, 4, :], frow[:, 2, :], xf[:, :], ALU.add))
            dve.wait_ge(f_sd, 2)
            flink(dve.reciprocal(fsc[:, 9:10], fsc[:, 11:12]))
            flink(dve.tensor_scalar(frow[:, 3, :], frow[:, 2, :], fsc[:, 9:10], None, ALU.mult),
                  f_z)
            dve.wait_ge(f_mlp, 1)
            flink(dve.tensor_tensor(frow[:, 5, :], q_ps[:, 0:C], frow[:, 4, :], ALU.add), f_row)


_W = ["Wq", "bq", "Wk", "bk", "Wv", "bv", "We", "Wp", "bp", "ln1_g", "ln1_b", "ln2_g", "ln2_b",
      "W1", "b1", "W2", "b2"]
_INS = ["x", "src", "dst", "edge_attr_32"] + [f"L0_gnn_{n}" for n in _W]


def kernel(**inputs):
    import numpy as _np
    import concourse.bacc as _bacc
    from concourse import mybir as _mybir
    from concourse.bass_utils import run_bass_kernel_spmd as _run

    nc = _bacc.Bacc("TRN2", target_bir_lowering=False, num_devices=1)
    f32 = _mybir.dt.float32
    arrays, args = {}, []
    for name in _INS:
        a = _np.ascontiguousarray(inputs[name])
        arrays[f"in_{name}"] = a
        args.append(nc.dram_tensor(f"in_{name}", a.shape, _mybir.dt.from_np(a.dtype),
                                   kind="ExternalInput").ap())
    n, c = inputs["x"].shape
    e = inputs["src"].shape[0]
    per = -(-e // (128 * 8)) * 8
    ends = nc.dram_tensor("ends", (128, 2 * per, c), f32, kind="Internal").ap()
    edge_rows = nc.dram_tensor("edge_rows", (128, per, c), f32, kind="Internal").ap()
    states = nc.dram_tensor("states", (128, per, 2 * c + 4), f32, kind="Internal").ap()
    out = nc.dram_tensor("out_0", (n, c), f32, kind="ExternalOutput").ap()
    gnn_layer(nc, *args, ends, edge_rows, states, out)
    r = _run(nc, [arrays], core_ids=[0])
    return r.results[0]["out_0"]
```
